# Optimizing a Trainium2 kernel written in Bass

```python
import numpy as np
import jax
import jax.numpy as jnp

def _softmax(x, axis=-1):
    return jax.nn.softmax(x, axis=axis)

def _gelu(x):
    return jax.nn.gelu(x, approximate=True)

def _silu(x):
    return jax.nn.silu(x)

def _sigmoid(x):
    return jax.nn.sigmoid(x)

def _layernorm(x, axis=-1, eps=1e-05):
    m = jnp.mean(x, axis=axis, keepdims=True)
    v = jnp.var(x, axis=axis, keepdims=True)
    return (x - m) / jnp.sqrt(v + eps)

def _scatter_add(tgt, idx, src, axis=0):
    return tgt.at[idx].add(src)

def _segment_sum(src, seg, n):
    return jax.ops.segment_sum(src, seg, n)
kernel_name = 'mk_vit_tower_d1_tok_img2048_r4_07efa1'

def setup_inputs(seed: int=0):
    np.random.seed(seed)
    _w = jnp.asarray

    def _rec_inputs():
        import jax
        import jax.numpy as jnp
        _rk = jax.random.key(seed)
        x = -0.00286756 + 0.998052 * jax.random.normal(jax.random.fold_in(_rk, 1), (16, 192, 64, 2), jnp.float32)
        return x
    x = _rec_inputs()

    def _L0_tok_setup():
        import jax, jax.numpy as jnp
        import numpy as np
        H = 192
        N = 64
        CH = 1
        NSSM = 192
        L_VAL = 512
        key = jax.random.key(seed)
        k_dt, k_C = jax.random.split(key, 2)
        log_dt = np.log(0.001) + jax.random.uniform(k_dt, (H,), dtype=jnp.float32) * (np.log(0.1) - np.log(0.001))
        B_ri = jnp.concatenate([jnp.ones((NSSM, N, 1), jnp.float32), jnp.zeros((NSSM, N, 1), jnp.float32)], axis=-1)
        inv_A_real = jnp.full((NSSM, N), np.log(0.5), dtype=jnp.float32)
        A_imag = jnp.tile(np.pi * jnp.arange(N, dtype=jnp.float32)[None, :], (NSSM, 1))
        C_ri = jax.random.normal(k_C, (CH, H, N, 2), dtype=jnp.float32)
        return {'log_dt': log_dt, 'B_ri': B_ri, 'inv_A_real': inv_A_real, 'A_imag': A_imag, 'C_ri': C_ri, 'L': L_VAL}
    _L0_tok_all = _L0_tok_setup()
    _L0_tok_in = {k: v for k, v in _L0_tok_all.items() if k in ('log_dt', 'B_ri', 'inv_A_real', 'A_imag')}
    del _L0_tok_all

    def _L0_attn_setup():
        import jax, jax.numpy as jnp
        import numpy as np
        HIDDEN = 512
        INTER = 1024
        KCONV = 1024
        DT_RANK = 128
        SSM_N = 16
        B_SZ, SEQ = (2, 1024)
        key = jax.random.key(seed)
        ks = jax.random.split(key, 8)
        s = 0.02
        return {'hidden_states': jax.random.normal(ks[0], (B_SZ, SEQ, HIDDEN), jnp.float32), 'W_in': jax.random.normal(ks[1], (2 * INTER, HIDDEN), jnp.float32) * s, 'conv_w': jax.random.normal(ks[2], (INTER, KCONV), jnp.float32) * s, 'W_x': jax.random.normal(ks[3], (DT_RANK + 2 * SSM_N, INTER), jnp.float32) * s, 'W_dt': jax.random.normal(ks[4], (INTER, DT_RANK), jnp.float32) * s, 'b_dt': jax.random.normal(ks[5], (INTER,), jnp.float32) * s, 'D': jnp.ones((INTER,), jnp.float32), 'W_out': jax.random.normal(ks[6], (HIDDEN, INTER), jnp.float32) * s}
    _L0_attn_all = _L0_attn_setup()
    _L0_attn_in = {k: v for k, v in _L0_attn_all.items() if k in ('W_in', 'conv_w', 'W_x', 'W_dt', 'b_dt', 'D', 'W_out')}
    del _L0_attn_all

    def _L0_ffn_setup():
        import jax, jax.numpy as jnp
        import numpy as np
        import math
        N_EMBD = 512
        N_HEAD = 16
        HEAD_DIM = N_EMBD // N_HEAD
        B, T = (2, 512)
        key = jax.random.key(seed)
        k1, k2, k3 = jax.random.split(key, 3)
        x = jax.random.normal(k1, (B, T, N_EMBD), dtype=jnp.float32)
        W_gate = jax.random.normal(k2, (N_HEAD, N_EMBD), dtype=jnp.float32) * 0.02
        W_qkv = jax.random.normal(k3, (3 * N_EMBD, N_EMBD), dtype=jnp.float32) * 0.02
        return {'x': x, 'W_gate': W_gate, 'W_qkv': W_qkv}
    _L0_ffn_all = _L0_ffn_setup()
    _L0_ffn_in = {k: v for k, v in _L0_ffn_all.items() if k in ('W_gate', 'W_qkv')}
    del _L0_ffn_all
    return {'x': x, 'L0_tok_log_dt': _L0_tok_in['log_dt'], 'L0_tok_B_ri': _L0_tok_in['B_ri'], 'L0_tok_inv_A_real': _L0_tok_in['inv_A_real'], 'L0_tok_A_imag': _L0_tok_in['A_imag'], 'L0_attn_W_in': _L0_attn_in['W_in'], 'L0_attn_conv_w': _L0_attn_in['conv_w'], 'L0_attn_W_x': _L0_attn_in['W_x'], 'L0_attn_W_dt': _L0_attn_in['W_dt'], 'L0_attn_b_dt': _L0_attn_in['b_dt'], 'L0_attn_D': _L0_attn_in['D'], 'L0_attn_W_out': _L0_attn_in['W_out'], 'L0_ffn_W_gate': _L0_ffn_in['W_gate'], 'L0_ffn_W_qkv': _L0_ffn_in['W_qkv']}

def reference(x, L0_tok_log_dt, L0_tok_B_ri, L0_tok_inv_A_real, L0_tok_A_imag, L0_attn_W_in, L0_attn_conv_w, L0_attn_W_x, L0_attn_W_dt, L0_attn_b_dt, L0_attn_D, L0_attn_W_out, L0_ffn_W_gate, L0_ffn_W_qkv):
    import jax
    import jax.numpy as jnp

    def _L0_tok_ref(log_dt, B_ri, inv_A_real, A_imag, C_ri, L):
        import jax, jax.numpy as jnp
        import numpy as np
        H = 192
        N = 64
        CH = 1
        NSSM = 192
        L_VAL = 512
        dt = jnp.exp(log_dt)
        A = -jnp.exp(inv_A_real) + 1j * A_imag
        rep = H // A.shape[0]
        A = jnp.tile(A, (rep, 1))
        B = B_ri[..., 0] + 1j * B_ri[..., 1]
        B = jnp.tile(B, (rep, 1))[None]
        C = C_ri[..., 0] + 1j * C_ri[..., 1]
        C = (B[:, None, :, :] * C).reshape(-1, H, N)
        dtA = A * dt[:, None]
        C = C * (jnp.exp(dtA) - 1.0) / A
        ell = jnp.arange(L, dtype=jnp.float32)
        V = jnp.exp(dtA[:, :, None] * ell)
        K = 2.0 * jnp.einsum('chn,hnl->chl', C, V).real
        return K.astype(jnp.float32)

    def _L0_attn_ref(hidden_states, W_in, conv_w, W_x, W_dt, b_dt, D, W_out):
        import jax, jax.numpy as jnp
        import numpy as np
        HIDDEN = 512
        INTER = 1024
        KCONV = 1024
        DT_RANK = 128
        SSM_N = 16
        B_SZ, SEQ = (2, 1024)
        xz = jnp.einsum('bsh,ih->bsi', hidden_states, W_in)
        x, z = jnp.split(xz, 2, axis=-1)
        x = jnp.einsum('bsk,ik->bsi', x, conv_w)
        x_proj = jnp.einsum('bsi,pi->bsp', x, W_x)
        delta_raw = x_proj[..., :DT_RANK]
        B = x_proj[..., DT_RANK:DT_RANK + SSM_N]
        C = x_proj[..., DT_RANK + SSM_N:]
        delta = jax.nn.softplus(jnp.einsum('bsr,ir->bsi', delta_raw, W_dt))
        y = x * D
        z = jax.nn.silu(z)
        return jnp.einsum('bsi,hi->bsh', y * z, W_out)

    def _L0_ffn_ref(x, W_gate, W_qkv):
        import jax, jax.numpy as jnp
        import numpy as np
        import math
        N_EMBD = 512
        N_HEAD = 16
        HEAD_DIM = N_EMBD // N_HEAD
        B, T = (2, 512)
        Bb, Tt, C = x.shape
        H, hd = (N_HEAD, HEAD_DIM)
        gating = jax.nn.softmax(x @ W_gate.T, axis=-1)
        idx = jnp.argmax(gating, axis=-1)
        indicator = jax.nn.one_hot(idx, H, dtype=gating.dtype)
        top1_val = jnp.max(gating, axis=-1, keepdims=True)
        gating_top1 = indicator * top1_val
        qkv = x @ W_qkv.T
        q, k, v = jnp.split(qkv, 3, axis=-1)
        k = k.reshape(Bb, Tt, H, hd)
        v = v.reshape(Bb, Tt, H, hd)
        k_shared = jnp.einsum('bth,bthd->btd', indicator, k)
        v_shared = jnp.einsum('bth,bthd->btd', gating_top1, v)
        q = q.reshape(Bb, Tt, H, hd).transpose(0, 2, 1, 3)
        att = jnp.einsum('bhqd,bkd->bhqk', q, k_shared) * (1.0 / math.sqrt(hd))
        causal = jnp.tril(jnp.ones((Tt, Tt), dtype=bool))
        att = jnp.where(causal[None, None, :, :], att, -jnp.inf)
        att = jax.nn.softmax(att, axis=-1)
        y = jnp.einsum('bhqk,bkd->bhqd', att, v_shared)
        y = y.transpose(0, 2, 1, 3).reshape(Bb, Tt, C)
        return y
    h = _L0_tok_ref(L0_tok_log_dt, L0_tok_B_ri, L0_tok_inv_A_real, L0_tok_A_imag, x, 512)
    h = h + _L0_attn_ref(_layernorm(h, axis=-1), L0_attn_W_in, L0_attn_conv_w, L0_attn_W_x, L0_attn_W_dt, L0_attn_b_dt, L0_attn_D, L0_attn_W_out)
    h = h + _L0_ffn_ref(_layernorm(h, axis=-1), L0_ffn_W_gate, L0_ffn_W_qkv)
    return h

_drawn_inputs = setup_inputs


def setup_inputs(seed=0):
    import zlib

    import numpy as np

    out = dict(_drawn_inputs(seed))
    spreads = {'L0_tok_inv_A_real': (-0.6931471824645996, 0.2), 'L0_attn_D': (1.0, 0.2)}
    factors = {}
    for name, (base, spread) in spreads.items():
        noise = np.random.default_rng([zlib.crc32(name.encode()), seed]).standard_normal(out[name].shape)
        drawn = base * np.exp(spread * noise) if base else spread * noise
        out[name] = jnp.asarray(drawn.astype(out[name].dtype))
    for name, factor in factors.items():
        out[name] = (out[name] * factor).astype(out[name].dtype)
    return out
```

```python
import numpy as np
from contextlib import ExitStack
import concourse.bass as bass
from concourse import mybir
from concourse.alu_op_type import AluOpType as ALU

F32 = mybir.dt.float32
F32R = mybir.dt.float32r
BF16 = mybir.dt.bfloat16
F16 = mybir.dt.float16
ACT = mybir.ActivationFunctionType
AX = mybir.AxisListType.X

P = 128
ROWS, STEPS, MODES, LEN = 16, 192, 64, 512
NF = LEN // P
INTER = 1024
NI = INTER // P
HEADS, HD = 16, 32
EPS = 1e-5

NK, NA, NB = NF, 16, 8
NT = NA + NB + NK
SUB = 8
ROUNDS = STEPS // SUB
TWO_PI = 6.283185
ROUND = 12582912.0
LOG2_E = 1.4426950408889634
LN2_HI, LN2_LO = 0.693359375, -2.12194440e-4
EXP_POLY = [1 / 5040, 1 / 720, 1 / 120, 1 / 24, 1 / 6, 1 / 2, 1.0]

CS = 32
CHUNKS = STEPS // CS
CT = ROWS * CS

PAIRS = ROWS // 2
PT = 2 * STEPS
QB = 64
NQ = STEPS // QB
GATE_COLS, KV_BANK = HEADS, (336, 352, 352)
VC = 3 * HD + 1


def steps_tables():
    return np.array([8 * i for i in range(NA)] + list(range(NB)) + [P * k for k in range(NK)], np.float32)


def build(nc, log_dt, a_imag, inv_a_real, b_ri, x_ri, w_x, conv_t, w_z, w_out, skip_d,
          w_q, w_kvg, mults, ident, mask_t, diag, rev, out, dbg=None, upto=3):
    ctx = ExitStack()
    with ctx:
        def sem(name):
            return ctx.enter_context(nc.semaphore(name))

        tok = ctx.enter_context(nc.sbuf_tensor("tok", [P, NF, ROWS, STEPS], F32))
        out_done = sem("out_done")
        stage_one(nc, tok, log_dt, a_imag, inv_a_real, b_ri, x_ri, w_x, conv_t, mults, ctx, sem,
                  w_z, w_out, skip_d, upto)
        if upto >= 3:
            stage_three(nc, tok, w_q, w_kvg, ident, mask_t, diag, rev, out, sem, out_done)
        if dbg is not None:
            with nc.Block() as block:
                @block.sync
                def _(sp):
                    sp.dma_start(dbg, tok[:, :, :, :]).then_inc(out_done, 16)
                    sp.wait_ge(out_done, 16)


def stage_one(nc, tok, log_dt, a_imag, inv_a_real, b_ri, x_ri, w_x, conv_t, mults, ctx, sem,
              w_z, w_out, skip_d, upto):
    wc_ctx = ExitStack()
    with wc_ctx:
        wc_hi = wc_ctx.enter_context(nc.sbuf_tensor("wc_hi", [P, NF, INTER], F32R))
        wc_lo = wc_ctx.enter_context(nc.sbuf_tensor("wc_lo", [P, NF, INTER], F32R))
        with ExitStack() as t:
            tokens_stage(nc, t, tok, wc_hi, wc_lo, log_dt, a_imag, inv_a_real, b_ri, x_ri, w_x, conv_t, mults, sem)
        if upto >= 2:
            with ExitStack() as t:
                mlp_stage(nc, t, tok, wc_hi, wc_lo, w_z, w_out, skip_d, sem)


def tokens_stage(nc, t, tok, wc_hi, wc_lo, log_dt, a_imag, inv_a_real, b_ri, x_ri, w_x, conv_t, mults, sem):
    def sb(name, shape, dt=F32):
        return t.enter_context(nc.sbuf_tensor(name, shape, dt))

    H = STEPS
    dar = sb("dt_and_a_real", [P, 2, H])
    ld, ar = dar[:, 0, :], dar[:, 1, :]
    ai = sb("a_imag_b", [P, H])
    br = sb("b_re", [P, H])
    bi = sb("b_im", [P, H])
    mul = sb("mults_b", [P, NT])
    xre = sb("xre", [P, H, ROWS])
    xim = sb("xim", [P, H, ROWS])
    conv_s = sb("conv_s", [P, 2, INTER])
    wx_s = sb("wx_s", [P, 2, LEN])
    pw = sb("powers", [P, H, 2, NT])
    flat = tok[:, :, :, :].rearrange("p a c s -> p (a c s)")
    phase = flat[:, 0:H * NT].rearrange("p (h n) -> p h n", n=NT)
    decay = flat[:, H * NT:2 * H * NT].rearrange("p (h n) -> p h n", n=NT)
    small = [sb(f"small{i}", [P, H]) for i in range(8)]
    q1 = sb("q1", [P, H, NK])
    q2 = sb("q2", [P, H, NK])
    t1 = sb("t1", [P, 2, SUB, NA, NB])
    t2 = sb("t2", [P, 2, SUB, NA, NB])
    z2 = sb("z2", [P, 2, SUB, ROWS, NK])
    cp = sb("cp", [P, 2, SUB, ROWS, NK])
    ek, er, ep = (sb(name, [P, 2, H]) for name in ("exp_whole", "exp_rest", "exp_poly"))
    e2 = sb("exp_bits", [P, 2, H], mybir.dt.int32)
    halfpi = sb("halfpi", [P, 1])
    minus_halfpi = sb("minus_halfpi", [P, 1])

    banks = t.enter_context(nc.psum_tensor("wc_ps", [P, NF, 2, 512], F32))

    consts_in = sem("consts_in")
    x_in = sem("x_in")
    wload = [sem("wload0"), sem("wload1")]
    w_used = sem("w_used")
    dt_ready = sem("dt_ready")
    angle_ready = sem("angle_ready")
    decay_arg = sem("decay_arg")
    decay_ready = sem("decay_ready")
    sines = sem("sines")
    powers = sem("powers")
    g_exp = sem("g_exp")
    tables = sem("tables")
    chain = sem("dve_chain")
    t2_ready = sem("t2_ready")
    z2_ready = sem("z2_ready")
    t1_ready = sem("t1_ready")
    z1_ready = sem("z1_ready")
    u_ready = sem("u_ready")
    cp_ready = sem("cp_ready")
    round_done = sem("round_done")
    tok_ready = sem("tok_ready")
    wc_done = sem("wc_done")
    wc_hi_ready = sem("wc_hi_ready")
    wc_lo_ready = sem("wc_lo_ready")

    block = t.enter_context(nc.Block())

    @block.sync
    def _(sp):
        sp.dma_start(ld, log_dt.rearrange("(o h) -> o h", o=1).broadcast_to([P, H])).then_inc(consts_in, 16)
        for half in (slice(0, MODES), slice(MODES, P)):
            sp.dma_start(ai[half, :], a_imag).then_inc(consts_in, 16)
            sp.dma_start(dar[half, 1, :], inv_a_real).then_inc(consts_in, 16)
            sp.dma_start(br[half, :], b_ri[0]).then_inc(consts_in, 16)
            sp.dma_start(bi[half, :], b_ri[1]).then_inc(consts_in, 16)
        sp.dma_start(mul[:, :], mults.rearrange("(o h) -> o h", o=1).broadcast_to([P, NT])).then_inc(consts_in, 16)

        def load_w(k, slot):
            sp.dma_start(conv_s[:, slot, :], conv_t[bass.ds(k * P, P), :]).then_inc(wload[slot], 16)
            sp.dma_start(wx_s[:, slot, :], w_x[bass.ds(k * P, P), :]).then_inc(wload[slot], 16)

        load_w(0, 0)
        load_w(1, 1)
        for half in (slice(0, MODES), slice(MODES, P)):
            sp.dma_start(xre[half, :, :], x_ri[0]).then_inc(x_in, 16)
            sp.dma_start(xim[half, :, :], x_ri[1]).then_inc(x_in, 16)
        with sp.Fori(0, NI // 2 - 1) as i:
            for slot in range(2):
                sp.wait_ge(w_used, 2 * i + slot + 1)
                load_w(2 * i + 2 + slot, slot)

    @block.gpsimd
    def _(pool):
        pool.wait_ge(angle_ready, 1)
        nc.gpsimd.tensor_tensor(decay, small[1][:, :].unsqueeze(2).to_broadcast([P, H, NT]),
                                mul[:, :].unsqueeze(1).to_broadcast([P, H, NT]), ALU.mult).then_inc(decay_arg, 1)
        pool.wait_ge(tables, 1)
        pool.wait_ge(x_in, 64)
        with pool.Fori(0, ROUNDS // 2) as i:
            for b in range(2):
                n = 2 * i + b
                hs = bass.ds(n * SUB, SUB)
                pool.wait_ge(u_ready, n + 1)
                nc.gpsimd.tensor_tensor(
                    t2[:, b, :, :, :], pw[:, hs, 1, 0:NA].unsqueeze(3).to_broadcast([P, SUB, NA, NB]),
                    pw[:, hs, 1, NA:NA + NB].unsqueeze(2).to_broadcast([P, SUB, NA, NB]), ALU.mult).then_inc(t2_ready, 1)
                pool.wait_ge(cp_ready, n + 1)
                nc.gpsimd.tensor_tensor(
                    z2[:, b, :, :, :], xim[:, hs, :].unsqueeze(3).to_broadcast([P, SUB, ROWS, NK]),
                    q2[:, hs, :].unsqueeze(2).to_broadcast([P, SUB, ROWS, NK]), ALU.mult).then_inc(z2_ready, 1)

    @block.vector
    def _(dve):
        links = [0]

        def link(ins):
            links[0] += 1
            ins.then_inc(chain, 1)
            dve.wait_ge(chain, links[0])

        def tt(o, a, b, op):
            link(nc.vector.tensor_tensor(o, a, b, op))

        th, adt = small[0][:, :], small[1][:, :]
        dve.sem_inc(u_ready, 2)
        dve.sem_inc(cp_ready, 2)
        nc.vector.memset(halfpi[:, :], TWO_PI / 4).then_inc(dt_ready, 1)
        nc.vector.memset(minus_halfpi[:, :], -TWO_PI / 4).then_inc(dt_ready, 1)
        dve.wait_ge(dt_ready, 2)
        dve.wait_ge(consts_in, 16 * 10)
        whole_k, rest, poly = ek[:, :, :], er[:, :, :], ep[:, :, :]
        x = dar[:, :, :]
        link(nc.vector.tensor_scalar(x, x, -87.0, 88.0, ALU.max, ALU.min))
        link(nc.vector.tensor_scalar(whole_k, x, LOG2_E, ROUND, ALU.mult, ALU.add))
        link(nc.vector.tensor_scalar(whole_k, whole_k, ROUND, None, ALU.subtract))
        link(nc.vector.scalar_tensor_tensor(rest, whole_k, -LN2_HI, x, ALU.mult, ALU.add))
        link(nc.vector.scalar_tensor_tensor(rest, whole_k, -LN2_LO, rest, ALU.mult, ALU.add))
        link(nc.vector.tensor_scalar(poly, rest, EXP_POLY[0], None, ALU.mult))
        for coefficient in EXP_POLY[1:]:
            link(nc.vector.scalar_tensor_tensor(poly, poly, coefficient, rest, ALU.add, ALU.mult))
        link(nc.vector.tensor_scalar(e2[:, :, :], whole_k, 127.0, float(2 ** 23), ALU.add, ALU.mult))
        link(nc.vector.scalar_tensor_tensor(x, poly, 1.0, e2[:, :, :].bitcast(F32), ALU.add, ALU.mult))
        tt(th, ai[:, :], ld, ALU.mult)
        link(nc.vector.tensor_scalar(th, th, float(1 / (2 * np.pi)), None, ALU.mult))
        link(nc.vector.scalar_tensor_tensor(adt, ar, -1.0, ld, ALU.mult, ALU.mult))
        nc.vector.tensor_tensor(phase, small[0][:, :].unsqueeze(2).to_broadcast([P, H, NT]),
                                mul[:, :].unsqueeze(1).to_broadcast([P, H, NT]), ALU.mult).then_inc(angle_ready, 1)
        dve.wait_ge(angle_ready, 1)
        whole = pw[:, :, 0, :]
        link(nc.vector.tensor_scalar(whole, phase, ROUND, ROUND, ALU.add, ALU.subtract))
        nc.vector.tensor_tensor(phase, phase, whole, ALU.subtract).then_inc(angle_ready, 1)
        s2, s3, s4, s5, s6, s7 = (s[:, :] for s in small[2:8])
        tt(s2, ar, ar, ALU.mult)
        tt(s3, ai[:, :], ai[:, :], ALU.mult)
        tt(s2, s2, s3, ALU.add)
        link(nc.vector.reciprocal(s2, s2))
        dve.wait_ge(sines, 1)
        dve.wait_ge(g_exp, 2)
        cosv, sinv = pw[:, :, 0, NA + 1], pw[:, :, 1, NA + 1]
        link(nc.vector.scalar_tensor_tensor(s3, s6, 1.0, s5, ALU.add, ALU.mult))
        tt(s3, s3, cosv, ALU.mult)
        link(nc.vector.scalar_tensor_tensor(s3, cosv, -1.0, s3, ALU.add, ALU.add))
        tt(s4, s6, sinv, ALU.mult)
        tt(s5, s3, ar, ALU.mult)
        tt(s6, s4, ai[:, :], ALU.mult)
        tt(s6, s6, s5, ALU.subtract)
        tt(s6, s6, s2, ALU.mult)
        tt(s4, s4, ar, ALU.mult)
        tt(s3, s3, ai[:, :], ALU.mult)
        link(nc.vector.scalar_tensor_tensor(s4, s4, -1.0, s3, ALU.mult, ALU.subtract))
        tt(s4, s4, s2, ALU.mult)
        tt(s3, br[:, :], s6, ALU.mult)
        tt(s5, bi[:, :], s4, ALU.mult)
        tt(s3, s3, s5, ALU.subtract)
        link(nc.vector.tensor_scalar(s3, s3, 2.0, None, ALU.mult))
        tt(s5, br[:, :], s4, ALU.mult)
        tt(s2, bi[:, :], s6, ALU.mult)
        tt(s5, s5, s2, ALU.add)
        link(nc.vector.tensor_scalar(s5, s5, 2.0, None, ALU.mult))
        gre = small[3][:, :].unsqueeze(2).to_broadcast([P, H, NK])
        gim = small[5][:, :].unsqueeze(2).to_broadcast([P, H, NK])
        dve.wait_ge(sines, 2)
        dve.wait_ge(decay_ready, 1)
        for kind in range(2):
            tt(pw[:, :, kind, :], pw[:, :, kind, :], decay, ALU.mult)
        p1, p2 = pw[:, :, 0, NA + NB:NT], pw[:, :, 1, NA + NB:NT]
        tq = decay[:, :, 0:NK]
        tt(q1[:, :, :], gre, p1, ALU.mult)
        tt(tq, gim, p2, ALU.mult)
        tt(q1[:, :, :], q1[:, :, :], tq, ALU.add)
        tt(q2[:, :, :], gre, p2, ALU.mult)
        tt(tq, gim, p1, ALU.mult)
        nc.vector.tensor_tensor(q2[:, :, :], q2[:, :, :], tq, ALU.subtract).then_inc(tables, 1)
        dve.wait_ge(tables, 1)
        for jc in range(NF):
            for ih in range(2):
                n = 2 * jc + ih
                dve.wait_ge(wc_hi_ready, n + 1)
                nc.vector.tensor_tensor(wc_lo[:, jc, 512 * ih:512 * ih + 512], banks[:, jc, ih, :],
                                        wc_hi[:, jc, 512 * ih:512 * ih + 512].bitcast(F32), ALU.subtract).then_inc(wc_lo_ready, 1)
        dve.wait_ge(x_in, 64)
        with dve.Fori(0, ROUNDS // 2) as i:
            for b in range(2):
                n = 2 * i + b
                hs = bass.ds(n * SUB, SUB)
                dve.wait_ge(round_done, n + 1)
                nc.vector.tensor_tensor(
                    t1[:, b, :, :, :], pw[:, hs, 0, 0:NA].unsqueeze(3).to_broadcast([P, SUB, NA, NB]),
                    pw[:, hs, 0, NA:NA + NB].unsqueeze(2).to_broadcast([P, SUB, NA, NB]), ALU.mult).then_inc(t1_ready, 1)
                nc.vector.tensor_tensor(
                    cp[:, b, :, :, :], xre[:, hs, :].unsqueeze(3).to_broadcast([P, SUB, ROWS, NK]),
                    q1[:, hs, :].unsqueeze(2).to_broadcast([P, SUB, ROWS, NK]), ALU.mult).then_inc(z1_ready, 1)
                dve.wait_ge(t1_ready, n + 1)
                dve.wait_ge(t2_ready, n + 1)
                nc.vector.tensor_tensor(t1[:, b, :, :, :], t1[:, b, :, :, :], t2[:, b, :, :, :], ALU.add).then_inc(u_ready, 1)
                dve.wait_ge(z1_ready, n + 1)
                dve.wait_ge(z2_ready, n + 1)
                nc.vector.tensor_tensor(cp[:, b, :, :, :], cp[:, b, :, :, :], z2[:, b, :, :, :], ALU.add).then_inc(cp_ready, 1)

    @block.scalar
    def _(act):
        act.wait_ge(angle_ready, 1)
        nc.scalar.activation(small[5][:, :], small[1][:, :], ACT.Tanh, scale=0.5).then_inc(g_exp, 1)
        nc.scalar.activation(small[6][:, :], small[1][:, :], ACT.Exp).then_inc(g_exp, 1)
        act.wait_ge(decay_arg, 1)
        nc.scalar.activation(decay, decay, ACT.Exp).then_inc(decay_ready, 1)
        act.wait_ge(angle_ready, 2)
        lo, hi = slice(0, MODES), slice(MODES, P)
        na, nb = slice(0, NA), slice(NA, NA + NB)
        nk = slice(NA + NB, NT)

        def sine(part, kind, cols, sign):
            nc.scalar.activation(pw[part, :, kind, cols], phase[part, :, cols], ACT.Sin, scale=sign * TWO_PI).then_inc(powers, 1)

        sine(hi, 0, na, 1)
        sine(lo, 1, na, -1)
        sine(slice(0, P), 1, nb, 1)
        sine(hi, 0, nk, -1)
        sine(lo, 1, nk, -1)
        act.wait_ge(powers, 5)
        nc.scalar.activation(phase, phase, ACT.Abs).then_inc(powers, 1)
        act.wait_ge(powers, 6)
        act.wait_ge(dt_ready, 2)
        nc.scalar.activation(pw[:, :, 0, nb], phase[:, :, nb], ACT.Sin, bias=halfpi[:, :], scale=-TWO_PI).then_inc(sines, 1)
        nc.scalar.activation(pw[lo, :, 0, na], phase[lo, :, na], ACT.Sin, bias=halfpi[lo, :], scale=-TWO_PI)
        nc.scalar.activation(pw[hi, :, 1, na], phase[hi, :, na], ACT.Sin, bias=halfpi[hi, :], scale=-TWO_PI)
        nc.scalar.activation(pw[lo, :, 0, nk], phase[lo, :, nk], ACT.Sin, bias=halfpi[lo, :], scale=-TWO_PI)
        nc.scalar.activation(pw[hi, :, 1, nk], phase[hi, :, nk], ACT.Sin, bias=minus_halfpi[hi, :], scale=TWO_PI).then_inc(sines, 1)
        act.wait_ge(wc_done, 1)
        for jc in range(NF):
            for ih in range(2):
                nc.scalar.activation(wc_hi[:, jc, 512 * ih:512 * ih + 512], banks[:, jc, ih, :], ACT.Copy).then_inc(wc_hi_ready, 1)
        with act.Fori(0, ROUNDS // 2) as i:
            for b in range(2):
                n = 2 * i + b
                act.wait_ge(round_done, n + 3)
                nc.scalar.activation(
                    tok[:, :, :, bass.ds(n * SUB, SUB)],
                    banks[:, 0, b, :].rearrange("p (h c a) -> p a c h", c=ROWS, a=NK), ACT.Copy).then_inc(tok_ready, 1)

    @block.tensor
    def _(pe):
        def join(slot, first, last):
            for jc in range(NF):
                for ih in range(2):
                    ins = nc.tensor.matmul(banks[:, jc, ih, :], wx_s[:, slot, jc * P:(jc + 1) * P],
                                           conv_s[:, slot, 512 * ih:512 * ih + 512], start=first, stop=last)
            return ins

        pe.sem_inc(round_done, 2)
        pe.wait_ge(wload[0], 32)
        join(0, True, False).then_inc(w_used, 1)
        pe.wait_ge(wload[1], 32)
        join(1, False, False).then_inc(w_used, 1)
        with pe.Fori(0, NI // 2 - 2) as i:
            for slot in range(2):
                pe.wait_ge(wload[slot], 32 * i + 64)
                join(slot, False, False).then_inc(w_used, 1)
        pe.wait_ge(wload[0], 32 * (NI // 2))
        join(0, False, False).then_inc(w_used, 1)
        pe.wait_ge(wload[1], 32 * (NI // 2))
        join(1, False, True).then_inc(wc_done, 1)
        pe.wait_ge(wc_lo_ready, 2)
        pe.sem_inc(tok_ready, 2)
        with pe.Fori(0, ROUNDS // 2) as i:
            for b in range(2):
                n = 2 * i + b
                pe.wait_ge(tok_ready, n + 1)
                pe.wait_ge(u_ready, n + 3)
                pe.wait_ge(cp_ready, n + 3)
                for h in range(SUB):
                    ins = nc.tensor.matmul(banks[:, 0, b, 64 * h:64 * h + 64],
                                           t1[:, b, h, :, :].rearrange("p i j -> p (i j)"),
                                           cp[:, b, h, :, :].rearrange("p c a -> p (c a)"), start=True, stop=True)
                ins.then_inc(round_done, 1)


def split_load(sp, src, stage, done):
    sp.dma_start(stage, src).then_inc(done, 16)


def mlp_stage(nc, t, tok, wc_hi, wc_lo, w_z, w_out, skip_d, sem):
    def sb(name, shape, dt=F32):
        return t.enter_context(nc.sbuf_tensor(name, shape, dt))

    def ps(name, shape):
        return t.enter_context(nc.psum_tensor(name, shape, F32))

    wz_hi = sb("wz_hi", [P, NF, INTER], F32R)
    wz_lo = sb("wz_lo", [P, NF, INTER], F32R)
    wo_hi = sb("wo_hi", [P, NI, LEN], F32R)
    wo_lo = sb("wo_lo", [P, NI, LEN], F32R)
    skip = sb("skip", [P, NI])
    mean_w = sb("mean_w", [P, P])
    eps = sb("eps", [P, 1])
    hsum = sb("hsum", [P, CT])
    cen = sb("cen", [P, NF, CT])
    sq = sb("sq", [P, NF, CT])
    stage = [cen, sq]
    ssum = hsum
    rstd = sb("rstd", [P, CT])
    xn_hi = sb("xn_hi", [P, NF, CT], F32R)
    xn_lo = sb("xn_lo", [P, NF, CT], F32R)
    gate = sb("silu", [P, 2, CT])
    g = gate
    g_hi = sb("g_hi", [P, 2, CT], F32R)
    g_lo = sb("g_lo", [P, 2, CT], F32R)

    y_ps = ps("y_ps", [P, NF, CT])
    z_ps = ps("z_ps", [P, CT])
    x_ps = ps("x_ps", [P, CT])
    mean_ps = ps("mean_ps", [P, CT])
    var_ps = ps("var_ps", [P, CT])

    w_in = [sem(f"mlp_w_in{q}") for q in range(4)]
    skip_in = sem("skip_in")
    whi = sem("mlp_w_hi")
    wlo = sem("mlp_w_lo")
    ready = sem("mlp_consts")
    summed = sem("mlp_summed")
    mean_done = sem("mlp_mean")
    centred = sem("mlp_centred")
    squared = sem("mlp_squared")
    sq_summed = sem("mlp_sq_summed")
    var_done = sem("mlp_var")
    std_ready = sem("mlp_std")
    rstd_ready = sem("mlp_rstd")
    xn_ready = sem("mlp_xn")
    xhi_ready = sem("mlp_xhi")
    xlo_ready = sem("mlp_xlo")
    z_done = sem("z_done")
    x_done = sem("x_done")
    silu_ready = sem("silu_ready")
    g_ready = sem("g_ready")
    ghi_ready = sem("ghi_ready")
    glo_ready = sem("glo_ready")
    y_done = sem("y_done")
    res_ready = sem("mlp_res")

    def quarters():
        for q in range(2):
            yield w_z[:, 2 * q:2 * q + 2, :], wz_hi[:, 2 * q:2 * q + 2, :], wz_lo[:, 2 * q:2 * q + 2, :]
        for q in range(2):
            yield w_out[:, 4 * q:4 * q + 4, :], wo_hi[:, 4 * q:4 * q + 4, :], wo_lo[:, 4 * q:4 * q + 4, :]

    def flat(ap):
        return ap.rearrange("p a b -> p (a b)")

    def chunk(n):
        return tok[:, :, :, bass.ds(n * CS, CS)]

    def rows(ap):
        return ap.rearrange("p (c s) -> p c s", c=ROWS) if len(ap.shape) == 2 else ap.rearrange("p a (c s) -> p a c s", c=ROWS)

    block = t.enter_context(nc.Block())

    @block.sync
    def _(sp):
        sp.dma_start(skip[:, :], skip_d).then_inc(skip_in, 16)
        for q, (src, hi, lo) in enumerate(quarters()):
            if q >= 2:
                sp.wait_ge(wlo, q - 1)
            split_load(sp, src, flat(stage[q % 2][:, :, :]).rearrange("p (a b) -> p a b", b=src.shape[2]), w_in[q])

    @block.scalar
    def _(act):
        for q, (src, hi, lo) in enumerate(quarters()):
            act.wait_ge(w_in[q], 16)
            nc.scalar.activation(flat(hi), flat(stage[q % 2][:, :, :]), ACT.Copy).then_inc(whi, 1)

        def square(n):
            act.wait_ge(centred, n + 1)
            nc.scalar.activation(sq[:, :, :], cen[:, :, :], ACT.Square).then_inc(squared, 1)

        def std(n):
            act.wait_ge(var_done, n + 1)
            nc.scalar.activation(rstd[:, :], var_ps[:, :], ACT.Sqrt, bias=eps[:, :]).then_inc(std_ready, 1)

        def high(n):
            act.wait_ge(xn_ready, n + 1)
            for a in range(NF):
                nc.scalar.activation(xn_hi[:, a, :], cen[:, a, :], ACT.Copy).then_inc(xhi_ready, 1)

        def chunk_steps(n, more):
            def ghi(i):
                act.wait_ge(g_ready, NI * n + i + 1)
                nc.scalar.activation(g_hi[:, i % 2, :], g[:, i % 2, :], ACT.Copy).then_inc(ghi_ready, 1)

            for i in range(NI):
                act.wait_ge(z_done, NI * n + i + 1)
                if i:
                    act.wait_ge(glo_ready, NI * n + i - 1) if i > 1 else None
                nc.scalar.activation(gate[:, i % 2, :], z_ps[:, :], ACT.Silu).then_inc(silu_ready, 1)
                if i:
                    ghi(i - 1)
                if more and i == 1:
                    square(n + 1)
                if more and i == 4:
                    std(n + 1)
            ghi(NI - 1)
            if more:
                act.wait_ge(x_done, NI * n + NI)
                high(n + 1)

        act.wait_ge(ready, 2)
        square(0)
        std(0)
        high(0)
        with act.Fori(0, CHUNKS - 1) as n:
            chunk_steps(n, True)
        chunk_steps(CHUNKS - 1, False)

    @block.vector
    def _(dve):
        nc.vector.memset(mean_w[:, :], 1.0 / LEN).then_inc(ready, 1)
        nc.vector.memset(eps[:, :], EPS).then_inc(ready, 1)
        for q, (src, hi, lo) in enumerate(quarters()):
            dve.wait_ge(whi, q + 1)
            nc.vector.tensor_tensor(flat(lo), flat(stage[q % 2][:, :, :]), flat(hi).bitcast(F32), ALU.subtract).then_inc(wlo, 1)

        def sum_chunk(n):
            nc.vector.tensor_reduce(rows(hsum[:, :]), chunk(n).rearrange("p a c s -> p c s a"), AX, ALU.add).then_inc(summed, 1)

        def centre(n):
            dve.wait_ge(mean_done, n + 1)
            nc.vector.tensor_tensor(rows(cen[:, :, :]), chunk(n),
                                    rows(mean_ps[:, :]).unsqueeze(1).to_broadcast([P, NF, ROWS, CS]), ALU.subtract).then_inc(centred, 1)

        def sum_squares(n):
            dve.wait_ge(squared, n + 1)
            nc.vector.tensor_reduce(ssum[:, :], sq[:, :, :].rearrange("p a t -> p t a"), AX, ALU.add).then_inc(sq_summed, 1)

        def normalise(n):
            dve.wait_ge(std_ready, n + 1)
            nc.vector.reciprocal(rstd[:, :], rstd[:, :]).then_inc(rstd_ready, 1)
            dve.wait_ge(rstd_ready, n + 1)
            nc.vector.tensor_tensor(cen[:, :, :], cen[:, :, :], rstd[:, :].unsqueeze(1).to_broadcast([P, NF, CT]),
                                    ALU.mult).then_inc(xn_ready, 1)

        def low(n):
            for a in range(NF):
                dve.wait_ge(xhi_ready, NF * n + a + 1)
                nc.vector.tensor_tensor(xn_lo[:, a, :], cen[:, a, :], xn_hi[:, a, :].bitcast(F32), ALU.subtract).then_inc(xlo_ready, 1)

        def chunk_steps(n, more):
            for i in range(NI):
                if more and i == 0:
                    sum_chunk(n + 1)
                dve.wait_ge(silu_ready, NI * n + i + 1)
                dve.wait_ge(x_done, NI * n + i + 1)
                nc.vector.scalar_tensor_tensor(g[:, i % 2, :], x_ps[:, :], skip[:, i:i + 1], gate[:, i % 2, :],
                                               ALU.mult, ALU.mult).then_inc(g_ready, 1)
                dve.wait_ge(ghi_ready, NI * n + i + 1)
                nc.vector.tensor_tensor(g_lo[:, i % 2, :], g[:, i % 2, :], g_hi[:, i % 2, :].bitcast(F32), ALU.subtract).then_inc(glo_ready, 1)
                if more and i == 0:
                    centre(n + 1)
                if more and i == 2:
                    sum_squares(n + 1)
                if more and i == 5:
                    normalise(n + 1)
            if more:
                low(n + 1)
            dve.wait_ge(y_done, NI * n + NI)
            nc.vector.tensor_tensor(chunk(n), rows(y_ps[:, :, :]), chunk(n), ALU.add).then_inc(res_ready, 1)

        dve.wait_ge(skip_in, 16)
        sum_chunk(0)
        centre(0)
        sum_squares(0)
        normalise(0)
        low(0)
        with dve.Fori(0, CHUNKS - 1) as n:
            chunk_steps(n, True)
        chunk_steps(CHUNKS - 1, False)

    @block.tensor
    def _(pe):
        def mean(n):
            pe.wait_ge(summed, n + 1)
            nc.tensor.matmul(mean_ps[:, :], mean_w[:, :], hsum[:, :], start=True, stop=True).then_inc(mean_done, 1)

        def var(n):
            pe.wait_ge(sq_summed, n + 1)
            nc.tensor.matmul(var_ps[:, :], mean_w[:, :], ssum[:, :], start=True, stop=True).then_inc(var_done, 1)

        def project(n, acc, hi, lo, i, wait):
            for a in range(NF):
                if wait:
                    pe.wait_ge(xhi_ready, NF * n + a + 1)
                    pe.wait_ge(xlo_ready, NF * n + a + 1)
                cols = slice(i * P, (i + 1) * P)
                nc.tensor.matmul(acc, hi[:, a, cols], xn_hi[:, a, :], start=(a == 0), stop=False)
                nc.tensor.matmul(acc, hi[:, a, cols], xn_lo[:, a, :], start=False, stop=False)
                ins = nc.tensor.matmul(acc, lo[:, a, cols], xn_hi[:, a, :], start=False, stop=(a == NF - 1))
            return ins

        def put_out(n, i):
            pe.wait_ge(ghi_ready, NI * n + i + 1)
            pe.wait_ge(glo_ready, NI * n + i + 1)
            for f in range(NF):
                cols = slice(f * P, (f + 1) * P)
                nc.tensor.matmul(y_ps[:, f, :], wo_hi[:, i, cols], g_hi[:, i % 2, :], start=(i == 0), stop=False)
                nc.tensor.matmul(y_ps[:, f, :], wo_hi[:, i, cols], g_lo[:, i % 2, :], start=False, stop=False)
                ins = nc.tensor.matmul(y_ps[:, f, :], wo_lo[:, i, cols], g_hi[:, i % 2, :], start=False, stop=(i == NI - 1))
            ins.then_inc(y_done, 1)

        def chunk_steps(n, more):
            for i in range(NI):
                if i:
                    pe.wait_ge(silu_ready, NI * n + i)
                project(n, z_ps[:, :], wz_hi, wz_lo, i, i == 0).then_inc(z_done, 1)
                if i:
                    pe.wait_ge(g_ready, NI * n + i)
                project(n, x_ps[:, :], wc_hi, wc_lo, i, False).then_inc(x_done, 1)
                if i:
                    put_out(n, i - 1)
                if more and i == 0:
                    mean(n + 1)
                if more and i == 3:
                    var(n + 1)
            put_out(n, NI - 1)

        pe.wait_ge(ready, 2)
        mean(0)
        var(0)
        pe.wait_ge(wlo, 4)
        with pe.Fori(0, CHUNKS - 1) as n:
            chunk_steps(n, True)
        chunk_steps(CHUNKS - 1, False)


PLACE_MEAN, PLACE_VAR, PLACE_STD, PLACE_XN, PLACE_Q, PLACE_KV, PLACES = 0, 1, 2, 3, 4, 8, 24
PLACE_RES = (2, 3, 20)
TILES = 2 * 2 * NQ
SEGS = 16
TOK_TILES = PT // P


def segments(j):
    return {0: [(False, 0, QB, 0)], 1: [(True, 0, P, 1)], 2: [(True, 0, P, 2), (False, P, QB, 3)]}[j]


def stage_three(nc, tok, w_q, w_kvg, ident_d, mask_d, diag_d, rev_d, out, sem, _):
    t3 = ExitStack()
    with t3:
        attention_stage(nc, t3, tok, w_q, w_kvg, ident_d, mask_d, diag_d, rev_d, out, sem)


class Links:

    def __init__(self, eng, sem, per, n):
        self.eng, self.sem, self.per, self.n, self.k = eng, sem, per, n, 0

    def __call__(self, ins):
        self.k += 1
        ins.then_inc(self.sem, 1)
        self.eng.wait_ge(self.sem, self.n * self.per + self.k)


def attention_stage(nc, t, tok, w_q, w_kvg, ident_d, mask_d, diag_d, rev_d, out, sem):
    def sb(name, shape, dt=F32):
        return t.enter_context(nc.sbuf_tensor(name, shape, dt))

    def ps(name, shape):
        return t.enter_context(nc.psum_tensor(name, shape, F32))

    G = P // HD
    KVG = HEADS + 2 * LEN
    wq_hi = sb("wq_hi", [P, NF, LEN], F32R)
    wq_lo = sb("wq_lo", [P, NF, LEN], F32R)
    wkv_hi = sb("wkv_hi", [P, NF, KVG], F32R)
    wkv_lo = sb("wkv_lo", [P, NF, KVG], F32R)
    ident = sb("ident", [P, P])
    ident_b = sb("ident_b", [P, QB], BF16)
    mask = sb("mask", [P, 2, QB], BF16)
    diag = sb("diag", [P, G])
    rev = sb("rev", [P, HEADS])
    mean_w = sb("mean_w3", [P, P])
    eps = sb("eps3", [P, 1])
    NBLK = PT // QB
    hpair = sb("hpair", [P, 2, NBLK, 2, QB])
    hsum = sb("hsum3", [P, PT])
    mask_f = hsum[:, 0:P]
    cen = sb("cen3", [P, NF, PT])
    sq = sb("sq3", [P, NF, PT])
    rstd = hsum
    xn_hi = sb("xn3_hi", [P, NF, PT], F32R)
    xn_lo = sb("xn3_lo", [P, NF, PT], F32R)
    q_hi = sb("q_hi", [P, 2, 2, NBLK, 2, QB], F32R)
    q_lo = sb("q_lo", [P, 2, 2, NBLK, 2, QB], F32R)
    kb_hi = sb("kb_hi", [P, 2, G, PT], F32R)
    kb_lo = sb("kb_lo", [P, 2, G, PT], F32R)
    vb = sb("vb", [P, 2, 4, VC], BF16)
    res = sb("res", [P, 2, TILES, P])
    spare = cen[:, :, :].rearrange("p a t -> p (a t)")
    km = spare[:, 0:LEN].rearrange("p (h d) -> p h d", d=HD)
    vm = spare[:, LEN:2 * LEN].rearrange("p (h d) -> p h d", d=HD)
    kex = sq
    ksel = sb("ksel", [P, HD])
    krep = spare[:, 2 * LEN:2 * LEN + P].rearrange("p (g d) -> p g d", d=HD)
    vsel = sb("vsel", [P, TOK_TILES, HD])
    one = sb("one", [P, 1])
    vblk = sb("vblk", [P, 4, HD])
    top = sb("top", [P, TOK_TILES])
    mx = sb("mx", [P, 1])
    below = sb("below", [P, HEADS])
    tie = sb("tie", [P, HEADS])
    tie_mx = sb("tie_mx", [P, 1])
    ind = sb("ind", [P, HEADS])
    gexp = sb("gexp", [P, HEADS])
    gsum = sb("gsum", [P, 1])
    prob = sb("prob", [P, 2, G, P + QB])
    smax = sb("smax", [P, 2, 2, G])
    pt_hi = sb("pt_hi", [P, 4, G * P], F16)
    pt_lo = sb("pt_lo", [P, 4, G * P], F16)
    rsum = sb("rsum", [P, 2, G])
    ysum = sb("ysum", [P, 2, G, HD])

    s_ps = ps("s_ps", [P, 4, 512])
    t_ps = ps("t_ps", [P, 2, 512])
    y_ps = ps("y_ps3", [P, 512])
    fill_ps = ps("fill_ps", [P, 512])

    w_in = [sem(f"qkv_in{i}") for i in range(6)]
    c_in = sem("att_consts_in")
    whi = sem("qkv_hi")
    wlo = sem("qkv_lo")
    ready = sem("att_consts")
    hpair_in = sem("hpair_in")
    summed = sem("att_summed")
    mean_done = sem("att_mean")
    centred = sem("att_centred")
    squared = sem("att_squared")
    sq_summed = sem("att_sq_summed")
    var_done = sem("att_var")
    std_ready = sem("att_std")
    xn_ready = sem("att_xn")
    xhi_ready = sem("att_xhi")
    xlo_ready = sem("att_xlo")
    q_done = sem("q_done")
    qhi_ready = sem("qhi_ready")
    qlo_ready = sem("qlo_ready")
    kv_done = sem("kv_done")
    shift_ready = sem("gate_shift")
    gexp_ready = sem("gate_exp")
    masked = sem("kv_masked")
    ksel_ready = sem("ksel_ready")
    krep_ready = sem("krep_ready")
    kt_done = sem("kt_done")
    kex_ready = sem("kex_ready")
    kbhi_ready = sem("kbhi_ready")
    kblo_ready = sem("kblo_ready")
    vblk_ready = sem("vblk_ready")
    vstep = sem("v_split_step")
    vb_ready = sem("vb_ready")
    res_done = sem("res_transposed")
    res_ready = sem("res_ready")
    link_proj = sem("proj_links")
    link_att = sem("att_links")
    s_done = sem("scores_done")
    less_ready = sem("less_ready")
    p_ready = sem("p_ready")
    t_done = sem("t_done")
    pthi_ready = sem("pthi_ready")
    ptlo_ready = sem("ptlo_ready")
    y_done = sem("y3_done")
    y_read = sem("y_read")
    ysum_ready = sem("ysum_ready")
    o_scaled = sem("o_scaled")
    o_ready = sem("o_ready")
    out_done = [sem("out_done0"), sem("out_done1")]

    def pieces():
        for a in range(NF):
            yield w_kvg[:, a, :], wkv_hi[:, a, :], wkv_lo[:, a, :]
        for a in range(0, NF, 2):
            yield (w_q[:, a:a + 2, :].rearrange("p a b -> p (a b)"), wq_hi[:, a:a + 2, :].rearrange("p a b -> p (a b)"),
                   wq_lo[:, a:a + 2, :].rearrange("p a b -> p (a b)"))

    def landing(i, width):
        return (cen, sq)[i % 2][:, :, :].rearrange("p a b -> p (a b)")[:, 0:width]

    def pair(n):
        return tok[:, :, bass.ds(2 * n, 2), :].rearrange("p a c s -> p a (c s)")

    def blocks(ap):
        return ap.rearrange("p (k q) -> p k q", q=QB)

    def tile(i):
        return i // (2 * NQ), i // NQ % 2, i % NQ

    SCALE = float(HD) ** -0.5
    KV_FILLS = 3
    OUT_CREDIT = 2 * TILES

    block = t.enter_context(nc.Block())

    @block.sync
    def _(sp):
        sp.dma_start(ident[:, :], ident_d).then_inc(c_in, 16)
        sp.dma_start(mask_f, mask_d).then_inc(c_in, 16)
        sp.dma_start(diag[:, :], diag_d).then_inc(c_in, 16)
        sp.dma_start(rev[:, :], rev_d.rearrange("(o h) -> o h", o=1).broadcast_to([P, HEADS])).then_inc(c_in, 16)
        for i, (src, hi, lo) in enumerate(pieces()):
            if i >= 2:
                sp.wait_ge(wlo, i - 1)
            sp.dma_start(landing(i, src.shape[1]), src).then_inc(w_in[i], 16)

        def load_pair(n):
            for g in range(NF):
                sp.dma_start(hpair[:, g // 2, :, g % 2, :], blocks(pair(n)[:, g, :])).then_inc(hpair_in, 16)

        load_pair(0)

        def pair_steps(p, b, last):
            if not last:
                sp.wait_ge(res_ready, 3 * p + 3)
                load_pair(p + 1)
            for r in range(2):
                sp.wait_ge(o_ready, TILES * p + 6 * (r + 1) + OUT_CREDIT)
                for x in range(2):
                    for gh in range(2):
                        g = 2 * x + gh
                        dst = out[bass.ds(2 * p + r, 1), :, P * g:P * (g + 1)].rearrange("r (j q) f -> q (r j) f", q=QB)
                        sp.dma_start(dst, res[gh * QB:(gh + 1) * QB, b, 6 * r + NQ * x:6 * r + NQ * (x + 1), :]).then_inc(out_done[r], 16)

        pair_steps(0, 0, False)
        with sp.Fori(0, PAIRS // 2 - 1) as i:
            pair_steps(2 * i + 1, 1, False)
            pair_steps(2 * i + 2, 0, False)
        pair_steps(PAIRS - 1, 1, True)
        for r in range(2):
            sp.wait_ge(out_done[r], 64 * (PAIRS + 2))

    @block.gpsimd
    def _(pool):
        pool.sem_inc(o_ready, OUT_CREDIT)
        pool.sem_inc(out_done[0], 128)
        pool.sem_inc(out_done[1], 128)
        nc.gpsimd.memset(vblk[:, :, :], 0.0).then_inc(ready, 1)
        nc.gpsimd.memset(one[:, :], 1.0).then_inc(ready, 1)
        for b in range(2):
            nc.gpsimd.memset(vb[:, b, :, VC - 1:VC], 1.0).then_inc(ready, 1)

        def low_keys(n, b, tt):
            pool.wait_ge(kbhi_ready, TOK_TILES * n + tt + 1)
            cols = slice(tt * P, (tt + 1) * P)
            nc.gpsimd.tensor_tensor(kb_lo[:, b, :, cols], kex[:, :, cols], kb_hi[:, b, :, cols].bitcast(F32), ALU.subtract)\
                .then_inc(kblo_ready, 1)

        def split_values(n, b):
            pool.wait_ge(vblk_ready, n + 1)
            step = Links(pool, vstep, 4, n)
            for part in range(3):
                piece = vb[:, b, :, (2 - part) * HD:(3 - part) * HD]
                ins = nc.gpsimd.tensor_tensor(piece, vblk[:, :, :], one[:, :].unsqueeze(2).to_broadcast([P, 4, HD]), ALU.mult)
                if part == 2:
                    ins.then_inc(vb_ready, 1)
                else:
                    step(ins)
                    step(nc.gpsimd.tensor_tensor(vblk[:, :, :], vblk[:, :, :], piece, ALU.subtract))

        def project(n, b, m):
            if PLACE_KV <= m < PLACE_KV + 4 * TOK_TILES and (m - PLACE_KV) % 4 == 3:
                low_keys(n, b, (m - PLACE_KV) // 4)
            if m == PLACE_KV + 4 * TOK_TILES - 1:
                split_values(n, b)

        def finish(p, i):
            r, gp, j = tile(i)
            b = pool_parity[0]
            e = i % 2
            pool.wait_ge(ysum_ready, TILES * p + i + 1)
            if i % 4 == 0:
                pool.wait_ge(res_ready, 3 * p + i // 4 + 1)
            nc.gpsimd.tensor_tensor(ysum[:, e, :, :], ysum[:, e, :, :], rsum[:, e, :].unsqueeze(2).to_broadcast([P, G, HD]), ALU.mult)\
                .then_inc(o_scaled, 1)
            pool.wait_ge(o_scaled, TILES * p + i + 1)
            nc.gpsimd.tensor_tensor(res[:, b, i, :], ysum[:, e, :, :].rearrange("p g d -> p (g d)"),
                                    res[:, b, i, :], ALU.add).then_inc(o_ready, 1)

        pool_parity = [0]

        def pair_steps(p, b, first, last):
            for i in range(TILES):
                if not last:
                    project(p + 1, 1 - b, 2 * i)
                    project(p + 1, 1 - b, 2 * i + 1)
                if i > 0:
                    pool_parity[0] = b
                    finish(p, i - 1)
                elif not first:
                    pool_parity[0] = 1 - b
                    finish(p - 1, TILES - 1)

        pool.wait_ge(ready, 4)
        for m in range(PLACES):
            project(0, 0, m)
        pair_steps(0, 0, True, False)
        with pool.Fori(0, PAIRS // 2 - 1) as i:
            pair_steps(2 * i + 1, 1, False, False)
            pair_steps(2 * i + 2, 0, False, False)
        pair_steps(PAIRS - 1, 1, False, True)
        pool_parity[0] = 1
        finish(PAIRS - 1, TILES - 1)

    @block.scalar
    def _(act):
        act.wait_ge(c_in, 64)
        nc.scalar.activation(mask[:, :, :], mask_f.rearrange("p (g q) -> p g q", g=2), ACT.Copy).then_inc(ready, 1)
        nc.scalar.activation(ident_b[:, :], ident[:, 0:QB], ACT.Copy).then_inc(ready, 1)
        for i, (src, hi, lo) in enumerate(pieces()):
            act.wait_ge(w_in[i], 16)
            nc.scalar.activation(hi, landing(i, src.shape[1]), ACT.Copy).then_inc(whi, 1)

        def project(n, b, m):
            if m == PLACE_VAR:
                act.wait_ge(centred, n + 1)
                nc.scalar.activation(sq[:, :, :], cen[:, :, :], ACT.Square).then_inc(squared, 1)
            if m == PLACE_STD:
                act.wait_ge(var_done, n + 1)
                nc.scalar.activation(rstd[:, :], fill_ps[:, 0:PT], ACT.Sqrt, bias=eps[:, :]).then_inc(std_ready, 1)
            if m in PLACE_RES:
                f = PLACE_RES.index(m)
                act.wait_ge(res_done, 3 * n + f + 1)
                for r in sorted({4 * f // 6, (4 * f + 3) // 6}):
                    act.wait_ge(out_done[r], 64 * (n + 1))
                nc.scalar.activation(res[:, b, 4 * f:4 * f + 4, :], fill_ps[:, :].rearrange("p (i f) -> p i f", i=4), ACT.Copy)\
                    .then_inc(res_ready, 1)
            if m == PLACE_XN:
                act.wait_ge(xn_ready, n + 1)
                for a in range(NF):
                    nc.scalar.activation(xn_hi[:, a, :], cen[:, a, :], ACT.Copy).then_inc(xhi_ready, 1)
            if PLACE_Q <= m < PLACE_KV:
                g = m - PLACE_Q
                act.wait_ge(q_done, NF * n + g + 1)
                nc.scalar.activation(q_hi[:, b, g // 2, :, g % 2, :], blocks(fill_ps[:, 0:PT]), ACT.Copy).then_inc(qhi_ready, 1)
            if PLACE_KV <= m < PLACE_KV + 4 * TOK_TILES:
                tt, part = divmod(m - PLACE_KV, 4)
                if part == 0:
                    act.wait_ge(shift_ready, TOK_TILES * n + tt + 1)
                    nc.scalar.activation(gexp[:, :], below[:, :], ACT.Exp, accum_out=gsum[:, :])\
                        .then_inc(gexp_ready, 1)
                if part == 2:
                    act.wait_ge(ksel_ready, TOK_TILES * n + tt + 1)
                    nc.scalar.activation(krep[:, :, :], ksel[:, :].unsqueeze(1).to_broadcast([P, G, HD]), ACT.Copy)\
                        .then_inc(krep_ready, 1)
                if part == 3:
                    act.wait_ge(kex_ready, TOK_TILES * n + tt + 1)
                    cols = slice(tt * P, (tt + 1) * P)
                    nc.scalar.activation(kb_hi[:, b, :, cols], kex[:, :, cols], ACT.Copy).then_inc(kbhi_ready, 1)

        def exps(p, i):
            r, gp, j = tile(i)
            act.wait_ge(less_ready, SEGS * p + 4 * (i // NQ) + segments(j)[-1][3] + 1)
            lo = 0 if segments(j)[0][0] else P
            hi = P + QB if not segments(j)[-1][0] else P
            nc.scalar.activation(prob[:, i % 2, :, lo:hi], prob[:, i % 2, :, lo:hi], ACT.Exp, scale=SCALE).then_inc(p_ready, 1)

        def high(p, i):
            for wide, k0, keys, s in segments(i % NQ):
                s += 4 * (i // NQ)
                act.wait_ge(t_done, SEGS * p + s + 1)
                nc.scalar.activation(pt_hi[0:keys, s % 4, :], t_ps[0:keys, s % 2, :], ACT.Copy).then_inc(pthi_ready, 1)

        def pair_steps(p, b, first, last):
            for i in range(TILES):
                if i + 1 < TILES:
                    exps(p, i + 1)
                elif not last:
                    exps(p + 1, 0)
                if not last:
                    project(p + 1, 1 - b, 2 * i)
                high(p, i)
                if not last:
                    project(p + 1, 1 - b, 2 * i + 1)

        act.wait_ge(ready, 8)
        for m in range(PLACES):
            project(0, 0, m)
        exps(0, 0)
        pair_steps(0, 0, True, False)
        with act.Fori(0, PAIRS // 2 - 1) as i:
            pair_steps(2 * i + 1, 1, False, False)
            pair_steps(2 * i + 2, 0, False, False)
        pair_steps(PAIRS - 1, 1, False, True)

    @block.vector
    def _(dve):
        nc.vector.memset(mean_w[:, :], 1.0 / LEN).then_inc(ready, 1)
        nc.vector.memset(eps[:, :], EPS).then_inc(ready, 1)
        dve.sem_inc(ptlo_ready, 2)
        dve.sem_inc(y_read, 1)
        for i, (src, hi, lo) in enumerate(pieces()):
            dve.wait_ge(whi, i + 1)
            nc.vector.tensor_tensor(lo, landing(i, src.shape[1]), hi.bitcast(F32), ALU.subtract).then_inc(wlo, 1)
        PROJ_LINKS = 1 + TOK_TILES * 5 + 1 + 1
        links = [None]

        def over_heads(x, heads):
            return x[:, heads].unsqueeze(2).to_broadcast([P, heads.stop - heads.start, HD])

        def by_head(x):
            return x.rearrange("p (h d) -> p h d", d=HD)

        def project(n, b, m):
            if m == PLACE_MEAN:
                links[0] = Links(dve, link_proj, PROJ_LINKS, n)
                nc.vector.tensor_reduce(hsum[:, :], pair(n).rearrange("p a t -> p t a"), AX, ALU.add).then_inc(summed, 1)
                dve.wait_ge(mean_done, n + 1)
                nc.vector.tensor_tensor(cen[:, :, :], pair(n), fill_ps[:, 0:PT].unsqueeze(1).to_broadcast([P, NF, PT]),
                                        ALU.subtract).then_inc(centred, 1)
            if m == PLACE_VAR:
                dve.wait_ge(squared, n + 1)
                nc.vector.tensor_reduce(hsum[:, :], sq[:, :, :].rearrange("p a t -> p t a"), AX, ALU.add).then_inc(sq_summed, 1)
            if m == PLACE_XN:
                dve.wait_ge(std_ready, n + 1)
                links[0](nc.vector.reciprocal(rstd[:, :], rstd[:, :]))
                nc.vector.tensor_tensor(cen[:, :, :], cen[:, :, :], rstd[:, :].unsqueeze(1).to_broadcast([P, NF, PT]),
                                        ALU.mult).then_inc(xn_ready, 1)
                for a in range(NF):
                    dve.wait_ge(xhi_ready, NF * n + a + 1)
                    nc.vector.tensor_tensor(xn_lo[:, a, :], cen[:, a, :], xn_hi[:, a, :].bitcast(F32), ALU.subtract)\
                        .then_inc(xlo_ready, 1)
            if PLACE_Q <= m < PLACE_KV:
                g = m - PLACE_Q
                dve.wait_ge(qhi_ready, NF * n + g + 1)
                nc.vector.tensor_tensor(q_lo[:, b, g // 2, :, g % 2, :], blocks(fill_ps[:, 0:PT]),
                                        q_hi[:, b, g // 2, :, g % 2, :].bitcast(F32), ALU.subtract)\
                    .then_inc(qlo_ready, 1)
            if PLACE_KV <= m < PLACE_KV + 4 * TOK_TILES:
                tt, part = divmod(m - PLACE_KV, 4)
                kv_part(n, b, tt, part)

        def kv_part(n, b, tt, part):
            link = links[0]
            if part < KV_FILLS:
                dve.wait_ge(kv_done, KV_FILLS * (TOK_TILES * n + tt) + part + 1)
            if part == 0:
                logits = fill_ps[:, 0:HEADS]
                link(nc.vector.tensor_reduce(mx[:, :], logits, AX, ALU.max))
                nc.vector.tensor_scalar(below[:, :], logits, mx[:, :], None, ALU.subtract).then_inc(shift_ready, 1)
                dve.wait_ge(shift_ready, TOK_TILES * n + tt + 1)
                link(nc.vector.scalar_tensor_tensor(tie[:, :], below[:, :], 0.0, rev[:, :], ALU.is_equal, ALU.mult))
                link(nc.vector.tensor_reduce(tie_mx[:, :], tie[:, :], AX, ALU.max))
                link(nc.vector.tensor_scalar(ind[:, :], tie[:, :], tie_mx[:, :], None, ALU.is_equal))
                nc.vector.tensor_tensor(km[:, 0:10, :], by_head(fill_ps[:, 16:336]), over_heads(ind, slice(0, 10)), ALU.mult)\
                    .then_inc(masked, 1)
            if part == 1:
                nc.vector.tensor_tensor(km[:, 10:16, :], by_head(fill_ps[:, 0:192]), over_heads(ind, slice(10, 16)), ALU.mult)
                nc.vector.tensor_tensor(vm[:, 0:5, :], by_head(fill_ps[:, 192:352]), over_heads(ind, slice(0, 5)), ALU.mult)\
                    .then_inc(masked, 1)
                dve.wait_ge(masked, KV_FILLS * (TOK_TILES * n + tt) + 2)
                nc.vector.tensor_reduce(ksel[:, :], km[:, :, :].rearrange("p h d -> p d h"), AX, ALU.add).then_inc(ksel_ready, 1)
            if part == 2:
                nc.vector.tensor_tensor(vm[:, 5:16, :], by_head(fill_ps[:, 0:352]), over_heads(ind, slice(5, 16)), ALU.mult)\
                    .then_inc(masked, 1)
                dve.wait_ge(gexp_ready, TOK_TILES * n + tt + 1)
                nc.vector.reciprocal(top[:, tt:tt + 1], gsum[:, :])
                dve.wait_ge(masked, KV_FILLS * (TOK_TILES * n + tt) + 3)
                link(nc.vector.tensor_reduce(vsel[:, tt, :], vm[:, :, :].rearrange("p h d -> p d h"), AX, ALU.add))
            if part == 3:
                dve.wait_ge(kt_done, TOK_TILES * n + tt + 1)
                nc.vector.tensor_tensor(kex[:, :, tt * P:(tt + 1) * P], fill_ps[:, 0:P].unsqueeze(1).to_broadcast([P, G, P]),
                                        diag[:, :].unsqueeze(2).to_broadcast([P, G, P]), ALU.mult).then_inc(kex_ready, 1)
                if tt == TOK_TILES - 1:
                    link(nc.vector.tensor_tensor(vsel[:, :, :], vsel[:, :, :], top[:, :].unsqueeze(2).to_broadcast([P, TOK_TILES, HD]),
                                                 ALU.mult))
                    nc.vector.tensor_copy(vblk[:, 0, :], vsel[:, 0, :])
                    nc.vector.tensor_copy(vblk[0:QB, 1, :], vsel[0:QB, 1, :])
                    nc.vector.tensor_copy(vblk[0:QB, 2, :], vsel[QB:P, 1, :])
                    nc.vector.tensor_copy(vblk[QB:P, 2, :], vsel[0:QB, 2, :])
                    link(nc.vector.tensor_copy(vblk[0:QB, 3, :], vsel[QB:P, 2, :]))
                    dve.sem_inc(vblk_ready, 1)
                    assert link.k == PROJ_LINKS, link.k

        def softmax(p, i):
            e = i % 2
            base = SEGS * p + 4 * (i // NQ)
            segs = segments(i % NQ)
            dve.wait_ge(s_done, TILES * p + i + 1)
            for wide, k0, keys, s in segs:
                ins = nc.vector.tensor_reduce(smax[:, e, 0 if wide else 1, :],
                                              s_ps[:, s, 0:G * keys].rearrange("p (g k) -> p g k", k=keys), AX, ALU.max)
                ins.then_inc(link_att, 1)
            done = 5 * (i // NQ) + (1, 2, 4)[i % NQ]
            dve.wait_ge(link_att, 20 * p + done)
            which = 0 if segs[0][0] else 1
            if len(segs) == 2:
                nc.vector.tensor_tensor(smax[:, e, 0, :], smax[:, e, 0, :], smax[:, e, 1, :], ALU.max).then_inc(link_att, 1)
                dve.wait_ge(link_att, 20 * p + done + 1)
            for wide, k0, keys, s in segs:
                cols = slice(0, P) if wide else slice(P, P + QB)
                nc.vector.tensor_tensor(prob[:, e, :, cols], s_ps[:, s, 0:G * keys].rearrange("p (g k) -> p g k", k=keys),
                                        smax[:, e, which, :].unsqueeze(2).to_broadcast([P, G, keys]), ALU.subtract)\
                    .then_inc(less_ready, 1)

        def low(p, i):
            for wide, k0, keys, s in segments(i % NQ):
                s += 4 * (i // NQ)
                dve.wait_ge(pthi_ready, SEGS * p + s + 1)
                nc.vector.tensor_tensor(pt_lo[0:keys, s % 4, :], t_ps[0:keys, s % 2, :], pt_hi[0:keys, s % 4, :], ALU.subtract)\
                    .then_inc(ptlo_ready, 1)

        def finish(p, i):
            e = i % 2
            dve.wait_ge(y_done, TILES * p + i + 1)
            dve.wait_ge(o_ready, TILES * p + i - 1 + OUT_CREDIT)
            y = y_ps[:, 0:G * VC].rearrange("p (g v) -> p g v", v=VC)
            nc.vector.reciprocal(rsum[:, e, :], y[:, :, VC - 1])
            nc.vector.tensor_reduce(ysum[:, e, :, :], y[:, :, 0:3 * HD].rearrange("p g (v d) -> p g d v", v=3), AX, ALU.add)\
                .then_inc(ysum_ready, 1)
            dve.wait_ge(ysum_ready, TILES * p + i + 1)
            dve.sem_inc(y_read, 1)

        def pair_steps(p, b, first, last):
            for i in range(TILES):
                if i + 1 < TILES:
                    softmax(p, i + 1)
                elif not last:
                    softmax(p + 1, 0)
                if not last:
                    project(p + 1, 1 - b, 2 * i)
                low(p, i)
                if not last:
                    project(p + 1, 1 - b, 2 * i + 1)
                if i:
                    finish(p, i - 1)
                elif not first:
                    finish(p - 1, TILES - 1)

        dve.wait_ge(ready, 8)
        for m in range(PLACES):
            project(0, 0, m)
        softmax(0, 0)
        pair_steps(0, 0, True, False)
        with dve.Fori(0, PAIRS // 2 - 1) as i:
            pair_steps(2 * i + 1, 1, False, False)
            pair_steps(2 * i + 2, 0, False, False)
        pair_steps(PAIRS - 1, 1, False, True)
        finish(PAIRS - 1, TILES - 1)

    @block.tensor
    def _(pe):
        def three(acc, lh, ll, rh, rl, first, last):
            nc.tensor.matmul(acc, lh, rh, start=first, stop=False)
            nc.tensor.matmul(acc, lh, rl, start=False, stop=False)
            return nc.tensor.matmul(acc, ll, rh, start=False, stop=last)

        def project(n, b, m):
            if m == PLACE_MEAN:
                pe.wait_ge(summed, n + 1)
                if not (isinstance(n, int) and n == 0):
                    pe.wait_ge(res_ready, 3 * n)
                nc.tensor.matmul(fill_ps[:, 0:PT], mean_w[:, :], hsum[:, :], start=True, stop=True).then_inc(mean_done, 1)
            if m == PLACE_VAR:
                pe.wait_ge(sq_summed, n + 1)
                nc.tensor.matmul(fill_ps[:, 0:PT], mean_w[:, :], hsum[:, :], start=True, stop=True).then_inc(var_done, 1)
            if m in PLACE_RES:
                f = PLACE_RES.index(m)
                pe.wait_ge(hpair_in, 64 * n + 64)
                if f == 0:
                    pe.wait_ge(std_ready, n + 1)
                if f == 1:
                    pe.wait_ge(res_ready, 3 * n + 1)
                if f == 2:
                    pe.wait_ge(kex_ready, TOK_TILES * n + TOK_TILES)
                for k in range(4):
                    r, gp, j = tile(4 * f + k)
                    ins = nc.tensor.transpose(fill_ps[:, k * P:(k + 1) * P],
                                              hpair[:, gp, NQ * r + j, :, :].rearrange("p g q -> p (g q)"), ident[:, :])
                ins.then_inc(res_done, 1)
            if PLACE_Q <= m < PLACE_KV:
                g = m - PLACE_Q
                if g == 0:
                    pe.wait_ge(res_ready, 3 * n + 2)
                else:
                    pe.wait_ge(qlo_ready, NF * n + g)
                cols = slice(g * P, (g + 1) * P)
                for a in range(NF):
                    if g == 0:
                        pe.wait_ge(xlo_ready, NF * n + a + 1)
                    ins = three(fill_ps[:, 0:PT], wq_hi[:, a, cols], wq_lo[:, a, cols], xn_hi[:, a, :], xn_lo[:, a, :], a == 0, a == NF - 1)
                ins.then_inc(q_done, 1)
            if PLACE_KV <= m < PLACE_KV + 4 * TOK_TILES:
                tt, part = divmod(m - PLACE_KV, 4)
                if part < KV_FILLS:
                    if part == 0 and tt == 0:
                        pe.wait_ge(qlo_ready, NF * n + NF)
                    elif part == 0:
                        pe.wait_ge(kex_ready, TOK_TILES * n + tt)
                    else:
                        pe.wait_ge(masked, KV_FILLS * (TOK_TILES * n + tt) + part)
                    if part == 1:
                        pe.wait_ge(gexp_ready, TOK_TILES * n + tt + 1)
                    c0 = sum(KV_BANK[:part])
                    cols = slice(c0, c0 + KV_BANK[part])
                    toks = slice(tt * P, (tt + 1) * P)
                    for a in range(NF):
                        ins = three(fill_ps[:, 0:KV_BANK[part]], xn_hi[:, a, toks], xn_lo[:, a, toks],
                                    wkv_hi[:, a, cols], wkv_lo[:, a, cols], a == 0, a == NF - 1)
                    ins.then_inc(kv_done, 1)
                else:
                    pe.wait_ge(krep_ready, TOK_TILES * n + tt + 1)
                    pe.wait_ge(masked, KV_FILLS * (TOK_TILES * n + tt) + 3)
                    nc.tensor.transpose(fill_ps[:, 0:P], krep[:, :, :].rearrange("p g d -> p (g d)"), ident[:, :]).then_inc(kt_done, 1)

        def scores(p, b, i):
            r, gp, j = tile(i)
            if i == 0:
                pe.wait_ge(kblo_ready, TOK_TILES * (p + 1))
                pe.wait_ge(qlo_ready, NF * (p + 1))
            qh, ql = (q[:, b, gp, NQ * r + j, :, :].rearrange("p g q -> p (g q)") for q in (q_hi, q_lo))
            for wide, k0, keys, s in segments(j):
                ks = slice(STEPS * r + k0, STEPS * r + k0 + keys)
                acc = s_ps[:, s, 0:G * keys].rearrange("p (g k) -> p g k", k=keys)
                masked_here = (keys + k0) == QB * (j + 1)
                ins = three(acc, qh, ql, kb_hi[:, b, :, ks], kb_lo[:, b, :, ks], True, not masked_here)
                if masked_here:
                    ins = nc.tensor.matmul(acc[:, :, keys - QB:keys], mask[:, :, :], ident_b[:, :].unsqueeze(1).to_broadcast([P, G, QB]),
                                           start=False, stop=True)
            ins.then_inc(s_done, 1)

        def transposes_free(p, i):
            pe.wait_ge(p_ready, TILES * p + i + 1)
            pe.wait_ge(ptlo_ready, SEGS * p + 4 * (i // NQ) + segments(i % NQ)[0][3] + 1)
            if i % NQ == 2:
                pe.wait_ge(ptlo_ready, SEGS * p + 4 * (i // NQ) + segments(i % NQ)[1][3] + 1)

        def transposes(p, i):
            for wide, k0, keys, s in segments(i % NQ):
                s += 4 * (i // NQ)
                cols = slice(0, P) if wide else slice(P, P + QB)
                for g in range(G):
                    ins = nc.tensor.transpose(t_ps[0:keys, s % 2, g * P:(g + 1) * P], prob[:, i % 2, g, cols], ident[:, :])
                ins.then_inc(t_done, 1)

        def values(p, b, i):
            r, gp, j = tile(i)
            segs = segments(j)
            if i == 0:
                pe.wait_ge(vb_ready, p + 1)
            pe.wait_ge(y_read, TILES * p + i + 1)
            last_seg = SEGS * p + 4 * (i // NQ) + segs[-1][3] + 1
            pe.wait_ge(ptlo_ready, last_seg + 2)
            for g in range(G):
                acc = y_ps[:, g * VC:(g + 1) * VC]
                for x, (wide, k0, keys, s) in enumerate(segs):
                    blk = 2 * r + (k0 > 0)
                    rows = slice(0, keys)
                    v = vb[rows, b, blk, :]
                    nc.tensor.matmul(acc, pt_hi[rows, s, g * P:(g + 1) * P], v, start=(x == 0), stop=False)
                    ins = nc.tensor.matmul(acc[:, HD:VC], pt_lo[rows, s, g * P:(g + 1) * P], v[:, HD:VC], start=False,
                                           stop=(x == len(segs) - 1))
            ins.then_inc(y_done, 1)

        def pair_steps(p, b, first, last):
            for i in range(TILES):
                if not last:
                    project(p + 1, 1 - b, 2 * i)
                if i % NQ == 0:
                    transposes_free(p, i)
                if i + 2 < TILES:
                    scores(p, b, i + 2)
                elif not last:
                    scores(p + 1, 1 - b, i + 2 - TILES)
                if i % NQ:
                    transposes_free(p, i)
                transposes(p, i)
                if not last:
                    project(p + 1, 1 - b, 2 * i + 1)
                if i:
                    values(p, b, i - 1)
                elif not first:
                    values(p - 1, 1 - b, TILES - 1)

        pe.wait_ge(ready, 8)
        pe.wait_ge(wlo, 6)
        for m in range(PLACES):
            project(0, 0, m)
        scores(0, 0, 0)
        scores(0, 0, 1)
        pair_steps(0, 0, True, False)
        with pe.Fori(0, PAIRS // 2 - 1) as i:
            pair_steps(2 * i + 1, 1, False, False)
            pair_steps(2 * i + 2, 0, False, False)
        pair_steps(PAIRS - 1, 1, False, True)
        values(PAIRS - 1, 1, TILES - 1)


def layout(inputs):
    import numpy as _np
    c = _np.ascontiguousarray
    w_in = _np.asarray(inputs["L0_attn_W_in"])
    qkv = _np.asarray(inputs["L0_ffn_W_qkv"])
    width = LEN

    def chunks(w):
        return c(w.reshape(-1, P, w.shape[1]).transpose(1, 0, 2))

    wq, wk, wv = qkv[:width].T, qkv[width:2 * width].T, qkv[2 * width:].T
    kvg = _np.concatenate([_np.asarray(inputs["L0_ffn_W_gate"]).T, wk, wv], axis=1)
    q, k = _np.arange(QB), _np.arange(QB)
    mask_t = _np.zeros((P, 2, QB), _np.float32)
    mask_t[:QB] = _np.where(k[:, None, None] > q[None, None, :], _np.float32(-1e30), _np.float32(0))
    diag = (_np.arange(P)[:, None] // HD == _np.arange(P // HD)[None, :]).astype(_np.float32)
    return {
        "log_dt": c(inputs["L0_tok_log_dt"]),
        "a_imag": c(_np.asarray(inputs["L0_tok_A_imag"]).T),
        "inv_a_real": c(_np.asarray(inputs["L0_tok_inv_A_real"]).T),
        "b_ri": c(_np.asarray(inputs["L0_tok_B_ri"]).transpose(2, 1, 0)),
        "x_ri": c(_np.asarray(inputs["x"]).transpose(3, 2, 1, 0)),
        "w_x": c(w_in[:INTER]),
        "conv_t": c(_np.asarray(inputs["L0_attn_conv_w"]).T),
        "w_z": chunks(w_in[INTER:].T),
        "w_out": chunks(_np.asarray(inputs["L0_attn_W_out"]).T),
        "skip_d": c(_np.asarray(inputs["L0_attn_D"]).reshape(NI, P).T),
        "w_q": chunks(wq),
        "w_kvg": chunks(kvg),
        "mults": steps_tables(),
        "ident": _np.eye(P, dtype=_np.float32),
        "mask_t": c(mask_t.reshape(P, P)),
        "diag": diag,
        "rev": _np.arange(HEADS, 0, -1).astype(_np.float32),
    }


def kernel(**inputs):
    import concourse.bacc as _bacc
    from concourse import mybir as _mybir
    from concourse.bass_utils import run_bass_kernel_spmd as _run

    nc = _bacc.Bacc("TRN2", target_bir_lowering=False, num_devices=1)
    arrays = {f"in_{k}": a for k, a in layout(inputs).items()}
    args = [nc.dram_tensor(k, a.shape, _mybir.dt.from_np(a.dtype), kind="ExternalInput").ap() for k, a in arrays.items()]
    out = nc.dram_tensor("out_0", (ROWS, STEPS, LEN), F32, kind="ExternalOutput").ap()
    build(nc, *args, out)
    r = _run(nc, [arrays], core_ids=[0])
    return r.results[0]["out_0"]
```

```python
import numpy as np
from contextlib import ExitStack
import concourse.bass as bass
from concourse import mybir
from concourse.alu_op_type import AluOpType as ALU

F32 = mybir.dt.float32
F32R = mybir.dt.float32r
BF16 = mybir.dt.bfloat16
F16 = mybir.dt.float16
ACT = mybir.ActivationFunctionType
AX = mybir.AxisListType.X

P = 128
ROWS, STEPS, MODES, LEN = 16, 192, 64, 512
NF = LEN // P
INTER = 1024
NI = INTER // P
HEADS, HD = 16, 32
EPS = 1e-5

NK, NA, NB = NF, 16, 8
NT = NA + NB + NK
SUB = 8
ROUNDS = STEPS // SUB
TWO_PI = 6.283185
ROUND = 12582912.0
LOG2_E = 1.4426950408889634
LN2_HI, LN2_LO = 0.693359375, -2.12194440e-4
EXP_POLY = [1 / 5040, 1 / 720, 1 / 120, 1 / 24, 1 / 6, 1 / 2, 1.0]

CS = 32
CHUNKS = STEPS // CS
CT = ROWS * CS

PAIRS = ROWS // 2
PT = 2 * STEPS
QB = 64
NQ = STEPS // QB
GATE_COLS, KV_BANK = HEADS, (336, 352, 352)
VC = 3 * HD + 1
KVG = HEADS + 2 * LEN

SPARE = NF * LEN + NF * KVG


def steps_tables():
    return np.array([8 * i for i in range(NA)] + list(range(NB)) + [P * k for k in range(NK)], np.float32)


def build(nc, log_dt, a_imag, inv_a_real, b_ri, x_ri, w_x, conv_t, w_z, w_out, skip_d,
          w_q, w_kvg, mults, ident, mask_t, diag, rev, out):
    ctx = ExitStack()
    with ctx:
        def sem(name):
            return ctx.enter_context(nc.semaphore(name))

        tok = ctx.enter_context(nc.sbuf_tensor("tok", [P, NF, ROWS, STEPS], F32))
        spare = ctx.enter_context(nc.sbuf_tensor("spare", [P, SPARE], F32))
        qkv_in = [sem(f"qkv_in{i}") for i in range(NF + 1)]
        with ExitStack() as two:
            wc_hi = two.enter_context(nc.sbuf_tensor("wc_hi", [P, NF, INTER], F32R))
            wc_lo = two.enter_context(nc.sbuf_tensor("wc_lo", [P, NF, INTER], F32R))
            with ExitStack() as t:
                tokens_stage(nc, t, tok, spare, wc_hi, wc_lo, log_dt, a_imag, inv_a_real, b_ri, x_ri, w_x, conv_t, mults, sem)
            with ExitStack() as t:
                mlp_stage(nc, t, tok, spare, wc_hi, wc_lo, w_z, w_out, skip_d, w_q, w_kvg, qkv_in, sem)
        with ExitStack() as t:
            attention_stage(nc, t, tok, spare, qkv_in, ident, mask_t, diag, rev, out, sem)


def tokens_stage(nc, t, tok, spare, wc_hi, wc_lo, log_dt, a_imag, inv_a_real, b_ri, x_ri, w_x, conv_t, mults, sem):
    def sb(name, shape, dt=F32):
        return t.enter_context(nc.sbuf_tensor(name, shape, dt))

    H = STEPS
    dar = sb("dt_and_a_real", [P, 2, H])
    ld, ar = dar[:, 0, :], dar[:, 1, :]
    ai = sb("a_imag_b", [P, H])
    br = sb("b_re", [P, H])
    bi = sb("b_im", [P, H])
    mul = sb("mults_b", [P, NT])
    xre, xim = (spare[:, part * H * ROWS:(part + 1) * H * ROWS].rearrange("p (h c) -> p h c", c=ROWS) for part in range(2))
    conv_s = sb("conv_s", [P, 2, INTER])
    wx_s = sb("wx_s", [P, 2, LEN])
    pw = sb("powers", [P, H, 2, NT])
    flat = tok[:, :, :, :].rearrange("p a c s -> p (a c s)")
    phase = flat[:, 0:H * NT].rearrange("p (h n) -> p h n", n=NT)
    decay = flat[:, H * NT:2 * H * NT].rearrange("p (h n) -> p h n", n=NT)
    small = [sb(f"small{i}", [P, H]) for i in range(8)]
    q1 = sb("q1", [P, H, NK])
    q2 = sb("q2", [P, H, NK])
    t1 = sb("t1", [P, 2, SUB, NA, NB])
    t2 = sb("t2", [P, 2, SUB, NA, NB])
    z2 = sb("z2", [P, 2, SUB, ROWS, NK])
    cp = sb("cp", [P, 2, SUB, ROWS, NK])
    ek, er, ep = (sb(name, [P, 2, H]) for name in ("exp_whole", "exp_rest", "exp_poly"))
    e2 = sb("exp_bits", [P, 2, H], mybir.dt.int32)
    halfpi = sb("halfpi", [P, 1])
    minus_halfpi = sb("minus_halfpi", [P, 1])

    banks = t.enter_context(nc.psum_tensor("wc_ps", [P, NF, 2, 512], F32))

    consts_in = sem("consts_in")
    x_in = sem("x_in")
    wload = [sem("wload0"), sem("wload1")]
    w_used = sem("w_used")
    dt_ready = sem("dt_ready")
    angle_ready = sem("angle_ready")
    decay_arg = sem("decay_arg")
    decay_ready = sem("decay_ready")
    sines = sem("sines")
    powers = sem("powers")
    g_exp = sem("g_exp")
    tables = sem("tables")
    chain = sem("dve_chain")
    t2_ready = sem("t2_ready")
    z2_ready = sem("z2_ready")
    t1_ready = sem("t1_ready")
    z1_ready = sem("z1_ready")
    u_ready = sem("u_ready")
    cp_ready = sem("cp_ready")
    round_done = sem("round_done")
    tok_ready = sem("tok_ready")
    wc_done = sem("wc_done")
    wc_hi_ready = sem("wc_hi_ready")
    wc_lo_ready = sem("wc_lo_ready")

    block = t.enter_context(nc.Block())

    @block.sync
    def _(sp):
        sp.dma_start(ld, log_dt.rearrange("(o h) -> o h", o=1).broadcast_to([P, H])).then_inc(consts_in, 16)
        for half in (slice(0, MODES), slice(MODES, P)):
            sp.dma_start(ai[half, :], a_imag).then_inc(consts_in, 16)
            sp.dma_start(dar[half, 1, :], inv_a_real).then_inc(consts_in, 16)
            sp.dma_start(br[half, :], b_ri[0]).then_inc(consts_in, 16)
            sp.dma_start(bi[half, :], b_ri[1]).then_inc(consts_in, 16)
        sp.dma_start(mul[:, :], mults.rearrange("(o h) -> o h", o=1).broadcast_to([P, NT])).then_inc(consts_in, 16)

        def load_w(k, slot):
            sp.dma_start(conv_s[:, slot, :], conv_t[bass.ds(k * P, P), :]).then_inc(wload[slot], 16)
            sp.dma_start(wx_s[:, slot, :], w_x[bass.ds(k * P, P), :]).then_inc(wload[slot], 16)

        load_w(0, 0)
        load_w(1, 1)
        for half in (slice(0, MODES), slice(MODES, P)):
            sp.dma_start(xre[half], x_ri[0]).then_inc(x_in, 16)
            sp.dma_start(xim[half], x_ri[1]).then_inc(x_in, 16)
        with sp.Fori(0, NI // 2 - 1) as i:
            for slot in range(2):
                sp.wait_ge(w_used, 2 * i + slot + 1)
                load_w(2 * i + 2 + slot, slot)

    @block.gpsimd
    def _(pool):
        pool.wait_ge(angle_ready, 1)
        nc.gpsimd.tensor_tensor(decay, small[1][:, :].unsqueeze(2).to_broadcast([P, H, NT]),
                                mul[:, :].unsqueeze(1).to_broadcast([P, H, NT]), ALU.mult).then_inc(decay_arg, 1)
        pool.wait_ge(tables, 1)
        pool.wait_ge(x_in, 64)
        with pool.Fori(0, ROUNDS // 2) as i:
            for b in range(2):
                n = 2 * i + b
                hs = bass.ds(n * SUB, SUB)
                pool.wait_ge(u_ready, n + 1)
                nc.gpsimd.tensor_tensor(
                    t2[:, b, :, :, :], pw[:, hs, 1, 0:NA].unsqueeze(3).to_broadcast([P, SUB, NA, NB]),
                    pw[:, hs, 1, NA:NA + NB].unsqueeze(2).to_broadcast([P, SUB, NA, NB]), ALU.mult).then_inc(t2_ready, 1)
                pool.wait_ge(cp_ready, n + 1)
                nc.gpsimd.tensor_tensor(
                    z2[:, b, :, :, :], xim[:, hs, :].unsqueeze(3).to_broadcast([P, SUB, ROWS, NK]),
                    q2[:, hs, :].unsqueeze(2).to_broadcast([P, SUB, ROWS, NK]), ALU.mult).then_inc(z2_ready, 1)

    @block.vector
    def _(dve):
        links = [0]

        def link(ins):
            links[0] += 1
            ins.then_inc(chain, 1)
            dve.wait_ge(chain, links[0])

        def tt(o, a, b, op):
            link(nc.vector.tensor_tensor(o, a, b, op))

        th, adt = small[0][:, :], small[1][:, :]
        dve.sem_inc(u_ready, 2)
        dve.sem_inc(cp_ready, 2)
        nc.vector.memset(halfpi[:, :], TWO_PI / 4).then_inc(dt_ready, 1)
        nc.vector.memset(minus_halfpi[:, :], -TWO_PI / 4).then_inc(dt_ready, 1)
        dve.wait_ge(dt_ready, 2)
        dve.wait_ge(consts_in, 16 * 10)
        whole_k, rest, poly = ek[:, :, :], er[:, :, :], ep[:, :, :]
        x = dar[:, :, :]
        link(nc.vector.tensor_scalar(x, x, -87.0, 88.0, ALU.max, ALU.min))
        link(nc.vector.tensor_scalar(whole_k, x, LOG2_E, ROUND, ALU.mult, ALU.add))
        link(nc.vector.tensor_scalar(whole_k, whole_k, ROUND, None, ALU.subtract))
        link(nc.vector.scalar_tensor_tensor(rest, whole_k, -LN2_HI, x, ALU.mult, ALU.add))
        link(nc.vector.scalar_tensor_tensor(rest, whole_k, -LN2_LO, rest, ALU.mult, ALU.add))
        link(nc.vector.tensor_scalar(poly, rest, EXP_POLY[0], None, ALU.mult))
        for coefficient in EXP_POLY[1:]:
            link(nc.vector.scalar_tensor_tensor(poly, poly, coefficient, rest, ALU.add, ALU.mult))
        link(nc.vector.tensor_scalar(e2[:, :, :], whole_k, 127.0, float(2 ** 23), ALU.add, ALU.mult))
        link(nc.vector.scalar_tensor_tensor(x, poly, 1.0, e2[:, :, :].bitcast(F32), ALU.add, ALU.mult))
        tt(th, ai[:, :], ld, ALU.mult)
        link(nc.vector.tensor_scalar(th, th, float(1 / (2 * np.pi)), None, ALU.mult))
        link(nc.vector.scalar_tensor_tensor(adt, ar, -1.0, ld, ALU.mult, ALU.mult))
        nc.vector.tensor_tensor(phase, small[0][:, :].unsqueeze(2).to_broadcast([P, H, NT]),
                                mul[:, :].unsqueeze(1).to_broadcast([P, H, NT]), ALU.mult).then_inc(angle_ready, 1)
        dve.wait_ge(angle_ready, 1)
        whole = pw[:, :, 0, :]
        link(nc.vector.tensor_scalar(whole, phase, ROUND, ROUND, ALU.add, ALU.subtract))
        nc.vector.tensor_tensor(phase, phase, whole, ALU.subtract).then_inc(angle_ready, 1)
        s2, s3, s4, s5, s6, s7 = (s[:, :] for s in small[2:8])
        tt(s2, ar, ar, ALU.mult)
        tt(s3, ai[:, :], ai[:, :], ALU.mult)
        tt(s2, s2, s3, ALU.add)
        link(nc.vector.reciprocal(s2, s2))
        dve.wait_ge(sines, 1)
        dve.wait_ge(g_exp, 2)
        cosv, sinv = pw[:, :, 0, NA + 1], pw[:, :, 1, NA + 1]
        link(nc.vector.scalar_tensor_tensor(s3, s6, 1.0, s5, ALU.add, ALU.mult))
        tt(s3, s3, cosv, ALU.mult)
        link(nc.vector.scalar_tensor_tensor(s3, cosv, -1.0, s3, ALU.add, ALU.add))
        tt(s4, s6, sinv, ALU.mult)
        tt(s5, s3, ar, ALU.mult)
        tt(s6, s4, ai[:, :], ALU.mult)
        tt(s6, s6, s5, ALU.subtract)
        tt(s6, s6, s2, ALU.mult)
        tt(s4, s4, ar, ALU.mult)
        tt(s3, s3, ai[:, :], ALU.mult)
        link(nc.vector.scalar_tensor_tensor(s4, s4, -1.0, s3, ALU.mult, ALU.subtract))
        tt(s4, s4, s2, ALU.mult)
        tt(s3, br[:, :], s6, ALU.mult)
        tt(s5, bi[:, :], s4, ALU.mult)
        tt(s3, s3, s5, ALU.subtract)
        link(nc.vector.tensor_scalar(s3, s3, 2.0, None, ALU.mult))
        tt(s5, br[:, :], s4, ALU.mult)
        tt(s2, bi[:, :], s6, ALU.mult)
        tt(s5, s5, s2, ALU.add)
        link(nc.vector.tensor_scalar(s5, s5, 2.0, None, ALU.mult))
        gre = small[3][:, :].unsqueeze(2).to_broadcast([P, H, NK])
        gim = small[5][:, :].unsqueeze(2).to_broadcast([P, H, NK])
        dve.wait_ge(sines, 2)
        dve.wait_ge(decay_ready, 1)
        for kind in range(2):
            tt(pw[:, :, kind, :], pw[:, :, kind, :], decay, ALU.mult)
        p1, p2 = pw[:, :, 0, NA + NB:NT], pw[:, :, 1, NA + NB:NT]
        tq = decay[:, :, 0:NK]
        tt(q1[:, :, :], gre, p1, ALU.mult)
        tt(tq, gim, p2, ALU.mult)
        tt(q1[:, :, :], q1[:, :, :], tq, ALU.add)
        tt(q2[:, :, :], gre, p2, ALU.mult)
        tt(tq, gim, p1, ALU.mult)
        nc.vector.tensor_tensor(q2[:, :, :], q2[:, :, :], tq, ALU.subtract).then_inc(tables, 1)
        dve.wait_ge(tables, 1)
        for jc in range(NF):
            for ih in range(2):
                n = 2 * jc + ih
                dve.wait_ge(wc_hi_ready, n + 1)
                nc.vector.tensor_tensor(wc_lo[:, jc, 512 * ih:512 * ih + 512], banks[:, jc, ih, :],
                                        wc_hi[:, jc, 512 * ih:512 * ih + 512].bitcast(F32), ALU.subtract).then_inc(wc_lo_ready, 1)
        dve.wait_ge(x_in, 64)
        with dve.Fori(0, ROUNDS // 2) as i:
            for b in range(2):
                n = 2 * i + b
                hs = bass.ds(n * SUB, SUB)
                dve.wait_ge(round_done, n + 1)
                nc.vector.tensor_tensor(
                    t1[:, b, :, :, :], pw[:, hs, 0, 0:NA].unsqueeze(3).to_broadcast([P, SUB, NA, NB]),
                    pw[:, hs, 0, NA:NA + NB].unsqueeze(2).to_broadcast([P, SUB, NA, NB]), ALU.mult).then_inc(t1_ready, 1)
                nc.vector.tensor_tensor(
                    cp[:, b, :, :, :], xre[:, hs, :].unsqueeze(3).to_broadcast([P, SUB, ROWS, NK]),
                    q1[:, hs, :].unsqueeze(2).to_broadcast([P, SUB, ROWS, NK]), ALU.mult).then_inc(z1_ready, 1)
                dve.wait_ge(t1_ready, n + 1)
                dve.wait_ge(t2_ready, n + 1)
                nc.vector.tensor_tensor(t1[:, b, :, :, :], t1[:, b, :, :, :], t2[:, b, :, :, :], ALU.add).then_inc(u_ready, 1)
                dve.wait_ge(z1_ready, n + 1)
                dve.wait_ge(z2_ready, n + 1)
                nc.vector.tensor_tensor(cp[:, b, :, :, :], cp[:, b, :, :, :], z2[:, b, :, :, :], ALU.add).then_inc(cp_ready, 1)

    @block.scalar
    def _(act):
        act.wait_ge(angle_ready, 1)
        nc.scalar.activation(small[5][:, :], small[1][:, :], ACT.Tanh, scale=0.5).then_inc(g_exp, 1)
        nc.scalar.activation(small[6][:, :], small[1][:, :], ACT.Exp).then_inc(g_exp, 1)
        act.wait_ge(decay_arg, 1)
        nc.scalar.activation(decay, decay, ACT.Exp).then_inc(decay_ready, 1)
        act.wait_ge(angle_ready, 2)
        lo, hi = slice(0, MODES), slice(MODES, P)
        na, nb = slice(0, NA), slice(NA, NA + NB)
        nk = slice(NA + NB, NT)

        def sine(part, kind, cols, sign):
            nc.scalar.activation(pw[part, :, kind, cols], phase[part, :, cols], ACT.Sin, scale=sign * TWO_PI).then_inc(powers, 1)

        sine(hi, 0, na, 1)
        sine(lo, 1, na, -1)
        sine(slice(0, P), 1, nb, 1)
        sine(hi, 0, nk, -1)
        sine(lo, 1, nk, -1)
        act.wait_ge(powers, 5)
        nc.scalar.activation(phase, phase, ACT.Abs).then_inc(powers, 1)
        act.wait_ge(powers, 6)
        act.wait_ge(dt_ready, 2)
        nc.scalar.activation(pw[:, :, 0, nb], phase[:, :, nb], ACT.Sin, bias=halfpi[:, :], scale=-TWO_PI).then_inc(sines, 1)
        nc.scalar.activation(pw[lo, :, 0, na], phase[lo, :, na], ACT.Sin, bias=halfpi[lo, :], scale=-TWO_PI)
        nc.scalar.activation(pw[hi, :, 1, na], phase[hi, :, na], ACT.Sin, bias=halfpi[hi, :], scale=-TWO_PI)
        nc.scalar.activation(pw[lo, :, 0, nk], phase[lo, :, nk], ACT.Sin, bias=halfpi[lo, :], scale=-TWO_PI)
        nc.scalar.activation(pw[hi, :, 1, nk], phase[hi, :, nk], ACT.Sin, bias=minus_halfpi[hi, :], scale=TWO_PI).then_inc(sines, 1)
        act.wait_ge(wc_done, 1)
        for jc in range(NF):
            for ih in range(2):
                nc.scalar.activation(wc_hi[:, jc, 512 * ih:512 * ih + 512], banks[:, jc, ih, :], ACT.Copy).then_inc(wc_hi_ready, 1)
        with act.Fori(0, ROUNDS // 2) as i:
            for b in range(2):
                n = 2 * i + b
                act.wait_ge(round_done, n + 3)
                nc.scalar.activation(
                    tok[:, :, :, bass.ds(n * SUB, SUB)],
                    banks[:, 0, b, :].rearrange("p (h c a) -> p a c h", c=ROWS, a=NK), ACT.Copy).then_inc(tok_ready, 1)

    @block.tensor
    def _(pe):
        def join(slot, first, last):
            for jc in range(NF):
                for ih in range(2):
                    ins = nc.tensor.matmul(banks[:, jc, ih, :], wx_s[:, slot, jc * P:(jc + 1) * P],
                                           conv_s[:, slot, 512 * ih:512 * ih + 512], start=first, stop=last)
            return ins

        pe.sem_inc(round_done, 2)
        pe.wait_ge(wload[0], 32)
        join(0, True, False).then_inc(w_used, 1)
        pe.wait_ge(wload[1], 32)
        join(1, False, False).then_inc(w_used, 1)
        with pe.Fori(0, NI // 2 - 2) as i:
            for slot in range(2):
                pe.wait_ge(wload[slot], 32 * i + 64)
                join(slot, False, False).then_inc(w_used, 1)
        pe.wait_ge(wload[0], 32 * (NI // 2))
        join(0, False, False).then_inc(w_used, 1)
        pe.wait_ge(wload[1], 32 * (NI // 2))
        join(1, False, True).then_inc(wc_done, 1)
        pe.wait_ge(wc_lo_ready, 2)
        pe.sem_inc(tok_ready, 2)
        with pe.Fori(0, ROUNDS // 2) as i:
            for b in range(2):
                n = 2 * i + b
                pe.wait_ge(tok_ready, n + 1)
                pe.wait_ge(u_ready, n + 3)
                pe.wait_ge(cp_ready, n + 3)
                for h in range(SUB):
                    ins = nc.tensor.matmul(banks[:, 0, b, 64 * h:64 * h + 64],
                                           t1[:, b, h, :, :].rearrange("p i j -> p (i j)"),
                                           cp[:, b, h, :, :].rearrange("p c a -> p (c a)"), start=True, stop=True)
                ins.then_inc(round_done, 1)


def mlp_stage(nc, t, tok, spare, wc_hi, wc_lo, w_z, w_out, skip_d, w_q, w_kvg, qkv_in, sem):
    def sb(name, shape, dt=F32):
        return t.enter_context(nc.sbuf_tensor(name, shape, dt))

    def ps(name, shape):
        return t.enter_context(nc.psum_tensor(name, shape, F32))

    PIECES, SLOTS = NF + NI // 2, (SPARE - NF * CT) // INTER
    wz_hi = sb("wz_hi", [P, NF, INTER], F32R)
    wz_lo = sb("wz_lo", [P, NF, INTER], F32R)
    wo_hi = sb("wo_hi", [P, NI, LEN], F32R)
    wo_lo = sb("wo_lo", [P, NI, LEN], F32R)
    skip = sb("skip", [P, NI])
    mean_w = sb("mean_w", [P, P])
    eps = sb("eps", [P, 1])
    hsum = sb("hsum", [P, CT])
    cen = sb("cen", [P, NF, CT])
    sq = spare[:, 0:NF * CT].rearrange("p (a t) -> p a t", a=NF)
    ssum = rstd = hsum
    xn_hi = sb("xn_hi", [P, NF, CT], F32R)
    xn_lo = sb("xn_lo", [P, NF, CT], F32R)
    gate = sb("silu", [P, 2, CT])
    g = gate
    g_hi = sb("g_hi", [P, 2, CT], F32R)
    g_lo = sb("g_lo", [P, 2, CT], F32R)

    y_ps = ps("y_ps", [P, NF, CT])
    z_ps = ps("z_ps", [P, CT])
    x_ps = ps("x_ps", [P, CT])
    mean_ps = ps("mean_ps", [P, CT])
    var_ps = ps("var_ps", [P, CT])

    w_in = [sem(f"mlp_w_in{q}") for q in range(PIECES)]
    skip_in = sem("skip_in")
    whi = sem("mlp_w_hi")
    wlo = sem("mlp_w_lo")
    ready = sem("mlp_consts")
    summed = sem("mlp_summed")
    mean_done = sem("mlp_mean")
    centred = sem("mlp_centred")
    squared = sem("mlp_squared")
    sq_summed = sem("mlp_sq_summed")
    var_done = sem("mlp_var")
    std_ready = sem("mlp_std")
    rstd_ready = sem("mlp_rstd")
    xn_ready = sem("mlp_xn")
    xhi_ready = sem("mlp_xhi")
    xlo_ready = sem("mlp_xlo")
    z_done = sem("z_done")
    x_done = sem("x_done")
    silu_ready = sem("silu_ready")
    g_ready = sem("g_ready")
    ghi_ready = sem("ghi_ready")
    glo_ready = sem("glo_ready")
    y_done = sem("y_done")
    res_ready = sem("mlp_res")

    def pieces():
        for a in range(NF):
            yield w_z[:, a, :], wz_hi[:, a, :], wz_lo[:, a, :]
        for i in range(0, NI, 2):
            yield w_out[:, i:i + 2, :].rearrange("p a b -> p (a b)"), flat(wo_hi[:, i:i + 2, :]), flat(wo_lo[:, i:i + 2, :])

    def landing(q):
        at = NF * CT + q % SLOTS * INTER
        return spare[:, at:at + INTER]

    def flat(ap):
        return ap.rearrange("p a b -> p (a b)")

    def chunk(n):
        return tok[:, :, :, bass.ds(n * CS, CS)]

    def rows(ap):
        return ap.rearrange("p (c s) -> p c s", c=ROWS) if len(ap.shape) == 2 else ap.rearrange("p a (c s) -> p a c s", c=ROWS)

    block = t.enter_context(nc.Block())

    @block.sync
    def _(sp):
        sp.dma_start(skip[:, :], skip_d).then_inc(skip_in, 16)
        for q, (src, hi, lo) in enumerate(pieces()):
            if q >= SLOTS:
                sp.wait_ge(wlo, q - SLOTS + 1)
            sp.dma_start(landing(q), src).then_inc(w_in[q], 16)
        sp.wait_ge(wlo, PIECES)
        for a in range(NF):
            sp.dma_start(spare[:, NF * LEN + a * KVG:NF * LEN + (a + 1) * KVG], w_kvg[:, a, :]).then_inc(qkv_in[a], 16)
        sp.wait_ge(sq_summed, CHUNKS)
        sp.dma_start(spare[:, 0:NF * LEN], w_q.rearrange("p a b -> p (a b)")).then_inc(qkv_in[NF], 16)

    @block.gpsimd
    def _(pool):
        for q, (src, hi, lo) in enumerate(pieces()):
            pool.wait_ge(whi, q + 1)
            nc.gpsimd.tensor_tensor(lo, landing(q), hi.bitcast(F32), ALU.subtract).then_inc(wlo, 1)

    @block.scalar
    def _(act):
        def whole(q0, q1):
            for q, (src, hi, lo) in list(enumerate(pieces()))[q0:q1]:
                act.wait_ge(w_in[q], 16)
                nc.scalar.activation(hi, landing(q), ACT.Copy).then_inc(whi, 1)

        def square(n):
            act.wait_ge(centred, n + 1)
            nc.scalar.activation(sq[:, :, :], cen[:, :, :], ACT.Square).then_inc(squared, 1)

        def std(n):
            act.wait_ge(var_done, n + 1)
            nc.scalar.activation(rstd[:, :], var_ps[:, :], ACT.Sqrt, bias=eps[:, :]).then_inc(std_ready, 1)

        def high(n):
            act.wait_ge(xn_ready, n + 1)
            for a in range(NF):
                nc.scalar.activation(xn_hi[:, a, :], cen[:, a, :], ACT.Copy).then_inc(xhi_ready, 1)

        def chunk_steps(n, more):
            def ghi(i):
                act.wait_ge(g_ready, NI * n + i + 1)
                nc.scalar.activation(g_hi[:, i % 2, :], g[:, i % 2, :], ACT.Copy).then_inc(ghi_ready, 1)

            for i in range(NI):
                act.wait_ge(z_done, NI * n + i + 1)
                if i:
                    act.wait_ge(glo_ready, NI * n + i - 1) if i > 1 else None
                nc.scalar.activation(gate[:, i % 2, :], z_ps[:, :], ACT.Silu).then_inc(silu_ready, 1)
                if i:
                    ghi(i - 1)
                if more and i == 1:
                    square(n + 1)
                if more and i == 4:
                    std(n + 1)
            ghi(NI - 1)
            if more:
                act.wait_ge(x_done, NI * n + NI)
                high(n + 1)

        act.wait_ge(ready, 2)
        square(0)
        whole(0, 3)
        std(0)
        whole(3, NF)
        high(0)
        whole(NF, PIECES)
        with act.Fori(0, CHUNKS - 1) as n:
            chunk_steps(n, True)
        chunk_steps(CHUNKS - 1, False)

    @block.vector
    def _(dve):
        nc.vector.memset(mean_w[:, :], 1.0 / LEN).then_inc(ready, 1)
        nc.vector.memset(eps[:, :], EPS).then_inc(ready, 1)
        def sum_chunk(n):
            if not (isinstance(n, int) and n == 0):
                dve.wait_ge(xn_ready, n)
            nc.vector.tensor_reduce(rows(hsum[:, :]), chunk(n).rearrange("p a c s -> p c s a"), AX, ALU.add).then_inc(summed, 1)

        def centre(n):
            dve.wait_ge(mean_done, n + 1)
            nc.vector.tensor_tensor(rows(cen[:, :, :]), chunk(n),
                                    rows(mean_ps[:, :]).unsqueeze(1).to_broadcast([P, NF, ROWS, CS]), ALU.subtract).then_inc(centred, 1)

        def sum_squares(n):
            dve.wait_ge(squared, n + 1)
            nc.vector.tensor_reduce(ssum[:, :], sq[:, :, :].rearrange("p a t -> p t a"), AX, ALU.add).then_inc(sq_summed, 1)

        def normalise(n):
            dve.wait_ge(std_ready, n + 1)
            nc.vector.reciprocal(rstd[:, :], rstd[:, :]).then_inc(rstd_ready, 1)
            dve.wait_ge(rstd_ready, n + 1)
            nc.vector.tensor_tensor(cen[:, :, :], cen[:, :, :], rstd[:, :].unsqueeze(1).to_broadcast([P, NF, CT]),
                                    ALU.mult).then_inc(xn_ready, 1)

        def low(n):
            for a in range(NF):
                dve.wait_ge(xhi_ready, NF * n + a + 1)
                nc.vector.tensor_tensor(xn_lo[:, a, :], cen[:, a, :], xn_hi[:, a, :].bitcast(F32), ALU.subtract).then_inc(xlo_ready, 1)

        def chunk_steps(n, more):
            for i in range(NI):
                if more and i == 0:
                    sum_chunk(n + 1)
                dve.wait_ge(silu_ready, NI * n + i + 1)
                dve.wait_ge(x_done, NI * n + i + 1)
                nc.vector.scalar_tensor_tensor(g[:, i % 2, :], x_ps[:, :], skip[:, i:i + 1], gate[:, i % 2, :],
                                               ALU.mult, ALU.mult).then_inc(g_ready, 1)
                dve.wait_ge(ghi_ready, NI * n + i + 1)
                nc.vector.tensor_tensor(g_lo[:, i % 2, :], g[:, i % 2, :], g_hi[:, i % 2, :].bitcast(F32), ALU.subtract).then_inc(glo_ready, 1)
                if more and i == 0:
                    centre(n + 1)
                if more and i == 2:
                    sum_squares(n + 1)
                if more and i == 5:
                    normalise(n + 1)
            if more:
                low(n + 1)
            dve.wait_ge(y_done, NI * n + NI)
            nc.vector.tensor_tensor(chunk(n), rows(y_ps[:, :, :]), chunk(n), ALU.add).then_inc(res_ready, 1)

        dve.wait_ge(skip_in, 16)
        sum_chunk(0)
        centre(0)
        sum_squares(0)
        normalise(0)
        low(0)
        with dve.Fori(0, CHUNKS - 1) as n:
            chunk_steps(n, True)
        chunk_steps(CHUNKS - 1, False)

    @block.tensor
    def _(pe):
        def mean(n):
            pe.wait_ge(summed, n + 1)
            nc.tensor.matmul(mean_ps[:, :], mean_w[:, :], hsum[:, :], start=True, stop=True).then_inc(mean_done, 1)

        def var(n):
            pe.wait_ge(sq_summed, n + 1)
            nc.tensor.matmul(var_ps[:, :], mean_w[:, :], ssum[:, :], start=True, stop=True).then_inc(var_done, 1)

        def project(n, acc, hi, lo, i, wait):
            for a in range(NF):
                if wait:
                    pe.wait_ge(xhi_ready, NF * n + a + 1)
                    pe.wait_ge(xlo_ready, NF * n + a + 1)
                cols = slice(i * P, (i + 1) * P)
                nc.tensor.matmul(acc, hi[:, a, cols], xn_hi[:, a, :], start=(a == 0), stop=False)
                nc.tensor.matmul(acc, hi[:, a, cols], xn_lo[:, a, :], start=False, stop=False)
                ins = nc.tensor.matmul(acc, lo[:, a, cols], xn_hi[:, a, :], start=False, stop=(a == NF - 1))
            return ins

        def put_out(n, i):
            if i % 2 == 0 and isinstance(n, int) and n == 0:
                pe.wait_ge(wlo, NF + i // 2 + 1)
            pe.wait_ge(ghi_ready, NI * n + i + 1)
            pe.wait_ge(glo_ready, NI * n + i + 1)
            for f in range(NF):
                cols = slice(f * P, (f + 1) * P)
                nc.tensor.matmul(y_ps[:, f, :], wo_hi[:, i, cols], g_hi[:, i % 2, :], start=(i == 0), stop=False)
                nc.tensor.matmul(y_ps[:, f, :], wo_hi[:, i, cols], g_lo[:, i % 2, :], start=False, stop=False)
                ins = nc.tensor.matmul(y_ps[:, f, :], wo_lo[:, i, cols], g_hi[:, i % 2, :], start=False, stop=(i == NI - 1))
            ins.then_inc(y_done, 1)

        def chunk_steps(n, more):
            for i in range(NI):
                if i:
                    pe.wait_ge(silu_ready, NI * n + i)
                project(n, z_ps[:, :], wz_hi, wz_lo, i, i == 0).then_inc(z_done, 1)
                if i:
                    pe.wait_ge(g_ready, NI * n + i)
                project(n, x_ps[:, :], wc_hi, wc_lo, i, False).then_inc(x_done, 1)
                if i:
                    put_out(n, i - 1)
                if more and i == 0:
                    mean(n + 1)
                if more and i == 3:
                    var(n + 1)
            put_out(n, NI - 1)

        pe.wait_ge(ready, 2)
        mean(0)
        var(0)
        pe.wait_ge(wlo, NF)
        chunk_steps(0, True)
        with pe.Fori(1, CHUNKS - 1) as n:
            chunk_steps(n, True)
        chunk_steps(CHUNKS - 1, False)


FILLS = (("k20", 0, 0), ("r0", 0, 1), ("k21", 2, 0), ("k22", 2, 0), ("r1", 3, 1), ("r2", 4, 1), ("t2", 5, 0),
         ("q0", 6, 1), ("q1", 6, 1), ("mean", 8, 2), ("k00", 9, 1), ("k01", 11, 1), ("k02", 12, 1),
         ("k10", 14, 1), ("k11", 15, 1), ("t0", 15, 1), ("var", 15, 2), ("k12", 18, 1), ("t1", 19, 1),
         ("q2", 21, 1), ("q3", 23, 1))
FILL_BANK = {name: k % 3 for k, (name, _, _) in enumerate(FILLS)}
PLACES = 24
OWN = [name for name, _, ahead in FILLS if ahead == 0]
AT_SUM, AT_CENTRE, AT_SQUARE, AT_SQ_SUM, AT_STD, AT_RSTD, AT_NORM = 3, 8, 10, 8, 17, 18, 20
AT_SPLIT = 4
AT_VALUES = {22: (0, 1), 6: (1, 0)}


def fills_at(m, p, some):
    return [(name, p + ahead) for name, place, ahead in FILLS if place == m and ahead in some]


TILES = 2 * 2 * NQ
SEGS = 16
TOK_TILES = PT // P


def segments(j):
    return {0: [(False, 0, QB, 0)], 1: [(True, 0, P, 1)], 2: [(True, 0, P, 2), (False, P, QB, 3)]}[j]


class Links:

    def __init__(self, eng, sem, per, n):
        self.eng, self.sem, self.per, self.n, self.k = eng, sem, per, n, 0

    def __call__(self, ins):
        self.k += 1
        ins.then_inc(self.sem, 1)
        self.eng.wait_ge(self.sem, self.n * self.per + self.k)


def attention_stage(nc, t, tok, spare, qkv_in, ident_d, mask_d, diag_d, rev_d, out, sem):
    def sb(name, shape, dt=F32):
        return t.enter_context(nc.sbuf_tensor(name, shape, dt))

    def ps(name, shape):
        return t.enter_context(nc.psum_tensor(name, shape, F32))

    def flat(ap):
        return ap.rearrange("p a b -> p (a b)")

    G = P // HD
    wq_hi = sb("wq_hi", [P, NF, LEN], F32R)
    wq_lo = sb("wq_lo", [P, NF, LEN], F32R)
    wkv_hi = sb("wkv_hi", [P, NF, KVG], F32R)
    wkv_lo = sb("wkv_lo", [P, NF, KVG], F32R)
    ident = sb("ident", [P, P])
    ident_b = sb("ident_b", [P, QB], BF16)
    mask = sb("mask", [P, 2, QB], BF16)
    diag = sb("diag", [P, G])
    rev = sb("rev", [P, HEADS])
    mean_w = sb("mean_w3", [P, P])
    eps = sb("eps3", [P, 1])
    NBLK = PT // QB
    res = spare[:, 0:2 * TILES * P].rearrange("p (b i f) -> p b i f", b=2, i=TILES)
    hpair = spare[:, 2 * TILES * P:2 * TILES * P + NF * PT].rearrange("p (x k g q) -> p x k g q", x=2, k=NBLK, g=2)
    sq_at = 2 * TILES * P + NF * PT
    sq = spare[:, sq_at:sq_at + NF * PT].rearrange("p (a s) -> p a s", a=NF)
    hsum = sb("hsum3", [P, PT])
    mask_f = hsum[:, 0:P]
    rstd = hsum
    xn_hi = sb("xn3_hi", [P, NF, PT], F32R)
    xn_lo = sb("xn3_lo", [P, NF, PT], F32R)
    q_hi = sb("q_hi", [P, 2, 2, NBLK, 2, QB], F32R)
    q_lo = sb("q_lo", [P, 2, 2, NBLK, 2, QB], F32R)
    kb_hi = sb("kb_hi", [P, 2, G, PT], F32R)
    kb_lo = sb("kb_lo", [P, 2, G, PT], F32R)
    vb = sb("vb", [P, 2, 4, VC], BF16)
    km = sb("km", [P, HEADS, HD])
    vm = sb("vm", [P, HEADS, HD])
    kex = flat(sq[:, :, :])[:, 0:G * P].rearrange("p (g k) -> p g k", k=P)
    krep = km[:, 4:4 + G, :]
    vsel = sb("vsel", [P, TOK_TILES, HD])
    one = sb("one", [P, 1])
    vblk = sb("vblk", [P, 4, HD])
    top = sb("top", [P, TOK_TILES])
    mx = sb("mx", [P, 1])
    below = sb("below", [P, HEADS])
    tie = sb("tie", [P, HEADS])
    tie_mx = sb("tie_mx", [P, 1])
    ind = sb("ind", [P, HEADS])
    gexp = sb("gexp", [P, HEADS])
    gsum = sb("gsum", [P, 1])
    prob = sb("prob", [P, 2, G, P + QB])
    smax = sb("smax", [P, 2, 2, G])
    pt_hi = sb("pt_hi", [P, 4, G * P], F16)
    pt_lo = sb("pt_lo", [P, 4, G * P], F16)
    rsum = sb("rsum", [P, 2, G])
    yparts = sb("yparts", [P, 2, G, VC])

    s_ps = ps("s_ps", [P, 2, 512])
    t_ps = ps("t_ps", [P, 2, 512])
    y_ps = ps("y_ps3", [P, 512])
    fill_banks = ps("fill_ps", [P, 3, 512])
    fill = {name: fill_banks[:, bank, :] for name, bank in FILL_BANK.items()}

    c_in = sem("att_consts_in")
    prob_set = sem("prob_set")
    settled_act = sem("settled_act")
    settled_pool = sem("settled_pool")
    whi = sem("qkv_hi")
    wlo = sem("qkv_lo")
    ready = sem("att_consts")
    hpair_in = sem("hpair_in")
    summed = sem("att_summed")
    mean_done = sem("att_mean")
    centred = sem("att_centred")
    squared = sem("att_squared")
    sq_summed = sem("att_sq_summed")
    var_done = sem("att_var")
    std_ready = sem("att_std")
    xn_ready = sem("att_xn")
    xhi_ready = sem("att_xhi")
    norm_step = sem("att_norm_step")
    rstd_ready = sem("att_rstd")
    top_ready = sem("gate_top")
    o_step = sem("o_step")
    xlo_ready = sem("att_xlo")
    q_done = sem("q_done")
    qhi_ready = sem("qhi_ready")
    qlo_ready = sem("qlo_ready")
    kv_done = sem("kv_done")
    shift_ready = sem("gate_shift")
    gexp_ready = sem("gate_exp")
    masked = sem("kv_masked")
    sum_step = sem("pool_sum_step")
    krep_ready = sem("krep_ready")
    kt_done = sem("kt_done")
    kex_ready = sem("kex_ready")
    kbhi_ready = sem("kbhi_ready")
    kblo_ready = sem("kblo_ready")
    vsel_ready = sem("vsel_ready")
    vblk_ready = sem("vblk_ready")
    vstep = sem("v_split_step")
    vb_ready = sem("vb_ready")
    res_done = sem("res_transposed")
    res_ready = sem("res_ready")
    link_proj = sem("proj_links")
    link_att = sem("att_links")
    s_done = sem("scores_done")
    less_ready = sem("less_ready")
    p_ready = sem("p_ready")
    t_done = sem("t_done")
    pthi_ready = sem("pthi_ready")
    ptlo_ready = sem("ptlo_ready")
    y_done = sem("y3_done")
    y_read = sem("y_read")
    rsum_ready = sem("rsum_ready")
    o_ready = sem("o_ready")
    out_done = [sem("out_done0"), sem("out_done1")]

    def pieces():
        for a in range(NF):
            at = NF * LEN + a * KVG
            yield qkv_in[a], spare[:, at:at + KVG], wkv_hi[:, a, :], wkv_lo[:, a, :]
        for a in range(0, NF, 2):
            yield qkv_in[NF], spare[:, a * LEN:(a + 2) * LEN], flat(wq_hi[:, a:a + 2, :]), flat(wq_lo[:, a:a + 2, :])

    def pair(n):
        return tok[:, :, bass.ds(2 * n, 2), :].rearrange("p a c s -> p a (c s)")

    def blocks(ap):
        return ap.rearrange("p (k q) -> p k q", q=QB)

    def tile(i):
        return i // (2 * NQ), i // NQ % 2, i % NQ

    def settle(eng):
        eng.sem_inc(settled_act if eng is nc.scalar else settled_pool, 1)

    SCALE = float(HD) ** -0.5
    OUT_CREDIT = 2 * TILES

    block = t.enter_context(nc.Block())

    @block.sync
    def _(sp):
        sp.dma_start(ident[:, :], ident_d).then_inc(c_in, 16)
        sp.dma_start(mask_f, mask_d).then_inc(c_in, 16)
        sp.dma_start(diag[:, :], diag_d).then_inc(c_in, 16)
        sp.dma_start(rev[:, :], rev_d.rearrange("(o h) -> o h", o=1).broadcast_to([P, HEADS])).then_inc(c_in, 16)
        def load_pair(n):
            for g in range(NF):
                sp.dma_start(hpair[:, g // 2, :, g % 2, :], blocks(pair(n)[:, g, :])).then_inc(hpair_in, 16)

        sp.wait_ge(wlo, NF)
        load_pair(0)
        sp.wait_ge(res_ready, 3)
        load_pair(1)

        def pair_steps(p, b, more):
            if more:
                sp.wait_ge(res_ready, 3 * p + 6)
                load_pair(p + 2)
            for r in range(2):
                sp.wait_ge(o_ready, TILES * p + 6 * (r + 1) + OUT_CREDIT)
                for x in range(2):
                    for gh in range(2):
                        g = 2 * x + gh
                        dst = out[bass.ds(2 * p + r, 1), :, P * g:P * (g + 1)].rearrange("r (j q) f -> q (r j) f", q=QB)
                        sp.dma_start(dst, res[gh * QB:(gh + 1) * QB, b, 6 * r + NQ * x:6 * r + NQ * (x + 1), :]).then_inc(out_done[r], 16)

        with sp.Fori(0, PAIRS // 2 - 1) as i:
            pair_steps(2 * i, 0, True)
            pair_steps(2 * i + 1, 1, True)
        pair_steps(PAIRS - 2, 0, False)
        pair_steps(PAIRS - 1, 1, False)
        for r in range(2):
            sp.wait_ge(out_done[r], 64 * (PAIRS + 2))

    @block.gpsimd
    def _(pool):
        pool.sem_inc(o_ready, OUT_CREDIT)
        pool.sem_inc(out_done[0], 128)
        pool.sem_inc(out_done[1], 128)
        nc.gpsimd.memset(vblk[:, :, :], 0.0).then_inc(ready, 1)
        nc.gpsimd.memset(one[:, :], 1.0).then_inc(ready, 1)
        nc.gpsimd.memset(prob[:, :, :, QB:P], 0.0).then_inc(prob_set, 1)
        for b in range(2):
            nc.gpsimd.memset(vb[:, b, :, VC - 1:VC], 1.0).then_inc(ready, 1)
        add = ALU.add
        SUM_STEPS = 2 * TOK_TILES * 3
        NORM_STEPS = 4
        norm_link = [None]

        def halve(x, step):
            for half in (8, 4, 2):
                step(nc.gpsimd.tensor_tensor(x[:, 0:half, :], x[:, 0:half, :], x[:, half:2 * half, :], add))

        def sum_chunks(x, step, done):
            step(nc.gpsimd.tensor_tensor(hsum[:, :], x[:, 0, :], x[:, 1, :], add))
            settle(nc.gpsimd)
            step(nc.gpsimd.tensor_tensor(hsum[:, :], hsum[:, :], x[:, 2, :], add))
            settle(nc.gpsimd)
            nc.gpsimd.tensor_tensor(hsum[:, :], hsum[:, :], x[:, 3, :], add).then_inc(done, 1)

        def norm(n, m):
            if m == AT_SUM:
                norm_link[0] = Links(pool, norm_step, NORM_STEPS, n)
                if not (isinstance(n, int) and n == 0):
                    pool.wait_ge(xn_ready, n)
                    settle(nc.gpsimd)
                sum_chunks(pair(n), norm_link[0], summed)
            if m == AT_SQ_SUM:
                pool.wait_ge(squared, n + 1)
                sum_chunks(sq, norm_link[0], sq_summed)
            if m == AT_NORM:
                pool.wait_ge(rstd_ready, n + 1)
                settle(nc.gpsimd)
                nc.gpsimd.tensor_tensor(pair(n), pair(n), rstd[:, :].unsqueeze(1).to_broadcast([P, NF, PT]), ALU.mult)\
                    .then_inc(xn_ready, 1)

        def values(n, b, r):
            pool.wait_ge(vblk_ready, 2 * n + r + 1)
            step = Links(pool, vstep, 8, n)
            step.k = 4 * r
            blks = slice(2 * r, 2 * r + 2)
            for part in range(3):
                piece = vb[:, b, blks, (2 - part) * HD:(3 - part) * HD]
                ins = nc.gpsimd.tensor_tensor(piece, vblk[:, blks, :], one[:, :].unsqueeze(2).to_broadcast([P, 2, HD]), ALU.mult)
                if part == 2:
                    ins.then_inc(vb_ready, 1)
                else:
                    step(ins)
                    step(nc.gpsimd.tensor_tensor(vblk[:, blks, :], vblk[:, blks, :], piece, ALU.subtract))

        def beside(p, b, m, some):
            for name, n in fills_at(m, p, some):
                nb = b if name in OWN else 1 - b
                tt = int(name[1]) if name[0] in "kt" else 0
                done = TOK_TILES * n + tt
                step = Links(pool, sum_step, SUM_STEPS, n)
                step.k = 6 * tt
                if name[0] == "k" and name[2] == "1":
                    pool.wait_ge(masked, 3 * done + 2)
                    halve(km, step)
                    pair_of = [km[:, h, :].unsqueeze(1).to_broadcast([P, G, HD]) for h in range(2)]
                    nc.gpsimd.tensor_tensor(krep, pair_of[0], pair_of[1], add).then_inc(krep_ready, 1)
                if name[0] == "k" and name[2] == "2":
                    step.k += 3
                    pool.wait_ge(masked, 3 * done + 3)
                    halve(vm, step)
                    nc.gpsimd.tensor_tensor(vsel[:, tt, :], vm[:, 0, :], vm[:, 1, :], add).then_inc(vsel_ready, 1)
                if name[0] == "t":
                    pool.wait_ge(kbhi_ready, done + 1)
                    nc.gpsimd.tensor_tensor(kb_lo[:, nb, :, tt * P:(tt + 1) * P], kex,
                                            kb_hi[:, nb, :, tt * P:(tt + 1) * P].bitcast(F32), ALU.subtract).then_inc(kblo_ready, 1)
            if m in AT_VALUES and AT_VALUES[m][1] in some:
                r, ahead = AT_VALUES[m]
                values(p + ahead, b if ahead == 0 else 1 - b, r)
            if 2 in some:
                norm(p + 2, m)

        def finish(p, b, i):
            e = i % 2
            step = Links(pool, o_step, 3 * TILES, p)
            step.k = 3 * i
            pool.wait_ge(rsum_ready, TILES * p + i + 1)
            if i % 4 == 0:
                pool.wait_ge(res_ready, 3 * p + i // 4 + 1)
            y = yparts[:, e, :, :]
            v1 = y[:, :, 2 * HD:3 * HD]
            step(nc.gpsimd.tensor_tensor(v1, v1, y[:, :, HD:2 * HD], add))
            step(nc.gpsimd.tensor_tensor(v1, v1, y[:, :, 0:HD], add))
            step(nc.gpsimd.tensor_tensor(v1, v1, rsum[:, e, :].unsqueeze(2).to_broadcast([P, G, HD]), ALU.mult))
            o = res[:, b, i, :].rearrange("p (g d) -> p g d", d=HD)
            nc.gpsimd.tensor_tensor(o, v1, o, add).then_inc(o_ready, 1)

        def pair_steps(p, b, some):
            for i in range(TILES):
                beside(p, b, 2 * i, some)
                beside(p, b, 2 * i + 1, some)
                if i > 0:
                    finish(p, b, i - 1)
            finish(p, b, TILES - 1)

        pool.wait_ge(ready, 8)
        for m in range(PLACES):
            norm(0, m)
        for m in range(PLACES):
            beside(-1, 1, m, (1, 2))
        with pool.Fori(0, PAIRS // 2 - 1) as i:
            pair_steps(2 * i, 0, (0, 1, 2))
            pair_steps(2 * i + 1, 1, (0, 1, 2))
        pair_steps(PAIRS - 2, 0, (0, 1))
        pair_steps(PAIRS - 1, 1, (0,))

    @block.scalar
    def _(act):
        act.wait_ge(c_in, 64)
        nc.scalar.activation(mask[:, :, :], mask_f.rearrange("p (g q) -> p g q", g=2), ACT.Copy).then_inc(ready, 1)
        nc.scalar.activation(ident_b[:, :], ident[:, 0:QB], ACT.Copy).then_inc(ready, 1)
        for w_in, raw, hi, lo in pieces():
            act.wait_ge(w_in, 16)
            nc.scalar.activation(hi, raw, ACT.Copy).then_inc(whi, 1)

        def norm(n, m):
            if m == AT_SQUARE:
                act.wait_ge(centred, n + 1)
                if not isinstance(n, int) or n > 1:
                    act.wait_ge(kblo_ready, TOK_TILES * (n - 1))
                settle(nc.scalar)
                nc.scalar.activation(sq[:, :, :], pair(n), ACT.Square).then_inc(squared, 1)
            if m == AT_STD:
                act.wait_ge(var_done, n + 1)
                nc.scalar.activation(rstd[:, :], fill["var"][:, 0:PT], ACT.Sqrt, bias=eps[:, :]).then_inc(std_ready, 1)

        def split(n):
            act.wait_ge(xn_ready, n + 1)
            if not (isinstance(n, int) and n == 0):
                act.wait_ge(kv_done, 3 * TOK_TILES * n)
            settle(nc.scalar)
            for a in range(NF):
                nc.scalar.activation(xn_hi[:, a, :], pair(n)[:, a, :], ACT.Copy).then_inc(xhi_ready, 1)

        def beside(p, b, m, some):
            for name, n in fills_at(m, p, some):
                nb = b if name in OWN else 1 - b
                src = fill[name]
                if name[0] == "r":
                    f = int(name[1])
                    act.wait_ge(res_done, 3 * n + f + 1)
                    for r in sorted({4 * f // 6, (4 * f + 3) // 6}):
                        act.wait_ge(out_done[r], 64 * (n + 1))
                    nc.scalar.activation(res[:, nb, 4 * f:4 * f + 4, :], src.rearrange("p (i f) -> p i f", i=4), ACT.Copy)\
                        .then_inc(res_ready, 1)
                if name[0] == "q":
                    g = int(name[1])
                    act.wait_ge(q_done, NF * n + g + 1)
                    nc.scalar.activation(q_hi[:, nb, g // 2, :, g % 2, :], blocks(src[:, 0:PT]), ACT.Copy).then_inc(qhi_ready, 1)
                if name[0] == "k" and name[2] == "0":
                    act.wait_ge(shift_ready, TOK_TILES * n + int(name[1]) + 1)
                    nc.scalar.activation(gexp[:, :], below[:, :], ACT.Exp, accum_out=gsum[:, :]).then_inc(gexp_ready, 1)
                if name[0] == "t":
                    tt = int(name[1])
                    act.wait_ge(kex_ready, TOK_TILES * n + tt + 1)
                    nc.scalar.activation(kb_hi[:, nb, :, tt * P:(tt + 1) * P], kex, ACT.Copy).then_inc(kbhi_ready, 1)
            if m == AT_SPLIT and 1 in some:
                split(p + 1)
            if 2 in some:
                norm(p + 2, m)

        def exps(p, i):
            segs = segments(i % NQ)
            act.wait_ge(less_ready, SEGS * p + 4 * (i // NQ) + segs[-1][3] + 3)
            keys = slice(0, segs[-1][1] + segs[-1][2])
            nc.scalar.activation(prob[:, i % 2, :, keys], prob[:, i % 2, :, keys], ACT.Exp, scale=SCALE).then_inc(p_ready, 1)

        def high(p, i):
            for wide, k0, keys, s in segments(i % NQ):
                s += 4 * (i // NQ)
                act.wait_ge(t_done, SEGS * p + s + 1)
                nc.scalar.activation(pt_hi[0:keys, s % 4, :], t_ps[0:keys, s % 2, :], ACT.Copy).then_inc(pthi_ready, 1)

        def keep_output(p, i):
            act.wait_ge(y_done, TILES * p + i + 1)
            act.wait_ge(o_ready, TILES * p + i - 1 + OUT_CREDIT)
            nc.scalar.activation(flat(yparts[:, i % 2, :, :]), y_ps[:, 0:G * VC], ACT.Copy).then_inc(y_read, 1)

        def pair_steps(p, b, some):
            for i in range(TILES):
                beside(p, b, 2 * i, some)
                if i + 1 < TILES:
                    exps(p, i + 1)
                elif 1 in some:
                    exps(p + 1, 0)
                high(p, i)
                if i:
                    keep_output(p, i - 1)
                beside(p, b, 2 * i + 1, some)
            keep_output(p, TILES - 1)

        act.sem_inc(y_read, 1)
        act.wait_ge(prob_set, 1)
        act.wait_ge(ready, 8)
        for m in range(PLACES):
            norm(0, m)
        for m in range(PLACES):
            beside(-1, 1, m, (1, 2))
        exps(0, 0)
        with act.Fori(0, PAIRS // 2 - 1) as i:
            pair_steps(2 * i, 0, (0, 1, 2))
            pair_steps(2 * i + 1, 1, (0, 1, 2))
        pair_steps(PAIRS - 2, 0, (0, 1))
        pair_steps(PAIRS - 1, 1, (0,))

    @block.vector
    def _(dve):
        nc.vector.memset(mean_w[:, :], 1.0 / LEN).then_inc(ready, 1)
        nc.vector.memset(eps[:, :], EPS).then_inc(ready, 1)
        dve.sem_inc(ptlo_ready, 2)
        for i, (w_in, raw, hi, lo) in enumerate(pieces()):
            dve.wait_ge(whi, i + 1)
            nc.vector.tensor_tensor(lo, raw, hi.bitcast(F32), ALU.subtract).then_inc(wlo, 1)
        dve.sem_inc(less_ready, 2)
        PROJ_LINKS = 4 * TOK_TILES + 2 * 2

        def over_heads(x, heads):
            return x[:, heads].unsqueeze(2).to_broadcast([P, heads.stop - heads.start, HD])

        def by_head(x):
            return x.rearrange("p (h d) -> p h d", d=HD)

        def norm(n, m):
            if m == AT_CENTRE:
                dve.wait_ge(mean_done, n + 1)
                dve.wait_ge(hpair_in, 64 * (n + 1))
                nc.vector.tensor_tensor(pair(n), pair(n), fill["mean"][:, 0:PT].unsqueeze(1).to_broadcast([P, NF, PT]),
                                        ALU.subtract).then_inc(centred, 1)
            if m == AT_RSTD:
                dve.wait_ge(std_ready, n + 1)
                nc.vector.reciprocal(rstd[:, :], rstd[:, :]).then_inc(rstd_ready, 1)

        def beside(p, b, m, some):
            for name, n in fills_at(m, p, some):
                nb = b if name in OWN else 1 - b
                if name[0] == "q":
                    g = int(name[1])
                    dve.wait_ge(qhi_ready, NF * n + g + 1)
                    nc.vector.tensor_tensor(q_lo[:, nb, g // 2, :, g % 2, :], blocks(fill[name][:, 0:PT]),
                                            q_hi[:, nb, g // 2, :, g % 2, :].bitcast(F32), ALU.subtract).then_inc(qlo_ready, 1)
                if name[0] == "k":
                    select(n, int(name[1]), int(name[2]), fill[name])
                if name[0] == "t":
                    tt = int(name[1])
                    dve.wait_ge(kt_done, TOK_TILES * n + tt + 1)
                    if tt:
                        dve.wait_ge(kblo_ready, TOK_TILES * n + tt)
                    squares = p + 2 if name in OWN or 2 not in some else p + 3
                    dve.wait_ge(sq_summed, min(squares, PAIRS) if isinstance(p, int) else squares)
                    nc.vector.tensor_tensor(kex, fill[name][:, 0:P].unsqueeze(1).to_broadcast([P, G, P]),
                                            diag[:, :].unsqueeze(2).to_broadcast([P, G, P]), ALU.mult).then_inc(kex_ready, 1)
            if m == AT_SPLIT and 1 in some:
                for a in range(NF):
                    dve.wait_ge(xhi_ready, NF * (p + 1) + a + 1)
                    nc.vector.tensor_tensor(xn_lo[:, a, :], pair(p + 1)[:, a, :], xn_hi[:, a, :].bitcast(F32), ALU.subtract)\
                        .then_inc(xlo_ready, 1)
            if m in AT_VALUES and AT_VALUES[m][1] in some:
                r, ahead = AT_VALUES[m]
                shift_values(p + ahead, r)
            if 2 in some:
                norm(p + 2, m)

        def select(n, tt, part, src):
            link = Links(dve, link_proj, PROJ_LINKS, n)
            link.k = 4 * tt + (2 if tt == TOK_TILES - 1 else 0)
            done = TOK_TILES * n + tt
            dve.wait_ge(kv_done, 3 * done + part + 1)
            if part == 0:
                logits = src[:, 0:HEADS]
                link(nc.vector.tensor_reduce(mx[:, :], logits, AX, ALU.max))
                nc.vector.tensor_scalar(below[:, :], logits, mx[:, :], None, ALU.subtract).then_inc(shift_ready, 1)
                dve.wait_ge(shift_ready, done + 1)
                link(nc.vector.scalar_tensor_tensor(tie[:, :], below[:, :], 0.0, rev[:, :], ALU.is_equal, ALU.mult))
                link(nc.vector.tensor_reduce(tie_mx[:, :], tie[:, :], AX, ALU.max))
                link(nc.vector.tensor_scalar(ind[:, :], tie[:, :], tie_mx[:, :], None, ALU.is_equal))
                if tt:
                    dve.wait_ge(kt_done, done)
                nc.vector.tensor_tensor(km[:, 0:10, :], by_head(src[:, 16:336]), over_heads(ind, slice(0, 10)), ALU.mult)\
                    .then_inc(masked, 1)
            if part == 1:
                nc.vector.tensor_tensor(km[:, 10:16, :], by_head(src[:, 0:192]), over_heads(ind, slice(10, 16)), ALU.mult)
                if tt:
                    dve.wait_ge(vsel_ready, done)
                nc.vector.tensor_tensor(vm[:, 0:5, :], by_head(src[:, 192:352]), over_heads(ind, slice(0, 5)), ALU.mult)\
                    .then_inc(masked, 1)
            if part == 2:
                nc.vector.tensor_tensor(vm[:, 5:16, :], by_head(src[:, 0:352]), over_heads(ind, slice(5, 16)), ALU.mult)\
                    .then_inc(masked, 1)
                dve.wait_ge(gexp_ready, done + 1)
                nc.vector.reciprocal(top[:, tt:tt + 1], gsum[:, :]).then_inc(top_ready, 1)

        def shift_values(n, r):
            link = Links(dve, link_proj, PROJ_LINKS, n)
            link.k = (4 * (TOK_TILES - 1), 4 * TOK_TILES + 2)[r]
            dve.wait_ge(vsel_ready, TOK_TILES * n + r + 2)
            dve.wait_ge(top_ready, TOK_TILES * n + r + 2)
            new = (slice(0, 2), slice(2, 3))[r]
            link(nc.vector.tensor_tensor(vsel[:, new, :], vsel[:, new, :],
                                         top[:, new].unsqueeze(2).to_broadcast([P, new.stop - new.start, HD]), ALU.mult))
            if r == 0:
                nc.vector.tensor_copy(vblk[:, 0, :], vsel[:, 0, :])
                link(nc.vector.tensor_copy(vblk[0:QB, 1, :], vsel[0:QB, 1, :]))
            else:
                nc.vector.tensor_copy(vblk[0:QB, 2, :], vsel[QB:P, 1, :])
                nc.vector.tensor_copy(vblk[QB:P, 2, :], vsel[0:QB, 2, :])
                link(nc.vector.tensor_copy(vblk[0:QB, 3, :], vsel[QB:P, 2, :]))
            dve.sem_inc(vblk_ready, 1)

        def softmax(p, i):
            e = i % 2
            segs = segments(i % NQ)
            dve.wait_ge(s_done, TILES * p + i + 1)
            for wide, k0, keys, s in segs:
                nc.vector.tensor_reduce(smax[:, e, int(k0 > 0), :], s_ps[:, s % 2, 0:G * keys].rearrange("p (g k) -> p g k", k=keys),
                                        AX, ALU.max).then_inc(link_att, 1)
            done = 5 * (i // NQ) + (1, 2, 4)[i % NQ]
            dve.wait_ge(link_att, 20 * p + done)
            if len(segs) == 2:
                nc.vector.tensor_tensor(smax[:, e, 0, :], smax[:, e, 0, :], smax[:, e, 1, :], ALU.max).then_inc(link_att, 1)
                dve.wait_ge(link_att, 20 * p + done + 1)
            for wide, k0, keys, s in segs:
                cols = slice(k0, k0 + keys)
                nc.vector.tensor_tensor(prob[:, e, :, cols], s_ps[:, s % 2, 0:G * keys].rearrange("p (g k) -> p g k", k=keys),
                                        smax[:, e, 0, :].unsqueeze(2).to_broadcast([P, G, keys]), ALU.subtract)\
                    .then_inc(less_ready, 1)

        def low(p, i):
            for wide, k0, keys, s in segments(i % NQ):
                s += 4 * (i // NQ)
                dve.wait_ge(pthi_ready, SEGS * p + s + 1)
                nc.vector.tensor_tensor(pt_lo[0:keys, s % 4, :], t_ps[0:keys, s % 2, :], pt_hi[0:keys, s % 4, :], ALU.subtract)\
                    .then_inc(ptlo_ready, 1)

        def invert_sum(p, i):
            dve.wait_ge(y_read, TILES * p + i + 2)
            nc.vector.reciprocal(rsum[:, i % 2, :], yparts[:, i % 2, :, VC - 1]).then_inc(rsum_ready, 1)

        def pair_steps(p, b, some):
            for i in range(TILES):
                if i + 1 < TILES:
                    softmax(p, i + 1)
                elif 1 in some:
                    softmax(p + 1, 0)
                beside(p, b, 2 * i, some)
                low(p, i)
                beside(p, b, 2 * i + 1, some)
                if i:
                    invert_sum(p, i - 1)
            invert_sum(p, TILES - 1)

        dve.wait_ge(ready, 8)
        for m in range(PLACES):
            norm(0, m)
        for m in range(PLACES):
            beside(-1, 1, m, (1, 2))
        softmax(0, 0)
        with dve.Fori(0, PAIRS // 2 - 1) as i:
            pair_steps(2 * i, 0, (0, 1, 2))
            pair_steps(2 * i + 1, 1, (0, 1, 2))
        pair_steps(PAIRS - 2, 0, (0, 1))
        pair_steps(PAIRS - 1, 1, (0,))

    @block.tensor
    def _(pe):
        def three(acc, lh, ll, rh, rl, first, last):
            nc.tensor.matmul(acc, lh, rh, start=first, stop=False)
            nc.tensor.matmul(acc, lh, rl, start=False, stop=False)
            return nc.tensor.matmul(acc, ll, rh, start=False, stop=last)

        def norm_fill(n, name):
            acc = fill[name][:, 0:PT]
            if name == "mean":
                pe.wait_ge(summed, n + 1)
                nc.tensor.matmul(acc, mean_w[:, :], hsum[:, :], start=True, stop=True).then_inc(mean_done, 1)
            else:
                pe.wait_ge(sq_summed, n + 1)
                nc.tensor.matmul(acc, mean_w[:, :], hsum[:, :], start=True, stop=True).then_inc(var_done, 1)

        def bank_free(p, k, some):
            while True:
                k -= 3
                name, _, ahead = FILLS[k]
                if k < 0:
                    if isinstance(p, int) and p < 0:
                        return
                    ahead -= 1
                elif ahead not in some:
                    continue
                break
            kind, n = name[0], p + ahead
            if kind == "r":
                pe.wait_ge(res_ready, 3 * n + int(name[1]) + 1)
            elif kind == "q":
                pe.wait_ge(qlo_ready, NF * n + int(name[1]) + 1)
            elif kind == "k":
                pe.wait_ge(masked, 3 * (TOK_TILES * n + int(name[1])) + int(name[2]) + 1)
            elif kind == "t":
                pe.wait_ge(kex_ready, TOK_TILES * n + int(name[1]) + 1)
            elif name == "mean":
                pe.wait_ge(centred, n + 1)
            elif name == "var":
                pe.wait_ge(std_ready, n + 1)

        def beside(p, b, m, some):
            for k, (name, place, ahead) in enumerate(FILLS):
                if place != m or ahead not in some:
                    continue
                bank_free(p, k, some)
                n = p + ahead
                src = fill[name]
                if name in ("mean", "var"):
                    norm_fill(n, name)
                if name[0] == "r":
                    f = int(name[1])
                    pe.wait_ge(hpair_in, 64 * n + 64)
                    for x in range(4):
                        r, gp, j = tile(4 * f + x)
                        ins = nc.tensor.transpose(src[:, x * P:(x + 1) * P], hpair[:, gp, NQ * r + j, :, :].rearrange("p g q -> p (g q)"),
                                                  ident[:, :])
                    ins.then_inc(res_done, 1)
                if name[0] == "q":
                    g = int(name[1])
                    cols = slice(g * P, (g + 1) * P)
                    for a in range(NF):
                        if g == 0:
                            pe.wait_ge(xlo_ready, NF * n + a + 1)
                        ins = three(src[:, 0:PT], wq_hi[:, a, cols], wq_lo[:, a, cols], xn_hi[:, a, :], xn_lo[:, a, :], a == 0, a == NF - 1)
                    ins.then_inc(q_done, 1)
                if name[0] == "k":
                    tt, part = int(name[1]), int(name[2])
                    c0 = sum(KV_BANK[:part])
                    cols = slice(c0, c0 + KV_BANK[part])
                    toks = slice(tt * P, (tt + 1) * P)
                    for a in range(NF):
                        ins = three(src[:, 0:KV_BANK[part]], xn_hi[:, a, toks], xn_lo[:, a, toks],
                                    wkv_hi[:, a, cols], wkv_lo[:, a, cols], a == 0, a == NF - 1)
                    ins.then_inc(kv_done, 1)
                if name[0] == "t":
                    pe.wait_ge(krep_ready, TOK_TILES * n + int(name[1]) + 1)
                    nc.tensor.transpose(src[:, 0:P], flat(krep), ident[:, :]).then_inc(kt_done, 1)

        def scores(p, b, i):
            r, gp, j = tile(i)
            if i in (0, TILES // 2):
                pe.wait_ge(kblo_ready, TOK_TILES * p + r + 2)
            if i in (0, NQ):
                pe.wait_ge(qlo_ready, NF * p + 2 * gp + 2)
            qh, ql = (q[:, b, gp, NQ * r + j, :, :].rearrange("p g q -> p (g q)") for q in (q_hi, q_lo))
            for wide, k0, keys, s in segments(j):
                ks = slice(STEPS * r + k0, STEPS * r + k0 + keys)
                acc = s_ps[:, s % 2, 0:G * keys].rearrange("p (g k) -> p g k", k=keys)
                pe.wait_ge(less_ready, SEGS * p + 4 * (i // NQ) + s + 1)
                masked_here = (keys + k0) == QB * (j + 1)
                ins = three(acc, qh, ql, kb_hi[:, b, :, ks], kb_lo[:, b, :, ks], True, not masked_here)
                if masked_here:
                    ins = nc.tensor.matmul(acc[:, :, keys - QB:keys], flat(mask[:, :, :]), ident_b[:, :].unsqueeze(1).to_broadcast([P, G, QB]),
                                           start=False, stop=True)
            ins.then_inc(s_done, 1)

        def transposes_free(p, i):
            pe.wait_ge(p_ready, TILES * p + i + 1)
            pe.wait_ge(ptlo_ready, SEGS * p + 4 * (i // NQ) + segments(i % NQ)[-1][3] + 1)

        def transposes(p, i):
            for wide, k0, keys, s in segments(i % NQ):
                s += 4 * (i // NQ)
                cols = slice(0, P) if k0 == 0 else slice(k0, k0 + keys)
                for g in range(G):
                    ins = nc.tensor.transpose(t_ps[0:cols.stop - cols.start, s % 2, g * P:(g + 1) * P], prob[:, i % 2, g, cols], ident[:, :])
                ins.then_inc(t_done, 1)

        def values(p, b, i):
            r, gp, j = tile(i)
            segs = segments(j)
            if i in (0, TILES // 2):
                pe.wait_ge(vb_ready, 2 * p + r + 1)
            pe.wait_ge(y_read, TILES * p + i + 1)
            last_seg = SEGS * p + 4 * (i // NQ) + segs[-1][3] + 1
            pe.wait_ge(ptlo_ready, last_seg + 2)
            for g in range(G):
                acc = y_ps[:, g * VC:(g + 1) * VC]
                for x, (wide, k0, keys, s) in enumerate(segs):
                    rows = slice(0, keys)
                    v = vb[rows, b, 2 * r + (k0 > 0), :]
                    nc.tensor.matmul(acc, pt_hi[rows, s, g * P:(g + 1) * P], v, start=(x == 0), stop=False)
                    ins = nc.tensor.matmul(acc[:, HD:VC], pt_lo[rows, s, g * P:(g + 1) * P], v[:, HD:VC], start=False,
                                           stop=(x == len(segs) - 1))
            ins.then_inc(y_done, 1)

        def pair_steps(p, b, some):
            for i in range(TILES):
                if i + 1 < TILES:
                    scores(p, b, i + 1)
                elif 1 in some:
                    scores(p + 1, 1 - b, 0)
                beside(p, b, 2 * i, some)
                transposes_free(p, i)
                transposes(p, i)
                if i:
                    values(p, b, i - 1)
                beside(p, b, 2 * i + 1, some)
            values(p, b, TILES - 1)

        pe.wait_ge(ready, 8)
        pe.wait_ge(wlo, 6)
        norm_fill(0, "mean")
        norm_fill(0, "var")
        pe.wait_ge(std_ready, 1)
        for m in range(PLACES):
            beside(-1, 1, m, (1, 2))
        scores(0, 0, 0)
        with pe.Fori(0, PAIRS // 2 - 1) as i:
            pair_steps(2 * i, 0, (0, 1, 2))
            pair_steps(2 * i + 1, 1, (0, 1, 2))
        pair_steps(PAIRS - 2, 0, (0, 1))
        pair_steps(PAIRS - 1, 1, (0,))


def layout(inputs):
    import numpy as _np
    c = _np.ascontiguousarray
    w_in = _np.asarray(inputs["L0_attn_W_in"])
    qkv = _np.asarray(inputs["L0_ffn_W_qkv"])
    width = LEN

    def chunks(w):
        return c(w.reshape(-1, P, w.shape[1]).transpose(1, 0, 2))

    wq, wk, wv = qkv[:width].T, qkv[width:2 * width].T, qkv[2 * width:].T
    kvg = _np.concatenate([_np.asarray(inputs["L0_ffn_W_gate"]).T, wk, wv], axis=1)
    q, k = _np.arange(QB), _np.arange(QB)
    mask_t = _np.zeros((P, 2, QB), _np.float32)
    mask_t[:QB] = _np.where(k[:, None, None] > q[None, None, :], _np.float32(-1e30), _np.float32(0))
    diag = (_np.arange(P)[:, None] // HD == _np.arange(P // HD)[None, :]).astype(_np.float32)
    return {
        "log_dt": c(inputs["L0_tok_log_dt"]),
        "a_imag": c(_np.asarray(inputs["L0_tok_A_imag"]).T),
        "inv_a_real": c(_np.asarray(inputs["L0_tok_inv_A_real"]).T),
        "b_ri": c(_np.asarray(inputs["L0_tok_B_ri"]).transpose(2, 1, 0)),
        "x_ri": c(_np.asarray(inputs["x"]).transpose(3, 2, 1, 0)),
        "w_x": c(w_in[:INTER]),
        "conv_t": c(_np.asarray(inputs["L0_attn_conv_w"]).T),
        "w_z": chunks(w_in[INTER:].T),
        "w_out": chunks(_np.asarray(inputs["L0_attn_W_out"]).T),
        "skip_d": c(_np.asarray(inputs["L0_attn_D"]).reshape(NI, P).T),
        "w_q": chunks(wq),
        "w_kvg": chunks(kvg),
        "mults": steps_tables(),
        "ident": _np.eye(P, dtype=_np.float32),
        "mask_t": c(mask_t.reshape(P, P)),
        "diag": diag,
        "rev": _np.arange(HEADS, 0, -1).astype(_np.float32),
    }


def kernel(**inputs):
    import concourse.bacc as _bacc
    from concourse import mybir as _mybir
    from concourse.bass_utils import run_bass_kernel_spmd as _run

    nc = _bacc.Bacc("TRN2", target_bir_lowering=False, num_devices=1)
    arrays = {f"in_{k}": a for k, a in layout(inputs).items()}
    args = [nc.dram_tensor(k, a.shape, _mybir.dt.from_np(a.dtype), kind="ExternalInput").ap() for k, a in arrays.items()]
    out = nc.dram_tensor("out_0", (ROWS, STEPS, LEN), F32, kind="ExternalOutput").ap()
    build(nc, *args, out)
    r = _run(nc, [arrays], core_ids=[0])
    return r.results[0]["out_0"]
```

```python
import numpy as np
from contextlib import ExitStack
import concourse.bass as bass
from concourse import mybir
from concourse.alu_op_type import AluOpType as ALU

F32 = mybir.dt.float32
F32R = mybir.dt.float32r
BF16 = mybir.dt.bfloat16
F16 = mybir.dt.float16
ACT = mybir.ActivationFunctionType
AX = mybir.AxisListType.X

P = 128
ROWS, STEPS, MODES, LEN = 16, 192, 64, 512
NF = LEN // P
INTER = 1024
NI = INTER // P
HEADS, HD = 16, 32
EPS = 1e-5

NK, NA, NB = NF, 16, 8
NT = NA + NB + NK
SUB = 8
ROUNDS = STEPS // SUB
UNROLL = 6
BUFS = 3
TWO_PI = 6.283185
ROUND = 12582912.0
LOG2_E = 1.4426950408889634
LN2_HI, LN2_LO = 0.693359375, -2.12194440e-4
EXP_POLY = [1 / 5040, 1 / 720, 1 / 120, 1 / 24, 1 / 6, 1 / 2, 1.0]

CS = 32
CHUNKS = STEPS // CS
CT = ROWS * CS

PAIRS = ROWS // 2
PT = 2 * STEPS
QB = 64
NQ = STEPS // QB
GATE_COLS, KV_BANK = HEADS, (336, 352, 352)
VC = 3 * HD + 1
KVG = HEADS + 2 * LEN

SPARE = NF * LEN + NF * KVG


def steps_tables():
    return np.array([8 * i for i in range(NA)] + list(range(NB)) + [P * k for k in range(NK)], np.float32)


def build(nc, log_dt, a_imag, inv_a_real, b_ri, x_ri, w_x, conv_t, w_z, w_out, skip_d,
          w_q, w_kvg, mults, ident, mask_t, diag, rev, out):
    ctx = ExitStack()
    with ctx:
        def sem(name):
            return ctx.enter_context(nc.semaphore(name))

        tok = ctx.enter_context(nc.sbuf_tensor("tok", [P, NF, ROWS, STEPS], F32))
        spare = ctx.enter_context(nc.sbuf_tensor("spare", [P, SPARE], F32))
        qkv_in = [sem(f"qkv_in{i}") for i in range(NF + 1)]
        hsum = ctx.enter_context(nc.sbuf_tensor("hsum", [P, CT], F32))
        summed = sem("mlp_summed")
        with ExitStack() as two:
            wc_hi = two.enter_context(nc.sbuf_tensor("wc_hi", [P, NF, INTER], F32R))
            wc_lo = two.enter_context(nc.sbuf_tensor("wc_lo", [P, NF, INTER], F32R))
            with ExitStack() as t:
                tokens_stage(nc, t, tok, spare, hsum, summed, wc_hi, wc_lo, log_dt, a_imag, inv_a_real, b_ri, x_ri, w_x, conv_t, mults, sem)
            with ExitStack() as t:
                mlp_stage(nc, t, tok, spare, hsum, summed, wc_hi, wc_lo, w_z, w_out, skip_d, w_q, w_kvg, qkv_in, sem)
        with ExitStack() as t:
            attention_stage(nc, t, tok, spare, hsum, qkv_in, ident, mask_t, diag, rev, out, sem)


def sum_chunk_of(nc, tok, hsum, n):
    return nc.vector.tensor_reduce(hsum[:, :].rearrange("p (c s) -> p c s", c=ROWS),
                                   tok[:, :, :, bass.ds(n * CS, CS)].rearrange("p a c s -> p c s a"), AX, ALU.add)


def tokens_stage(nc, t, tok, spare, hsum, summed, wc_hi, wc_lo, log_dt, a_imag, inv_a_real, b_ri, x_ri, w_x, conv_t, mults, sem):
    def sb(name, shape, dt=F32):
        return t.enter_context(nc.sbuf_tensor(name, shape, dt))

    H = STEPS
    dar = sb("dt_and_a_real", [P, 2, H])
    ld, ar = dar[:, 0, :], dar[:, 1, :]
    ai = sb("a_imag_b", [P, H])
    br = sb("b_re", [P, H])
    bi = sb("b_im", [P, H])
    mul = sb("mults_b", [P, NT])
    xre, xim = (spare[:, part * H * ROWS:(part + 1) * H * ROWS].rearrange("p (h c) -> p h c", c=ROWS) for part in range(2))
    conv_s = sb("conv_s", [P, 2, INTER])
    wx_s = sb("wx_s", [P, 2, LEN])
    pw = sb("powers", [P, H, 2, NT])
    flat = tok[:, :, :, :].rearrange("p a c s -> p (a c s)")
    phase = flat[:, 0:H * NT].rearrange("p (h n) -> p h n", n=NT)
    decay = flat[:, H * NT:2 * H * NT].rearrange("p (h n) -> p h n", n=NT)
    na, nb, nk = slice(0, NA), slice(NA, NA + NB), slice(NA + NB, NT)
    DVE_STEPS = 2 * H // 3
    small = [sb(f"small{i}", [P, H]) for i in range(7)]
    q1 = sb("q1", [P, H, NK])
    q2 = sb("q2", [P, H, NK])
    t_size, z_size = SUB * NA * NB, SUB * ROWS * NK
    ring = sb("ring", [P, (BUFS + 2) * (t_size + z_size)])
    absolute = ring[:, 0:H * NT].rearrange("p (h n) -> p h n", n=NT)
    parts, at = [], 0
    for size, bufs in ((t_size, BUFS), (t_size, 2), (z_size, 2), (z_size, BUFS)):
        parts.append(ring[:, at:at + bufs * size])
        at += bufs * size
    t1, t2 = (parts[k].rearrange("p (b h i j) -> p b h i j", h=SUB, i=NA, j=NB) for k in (0, 1))
    z2, cp = (parts[k].rearrange("p (b h c a) -> p b h c a", h=SUB, c=ROWS, a=NK) for k in (2, 3))
    exp_at = H * NT
    ek, er, ep = (ring[:, exp_at + 2 * H * k:exp_at + 2 * H * (k + 1)].rearrange("p (a h) -> p a h", a=2) for k in range(3))
    e2 = sb("exp_bits", [P, 2, H], mybir.dt.int32)
    halfpi = sb("halfpi", [P, 1])
    minus_halfpi = sb("minus_halfpi", [P, 1])

    banks = t.enter_context(nc.psum_tensor("wc_ps", [P, NF, 2, 512], F32))

    dar_in = sem("dt_and_a_real_in")
    consts_in = sem("consts_in")
    b_in = sem("b_in")
    x_in = sem("x_in")
    wload = [sem("wload0"), sem("wload1")]
    w_used = sem("w_used")
    dt_ready = sem("dt_ready")
    adt_ready = sem("adt_ready")
    angle_ready = sem("angle_ready")
    rest_turns = sem("rest_turns")
    rest_whole = sem("rest_whole")
    abs_ready = sem("abs_ready")
    e_read = sem("e_read")
    decayed = sem("decayed")
    decay_ready = sem("decay_ready")
    sines = sem("sines")
    g_exp = sem("g_exp")
    tables = sem("tables")
    chain = sem("dve_chain")
    t2_ready = sem("t2_ready")
    z2_ready = sem("z2_ready")
    t1_ready = sem("t1_ready")
    z1_ready = sem("z1_ready")
    u_ready = sem("u_ready")
    cp_ready = sem("cp_ready")
    round_done = sem("round_done")
    tok_ready = sem("tok_ready")
    wc_done = sem("wc_done")
    wc_hi_ready = sem("wc_hi_ready")
    wc_lo_ready = sem("wc_lo_ready")

    block = t.enter_context(nc.Block())

    @block.sync
    def _(sp):
        sp.dma_start(ld, log_dt.rearrange("(o h) -> o h", o=1).broadcast_to([P, H])).then_inc(dar_in, 16)
        for half in (slice(0, MODES), slice(MODES, P)):
            sp.dma_start(dar[half, 1, :], inv_a_real).then_inc(dar_in, 16)
        for half in (slice(0, MODES), slice(MODES, P)):
            sp.dma_start(ai[half, :], a_imag).then_inc(consts_in, 16)
        sp.dma_start(mul[:, :], mults.rearrange("(o h) -> o h", o=1).broadcast_to([P, NT])).then_inc(consts_in, 16)

        def load_w(k, slot):
            sp.dma_start(conv_s[:, slot, :], conv_t[k * P:(k + 1) * P, :]).then_inc(wload[slot], 16)
            sp.dma_start(wx_s[:, slot, :], w_x[k * P:(k + 1) * P, :]).then_inc(wload[slot], 16)

        x_parts = [(xre[:MODES], x_ri[0]), (xim[:MODES], x_ri[1]), (xre[MODES:], x_ri[0]), (xim[MODES:], x_ri[1])]
        for k in range(2, NI):
            sp.wait_ge(w_used, k - 1)
            load_w(k, k % 2)
            if k < 2 + len(x_parts):
                dst, src = x_parts[k - 2]
                sp.dma_start(dst, src).then_inc(x_in, 16)

    @block.gpsimd
    def _(pool):
        pool.wait_ge(angle_ready, 1)
        phase_p, whole_p = phase[:, DVE_STEPS:, :], pw[:, DVE_STEPS:, 0, :]
        rest_of_steps = [P, H - DVE_STEPS, NT]
        nc.gpsimd.tensor_tensor(phase_p, small[0][:, DVE_STEPS:].unsqueeze(2).to_broadcast(rest_of_steps),
                                mul[:, :].unsqueeze(1).to_broadcast(rest_of_steps), ALU.mult).then_inc(rest_turns, 1)
        pool.wait_ge(rest_whole, 1)
        nc.gpsimd.tensor_tensor(phase_p, phase_p, whole_p, ALU.subtract).then_inc(rest_turns, 1)
        pool.wait_ge(sines, 2)
        pool.wait_ge(decay_ready, 1)
        pool.wait_ge(e_read, 1)
        nc.gpsimd.tensor_tensor(pw[:, :, 1, 0:NA + NB], pw[:, :, 1, 0:NA + NB], decay[:, :, 0:NA + NB], ALU.mult).then_inc(decayed, 1)
        pool.wait_ge(decayed, 1)
        pool.wait_ge(x_in, 64)
        with pool.Fori(0, ROUNDS // UNROLL) as i:
            for u in range(UNROLL):
                n, b = UNROLL * i + u, u % 2
                hs = bass.ds(n * SUB, SUB)
                pool.wait_ge(u_ready, n + 1)
                nc.gpsimd.tensor_tensor(
                    t2[:, b, :, :, :], pw[:, hs, 1, 0:NA].unsqueeze(3).to_broadcast([P, SUB, NA, NB]),
                    pw[:, hs, 1, NA:NA + NB].unsqueeze(2).to_broadcast([P, SUB, NA, NB]), ALU.mult).then_inc(t2_ready, 1)
                pool.wait_ge(cp_ready, n + 1)
                pool.wait_ge(tables, 1)
                nc.gpsimd.tensor_tensor(
                    z2[:, b, :, :, :], xim[:, hs, :].unsqueeze(3).to_broadcast([P, SUB, ROWS, NK]),
                    q2[:, hs, :].unsqueeze(2).to_broadcast([P, SUB, ROWS, NK]), ALU.mult).then_inc(z2_ready, 1)

    @block.vector
    def _(dve):
        links = [0]

        def link(ins):
            links[0] += 1
            ins.then_inc(chain, 1)
            dve.wait_ge(chain, links[0])

        def tt(o, a, b, op):
            link(nc.vector.tensor_tensor(o, a, b, op))

        th, adt = small[0][:, :], small[1][:, :]
        dve.sem_inc(u_ready, 2)
        dve.sem_inc(cp_ready, 2)
        nc.vector.memset(halfpi[:, :], TWO_PI / 4).then_inc(dt_ready, 1)
        nc.vector.memset(minus_halfpi[:, :], -TWO_PI / 4).then_inc(dt_ready, 1)
        dve.wait_ge(dt_ready, 2)
        dve.wait_ge(dar_in, 16 * 3)
        whole_k, rest, poly = ek[:, :, :], er[:, :, :], ep[:, :, :]
        x = dar[:, :, :]
        link(nc.vector.tensor_scalar(x, x, -87.0, 88.0, ALU.max, ALU.min))
        link(nc.vector.tensor_scalar(whole_k, x, LOG2_E, ROUND, ALU.mult, ALU.add))
        link(nc.vector.tensor_scalar(whole_k, whole_k, ROUND, None, ALU.subtract))
        link(nc.vector.scalar_tensor_tensor(rest, whole_k, -LN2_HI, x, ALU.mult, ALU.add))
        link(nc.vector.scalar_tensor_tensor(rest, whole_k, -LN2_LO, rest, ALU.mult, ALU.add))
        link(nc.vector.tensor_scalar(poly, rest, EXP_POLY[0], None, ALU.mult))
        for coefficient in EXP_POLY[1:]:
            link(nc.vector.scalar_tensor_tensor(poly, poly, coefficient, rest, ALU.add, ALU.mult))
        link(nc.vector.tensor_scalar(e2[:, :, :], whole_k, 127.0, float(2 ** 23), ALU.add, ALU.mult))
        link(nc.vector.scalar_tensor_tensor(x, poly, 1.0, e2[:, :, :].bitcast(F32), ALU.add, ALU.mult))
        nc.vector.scalar_tensor_tensor(adt, ar, -1.0, ld, ALU.mult, ALU.mult).then_inc(adt_ready, 1)
        dve.wait_ge(consts_in, 16 * 3)
        tt(th, ai[:, :], ld, ALU.mult)
        nc.vector.tensor_scalar(th, th, float(1 / (2 * np.pi)), None, ALU.mult).then_inc(angle_ready, 1)
        dve.wait_ge(angle_ready, 1)
        phase_v, whole_v = phase[:, 0:DVE_STEPS, :], pw[:, 0:DVE_STEPS, 0, :]
        phase_p, whole_p = phase[:, DVE_STEPS:, :], pw[:, DVE_STEPS:, 0, :]
        tt(phase_v, small[0][:, 0:DVE_STEPS].unsqueeze(2).to_broadcast([P, DVE_STEPS, NT]),
           mul[:, :].unsqueeze(1).to_broadcast([P, DVE_STEPS, NT]), ALU.mult)
        dve.wait_ge(rest_turns, 1)
        nc.vector.tensor_scalar(whole_p, phase_p, ROUND, ROUND, ALU.add, ALU.subtract).then_inc(rest_whole, 1)
        link(nc.vector.tensor_scalar(whole_v, phase_v, ROUND, ROUND, ALU.add, ALU.subtract))
        nc.vector.tensor_tensor(phase_v, phase_v, whole_v, ALU.subtract).then_inc(angle_ready, 1)
        dve.wait_ge(angle_ready, 2)
        dve.wait_ge(rest_turns, 2)
        for cols in (nb, na, nk):
            nc.vector.scalar_tensor_tensor(absolute[:, :, cols], phase[:, :, cols], -1.0, phase[:, :, cols], ALU.mult, ALU.max)\
                .then_inc(abs_ready, 1)
        s2, s3, s4, s5, s6 = (s[:, :] for s in small[2:7])
        tt(s2, ar, ar, ALU.mult)
        tt(s3, ai[:, :], ai[:, :], ALU.mult)
        tt(s2, s2, s3, ALU.add)
        link(nc.vector.reciprocal(s2, s2))
        dve.wait_ge(sines, 1)
        dve.wait_ge(g_exp, 2)
        cosv, sinv = pw[:, :, 0, NA + 1], pw[:, :, 1, NA + 1]
        link(nc.vector.scalar_tensor_tensor(s3, s6, 1.0, s5, ALU.add, ALU.mult))
        tt(s3, s3, cosv, ALU.mult)
        link(nc.vector.scalar_tensor_tensor(s3, cosv, -1.0, s3, ALU.add, ALU.add))
        tt(s4, s6, sinv, ALU.mult)
        dve.sem_inc(e_read, 1)
        tt(s5, s3, ar, ALU.mult)
        tt(s6, s4, ai[:, :], ALU.mult)
        tt(s6, s6, s5, ALU.subtract)
        tt(s6, s6, s2, ALU.mult)
        tt(s4, s4, ar, ALU.mult)
        tt(s3, s3, ai[:, :], ALU.mult)
        link(nc.vector.scalar_tensor_tensor(s4, s4, -1.0, s3, ALU.mult, ALU.subtract))
        tt(s4, s4, s2, ALU.mult)
        dve.wait_ge(b_in, 16 * 4)
        tt(s3, br[:, :], s6, ALU.mult)
        tt(s5, bi[:, :], s4, ALU.mult)
        tt(s3, s3, s5, ALU.subtract)
        link(nc.vector.tensor_scalar(s3, s3, 2.0, None, ALU.mult))
        tt(s5, br[:, :], s4, ALU.mult)
        tt(s2, bi[:, :], s6, ALU.mult)
        tt(s5, s5, s2, ALU.add)
        link(nc.vector.tensor_scalar(s5, s5, 2.0, None, ALU.mult))
        gre = small[3][:, :].unsqueeze(2).to_broadcast([P, H, NK])
        gim = small[5][:, :].unsqueeze(2).to_broadcast([P, H, NK])
        dve.wait_ge(sines, 2)
        dve.wait_ge(decay_ready, 1)
        tt(pw[:, :, 0, :], pw[:, :, 0, :], decay, ALU.mult)
        tt(pw[:, :, 1, nk], pw[:, :, 1, nk], decay[:, :, nk], ALU.mult)
        p1, p2 = pw[:, :, 0, NA + NB:NT], pw[:, :, 1, NA + NB:NT]
        tq = phase[:, :, 0:NK]
        tt(q1[:, :, :], gre, p1, ALU.mult)
        tt(tq, gim, p2, ALU.mult)
        tt(q1[:, :, :], q1[:, :, :], tq, ALU.add)
        tt(q2[:, :, :], gre, p2, ALU.mult)
        tt(tq, gim, p1, ALU.mult)
        nc.vector.tensor_tensor(q2[:, :, :], q2[:, :, :], tq, ALU.subtract).then_inc(tables, 1)
        dve.wait_ge(tables, 1)
        dve.wait_ge(x_in, 64)

        def one_round(n, u):
            b, full = u % 2, u % BUFS
            hs = bass.ds(n * SUB, SUB)
            dve.wait_ge(round_done, n + 1)
            nc.vector.tensor_tensor(
                t1[:, full, :, :, :], pw[:, hs, 0, 0:NA].unsqueeze(3).to_broadcast([P, SUB, NA, NB]),
                pw[:, hs, 0, NA:NA + NB].unsqueeze(2).to_broadcast([P, SUB, NA, NB]), ALU.mult).then_inc(t1_ready, 1)
            nc.vector.tensor_tensor(
                cp[:, full, :, :, :], xre[:, hs, :].unsqueeze(3).to_broadcast([P, SUB, ROWS, NK]),
                q1[:, hs, :].unsqueeze(2).to_broadcast([P, SUB, ROWS, NK]), ALU.mult).then_inc(z1_ready, 1)
            dve.wait_ge(t1_ready, n + 1)
            dve.wait_ge(t2_ready, n + 1)
            nc.vector.tensor_tensor(t1[:, full, :, :, :], t1[:, full, :, :, :], t2[:, b, :, :, :], ALU.add).then_inc(u_ready, 1)
            dve.wait_ge(z1_ready, n + 1)
            dve.wait_ge(z2_ready, n + 1)
            nc.vector.tensor_tensor(cp[:, full, :, :, :], cp[:, full, :, :, :], z2[:, b, :, :, :], ALU.add).then_inc(cp_ready, 1)

        one_round(0, 0)
        one_round(1, 1)
        for jc in range(NF):
            for ih in range(2):
                n = 2 * jc + ih
                dve.wait_ge(wc_hi_ready, n + 1)
                nc.vector.tensor_tensor(wc_lo[:, jc, 512 * ih:512 * ih + 512], banks[:, jc, ih, :],
                                        wc_hi[:, jc, 512 * ih:512 * ih + 512].bitcast(F32), ALU.subtract).then_inc(wc_lo_ready, 1)
        for u in range(2, UNROLL):
            one_round(u, u)
        with dve.Fori(1, ROUNDS // UNROLL) as i:
            for u in range(UNROLL):
                one_round(UNROLL * i + u, u)
        dve.wait_ge(tok_ready, 2 + CS // SUB)
        sum_chunk_of(nc, tok, hsum, 0).then_inc(summed, 1)

    @block.scalar
    def _(act):
        for k in range(2):
            act.dma_start(conv_s[:, k, :], conv_t[k * P:(k + 1) * P, :]).then_inc(wload[k], 16)
            act.dma_start(wx_s[:, k, :], w_x[k * P:(k + 1) * P, :]).then_inc(wload[k], 16)
        for half in (slice(0, MODES), slice(MODES, P)):
            act.dma_start(br[half, :], b_ri[0]).then_inc(b_in, 16)
            act.dma_start(bi[half, :], b_ri[1]).then_inc(b_in, 16)
        act.wait_ge(adt_ready, 1)
        nc.scalar.activation(small[5][:, :], small[1][:, :], ACT.Tanh, scale=0.5).then_inc(g_exp, 1)
        nc.scalar.activation(small[6][:, :], small[1][:, :], ACT.Exp).then_inc(g_exp, 1)
        for k, multiple in enumerate(steps_tables()):
            ins = nc.scalar.activation(decay[:, :, k], small[1][:, :], ACT.Exp, scale=float(multiple))
        ins.then_inc(decay_ready, 1)
        lo, hi = slice(0, MODES), slice(MODES, P)

        def sine(part, kind, cols, sign):
            nc.scalar.activation(pw[part, :, kind, cols], phase[part, :, cols], ACT.Sin, scale=sign * TWO_PI)

        def cosine(part, kind, cols, sign):
            bias = halfpi if sign > 0 else minus_halfpi
            return nc.scalar.activation(pw[part, :, kind, cols], absolute[part, :, cols], ACT.Sin, bias=bias[part, :], scale=-sign * TWO_PI)

        act.wait_ge(angle_ready, 2)
        act.wait_ge(rest_turns, 2)
        act.wait_ge(dt_ready, 2)
        sine(slice(0, P), 1, nb, 1)
        act.wait_ge(abs_ready, 1)
        cosine(slice(0, P), 0, nb, 1).then_inc(sines, 1)
        sine(hi, 0, na, 1)
        sine(lo, 1, na, -1)
        sine(hi, 0, nk, -1)
        sine(lo, 1, nk, -1)
        act.wait_ge(abs_ready, 3)
        cosine(lo, 0, na, 1)
        cosine(hi, 1, na, 1)
        cosine(lo, 0, nk, 1)
        cosine(hi, 1, nk, -1).then_inc(sines, 1)
        for jc in range(NF):
            for ih in range(2):
                act.wait_ge(wc_done, 2 * jc + ih + 1)
                nc.scalar.activation(wc_hi[:, jc, 512 * ih:512 * ih + 512], banks[:, jc, ih, :], ACT.Copy).then_inc(wc_hi_ready, 1)
        with act.Fori(0, ROUNDS // UNROLL) as i:
            for u in range(UNROLL):
                n, b = UNROLL * i + u, u % 2
                act.wait_ge(round_done, n + 1 + BUFS)
                nc.scalar.activation(
                    tok[:, :, :, bass.ds(n * SUB, SUB)],
                    banks[:, 0, b, :].rearrange("p (h c a) -> p a c h", c=ROWS, a=NK), ACT.Copy).then_inc(tok_ready, 1)

    @block.tensor
    def _(pe):
        def join(slot, first, last=False):
            for jc in range(NF):
                for ih in range(2):
                    ins = nc.tensor.matmul(banks[:, jc, ih, :], wx_s[:, slot, jc * P:(jc + 1) * P],
                                           conv_s[:, slot, 512 * ih:512 * ih + 512], start=first, stop=last)
                    if last:
                        ins.then_inc(wc_done, 1)
            return ins

        pe.sem_inc(round_done, BUFS)
        pe.wait_ge(wload[0], 32)
        join(0, True).then_inc(w_used, 1)
        pe.wait_ge(wload[1], 32)
        join(1, False).then_inc(w_used, 1)
        with pe.Fori(0, NI // 2 - 2) as i:
            for slot in range(2):
                pe.wait_ge(wload[slot], 32 * i + 64)
                join(slot, False).then_inc(w_used, 1)
        pe.wait_ge(wload[0], 32 * (NI // 2))
        join(0, False).then_inc(w_used, 1)
        pe.wait_ge(wload[1], 32 * (NI // 2))
        join(1, False, last=True)
        pe.wait_ge(wc_lo_ready, 2)
        pe.sem_inc(tok_ready, 2)
        with pe.Fori(0, ROUNDS // UNROLL) as i:
            for u in range(UNROLL):
                n, b = UNROLL * i + u, u % 2
                pe.wait_ge(tok_ready, n + 1)
                pe.wait_ge(u_ready, n + 3)
                pe.wait_ge(cp_ready, n + 3)
                for h in range(SUB):
                    ins = nc.tensor.matmul(banks[:, 0, b, 64 * h:64 * h + 64],
                                           t1[:, u % BUFS, h, :, :].rearrange("p i j -> p (i j)"),
                                           cp[:, u % BUFS, h, :, :].rearrange("p c a -> p (c a)"), start=True, stop=True)
                ins.then_inc(round_done, 1)


def mlp_stage(nc, t, tok, spare, hsum, summed, wc_hi, wc_lo, w_z, w_out, skip_d, w_q, w_kvg, qkv_in, sem):
    def sb(name, shape, dt=F32):
        return t.enter_context(nc.sbuf_tensor(name, shape, dt))

    def ps(name, shape):
        return t.enter_context(nc.psum_tensor(name, shape, F32))

    PIECES, SLOTS = NF + NI // 2, (SPARE - NF * CT) // INTER
    wz_hi = sb("wz_hi", [P, NF, INTER], F32R)
    wz_lo = sb("wz_lo", [P, NF, INTER], F32R)
    wo_hi = sb("wo_hi", [P, NI, LEN], F32R)
    wo_lo = sb("wo_lo", [P, NI, LEN], F32R)
    skip = sb("skip", [P, NI])
    mean_w = sb("mean_w", [P, P])
    eps = sb("eps", [P, 1])
    cen = sb("cen", [P, NF, CT])
    sq = spare[:, 0:NF * CT].rearrange("p (a t) -> p a t", a=NF)
    ssum = rstd = hsum
    xn_hi = sb("xn_hi", [P, NF, CT], F32R)
    xn_lo = sb("xn_lo", [P, NF, CT], F32R)
    gate = sb("silu", [P, 2, CT])
    g = gate
    g_hi = sb("g_hi", [P, 2, CT], F32R)
    g_lo = sb("g_lo", [P, 2, CT], F32R)

    y_ps = ps("y_ps", [P, NF, CT])
    z_ps = ps("z_ps", [P, CT])
    x_ps = ps("x_ps", [P, CT])
    mean_ps = ps("mean_ps", [P, CT])
    var_ps = ps("var_ps", [P, CT])

    w_in = [sem(f"mlp_w_in{q}") for q in range(PIECES)]
    skip_in = sem("skip_in")
    whi = sem("mlp_w_hi")
    wlo = sem("mlp_w_lo")
    ready = sem("mlp_consts")
    mean_done = sem("mlp_mean")
    centred = sem("mlp_centred")
    squared = sem("mlp_squared")
    sq_summed = sem("mlp_sq_summed")
    var_done = sem("mlp_var")
    std_ready = sem("mlp_std")
    rstd_ready = sem("mlp_rstd")
    xn_ready = sem("mlp_xn")
    xhi_ready = sem("mlp_xhi")
    xlo_ready = sem("mlp_xlo")
    z_done = sem("z_done")
    x_done = sem("x_done")
    silu_ready = sem("silu_ready")
    g_ready = sem("g_ready")
    ghi_ready = sem("ghi_ready")
    glo_ready = sem("glo_ready")
    y_done = sem("y_done")
    res_ready = sem("mlp_res")

    def pieces():
        for a in range(NF):
            yield w_z[:, a, :], wz_hi[:, a, :], wz_lo[:, a, :]
        for i in range(0, NI, 2):
            yield w_out[:, i:i + 2, :].rearrange("p a b -> p (a b)"), flat(wo_hi[:, i:i + 2, :]), flat(wo_lo[:, i:i + 2, :])

    def landing(q):
        at = NF * CT + q % SLOTS * INTER
        return spare[:, at:at + INTER]

    def flat(ap):
        return ap.rearrange("p a b -> p (a b)")

    def chunk(n):
        return tok[:, :, :, bass.ds(n * CS, CS)]

    def rows(ap):
        return ap.rearrange("p (c s) -> p c s", c=ROWS) if len(ap.shape) == 2 else ap.rearrange("p a (c s) -> p a c s", c=ROWS)

    block = t.enter_context(nc.Block())

    @block.sync
    def _(sp):
        sp.dma_start(skip[:, :], skip_d).then_inc(skip_in, 16)
        for q, (src, hi, lo) in enumerate(pieces()):
            if q >= SLOTS:
                sp.wait_ge(wlo, q - SLOTS + 1)
            sp.dma_start(landing(q), src).then_inc(w_in[q], 16)
        sp.wait_ge(wlo, PIECES)
        for a in range(NF):
            sp.dma_start(spare[:, NF * LEN + a * KVG:NF * LEN + (a + 1) * KVG], w_kvg[:, a, :]).then_inc(qkv_in[a], 16)
        sp.wait_ge(sq_summed, CHUNKS)
        sp.dma_start(spare[:, 0:NF * LEN], w_q.rearrange("p a b -> p (a b)")).then_inc(qkv_in[NF], 16)

    @block.gpsimd
    def _(pool):
        for q, (src, hi, lo) in enumerate(pieces()):
            pool.wait_ge(whi, q + 1)
            nc.gpsimd.tensor_tensor(lo, landing(q), hi.bitcast(F32), ALU.subtract).then_inc(wlo, 1)

    @block.scalar
    def _(act):
        def whole(q0, q1):
            for q, (src, hi, lo) in list(enumerate(pieces()))[q0:q1]:
                act.wait_ge(w_in[q], 16)
                nc.scalar.activation(hi, landing(q), ACT.Copy).then_inc(whi, 1)

        def square(n):
            act.wait_ge(centred, n + 1)
            nc.scalar.activation(sq[:, :, :], cen[:, :, :], ACT.Square).then_inc(squared, 1)

        def std(n):
            act.wait_ge(var_done, n + 1)
            nc.scalar.activation(rstd[:, :], var_ps[:, :], ACT.Sqrt, bias=eps[:, :]).then_inc(std_ready, 1)

        def high(n):
            act.wait_ge(xn_ready, n + 1)
            for a in range(NF):
                nc.scalar.activation(xn_hi[:, a, :], cen[:, a, :], ACT.Copy).then_inc(xhi_ready, 1)

        def chunk_steps(n, more):
            def ghi(i):
                act.wait_ge(g_ready, NI * n + i + 1)
                nc.scalar.activation(g_hi[:, i % 2, :], g[:, i % 2, :], ACT.Copy).then_inc(ghi_ready, 1)

            for i in range(NI):
                act.wait_ge(z_done, NI * n + i + 1)
                if i:
                    act.wait_ge(glo_ready, NI * n + i - 1) if i > 1 else None
                nc.scalar.activation(gate[:, i % 2, :], z_ps[:, :], ACT.Silu).then_inc(silu_ready, 1)
                if i:
                    ghi(i - 1)
                if more and i == 1:
                    square(n + 1)
                if more and i == 4:
                    std(n + 1)
            ghi(NI - 1)
            if more:
                act.wait_ge(x_done, NI * n + NI)
                high(n + 1)

        act.wait_ge(ready, 2)
        square(0)
        whole(0, 3)
        std(0)
        whole(3, NF)
        high(0)
        whole(NF, PIECES)
        with act.Fori(0, CHUNKS - 1) as n:
            chunk_steps(n, True)
        chunk_steps(CHUNKS - 1, False)

    @block.vector
    def _(dve):
        nc.vector.memset(mean_w[:, :], 1.0 / LEN).then_inc(ready, 1)
        nc.vector.memset(eps[:, :], EPS).then_inc(ready, 1)
        def sum_chunk(n):
            dve.wait_ge(xn_ready, n)
            sum_chunk_of(nc, tok, hsum, n).then_inc(summed, 1)

        def centre(n):
            dve.wait_ge(mean_done, n + 1)
            nc.vector.tensor_tensor(rows(cen[:, :, :]), chunk(n),
                                    rows(mean_ps[:, :]).unsqueeze(1).to_broadcast([P, NF, ROWS, CS]), ALU.subtract).then_inc(centred, 1)

        def sum_squares(n):
            dve.wait_ge(squared, n + 1)
            nc.vector.tensor_reduce(ssum[:, :], sq[:, :, :].rearrange("p a t -> p t a"), AX, ALU.add).then_inc(sq_summed, 1)

        def normalise(n):
            dve.wait_ge(std_ready, n + 1)
            nc.vector.reciprocal(rstd[:, :], rstd[:, :]).then_inc(rstd_ready, 1)
            dve.wait_ge(rstd_ready, n + 1)
            nc.vector.tensor_tensor(cen[:, :, :], cen[:, :, :], rstd[:, :].unsqueeze(1).to_broadcast([P, NF, CT]),
                                    ALU.mult).then_inc(xn_ready, 1)

        def low(n):
            for a in range(NF):
                dve.wait_ge(xhi_ready, NF * n + a + 1)
                nc.vector.tensor_tensor(xn_lo[:, a, :], cen[:, a, :], xn_hi[:, a, :].bitcast(F32), ALU.subtract).then_inc(xlo_ready, 1)

        def chunk_steps(n, more):
            for i in range(NI):
                if more and i == 0:
                    sum_chunk(n + 1)
                dve.wait_ge(silu_ready, NI * n + i + 1)
                dve.wait_ge(x_done, NI * n + i + 1)
                nc.vector.scalar_tensor_tensor(g[:, i % 2, :], x_ps[:, :], skip[:, i:i + 1], gate[:, i % 2, :],
                                               ALU.mult, ALU.mult).then_inc(g_ready, 1)
                dve.wait_ge(ghi_ready, NI * n + i + 1)
                nc.vector.tensor_tensor(g_lo[:, i % 2, :], g[:, i % 2, :], g_hi[:, i % 2, :].bitcast(F32), ALU.subtract).then_inc(glo_ready, 1)
                if more and i == 0:
                    centre(n + 1)
                if more and i == 2:
                    sum_squares(n + 1)
                if more and i == 5:
                    normalise(n + 1)
            if more:
                low(n + 1)
            dve.wait_ge(y_done, NI * n + NI)
            nc.vector.tensor_tensor(chunk(n), rows(y_ps[:, :, :]), chunk(n), ALU.add).then_inc(res_ready, 1)

        centre(0)
        sum_squares(0)
        normalise(0)
        low(0)
        dve.wait_ge(skip_in, 16)
        with dve.Fori(0, CHUNKS - 1) as n:
            chunk_steps(n, True)
        chunk_steps(CHUNKS - 1, False)

    @block.tensor
    def _(pe):
        def mean(n):
            pe.wait_ge(summed, n + 1)
            nc.tensor.matmul(mean_ps[:, :], mean_w[:, :], hsum[:, :], start=True, stop=True).then_inc(mean_done, 1)

        def var(n):
            pe.wait_ge(sq_summed, n + 1)
            nc.tensor.matmul(var_ps[:, :], mean_w[:, :], ssum[:, :], start=True, stop=True).then_inc(var_done, 1)

        def project(n, acc, hi, lo, i, wait):
            for a in range(NF):
                if wait:
                    pe.wait_ge(xhi_ready, NF * n + a + 1)
                    pe.wait_ge(xlo_ready, NF * n + a + 1)
                cols = slice(i * P, (i + 1) * P)
                nc.tensor.matmul(acc, hi[:, a, cols], xn_hi[:, a, :], start=(a == 0), stop=False)
                nc.tensor.matmul(acc, hi[:, a, cols], xn_lo[:, a, :], start=False, stop=False)
                ins = nc.tensor.matmul(acc, lo[:, a, cols], xn_hi[:, a, :], start=False, stop=(a == NF - 1))
            return ins

        def put_out(n, i):
            if i % 2 == 0 and isinstance(n, int) and n == 0:
                pe.wait_ge(wlo, NF + i // 2 + 1)
            pe.wait_ge(ghi_ready, NI * n + i + 1)
            pe.wait_ge(glo_ready, NI * n + i + 1)
            for f in range(NF):
                cols = slice(f * P, (f + 1) * P)
                nc.tensor.matmul(y_ps[:, f, :], wo_hi[:, i, cols], g_hi[:, i % 2, :], start=(i == 0), stop=False)
                nc.tensor.matmul(y_ps[:, f, :], wo_hi[:, i, cols], g_lo[:, i % 2, :], start=False, stop=False)
                ins = nc.tensor.matmul(y_ps[:, f, :], wo_lo[:, i, cols], g_hi[:, i % 2, :], start=False, stop=(i == NI - 1))
            ins.then_inc(y_done, 1)

        def chunk_steps(n, more):
            for i in range(NI):
                if i:
                    pe.wait_ge(silu_ready, NI * n + i)
                project(n, z_ps[:, :], wz_hi, wz_lo, i, i == 0).then_inc(z_done, 1)
                if i:
                    pe.wait_ge(g_ready, NI * n + i)
                project(n, x_ps[:, :], wc_hi, wc_lo, i, False).then_inc(x_done, 1)
                if i:
                    put_out(n, i - 1)
                if more and i == 0:
                    mean(n + 1)
                if more and i == 3:
                    var(n + 1)
            put_out(n, NI - 1)

        pe.wait_ge(ready, 2)
        mean(0)
        var(0)
        pe.wait_ge(wlo, NF)
        chunk_steps(0, True)
        with pe.Fori(1, CHUNKS - 1) as n:
            chunk_steps(n, True)
        chunk_steps(CHUNKS - 1, False)


FILLS = (("k20", 0, 0), ("k21", 0, 0), ("r0", 2, 1), ("k22", 2, 0), ("r1", 3, 1), ("r2", 4, 1), ("q0", 4, 1),
         ("t2", 7, 0), ("mean", 7, 2), ("q1", 8, 1), ("k00", 10, 1), ("k01", 10, 1), ("k02", 12, 1),
         ("t0", 14, 1), ("k10", 14, 1), ("k11", 15, 1), ("var", 15, 2), ("k12", 18, 1), ("t1", 19, 1),
         ("q2", 21, 1), ("q3", 23, 1))
FILL_BANK = {name: k % 3 for k, (name, _, _) in enumerate(FILLS)}
PLACES = 24
OWN = [name for name, _, ahead in FILLS if ahead == 0]
AT_SUM, AT_CENTRE, AT_SQUARE, AT_SQ_SUM, AT_STD, AT_RSTD, AT_NORM = 2, 8, 10, 10, 18, 18, 23
AT_SPLIT = 2
AT_VALUES = {23: (0, 1), 7: (1, 0)}


def fills_at(m, p, some):
    return [(name, p + ahead) for name, place, ahead in FILLS if place == m and ahead in some]


TILES = 2 * 2 * NQ
SEGS = 16
TOK_TILES = PT // P


def segments(j):
    return {0: [(0, QB, 0)], 1: [(0, P, 1)], 2: [(0, P, 2), (P, QB, 3)]}[j]


class Links:

    def __init__(self, eng, sem, per, n):
        self.eng, self.sem, self.per, self.n, self.k = eng, sem, per, n, 0

    def __call__(self, ins):
        self.k += 1
        ins.then_inc(self.sem, 1)
        self.eng.wait_ge(self.sem, self.n * self.per + self.k)


def attention_stage(nc, t, tok, spare, hsum, qkv_in, ident_d, mask_d, diag_d, rev_d, out, sem):
    def sb(name, shape, dt=F32):
        return t.enter_context(nc.sbuf_tensor(name, shape, dt))

    def ps(name, shape):
        return t.enter_context(nc.psum_tensor(name, shape, F32))

    def flat(ap):
        return ap.rearrange("p a b -> p (a b)")

    G = P // HD
    wq_hi = sb("wq_hi", [P, NF, LEN], F32R)
    wq_lo = sb("wq_lo", [P, NF, LEN], F32R)
    wkv_hi = sb("wkv_hi", [P, NF, KVG], F32R)
    wkv_lo = sb("wkv_lo", [P, NF, KVG], F32R)
    ident = sb("ident", [P, P])
    ident_b = sb("ident_b", [P, QB], BF16)
    mask = sb("mask", [P, 2, QB], BF16)
    diag = sb("diag", [P, G])
    rev = sb("rev", [P, HEADS])
    eps = sb("eps3", [P, 1])
    NBLK = PT // QB
    res = spare[:, 0:2 * TILES * P].rearrange("p (b i f) -> p b i f", b=2, i=TILES)
    hpair = spare[:, 2 * TILES * P:2 * TILES * P + NF * PT].rearrange("p (x k g q) -> p x k g q", x=2, k=NBLK, g=2)
    sq_at = 2 * TILES * P + NF * PT
    sq = spare[:, sq_at:sq_at + NF * PT].rearrange("p (a s) -> p a s", a=NF)
    hsum, mean_w = hsum[:, 0:PT], hsum[:, PT:PT + P]
    rstd = hsum
    xn_hi = sb("xn3_hi", [P, NF, PT], F32R)
    xn_lo = sb("xn3_lo", [P, NF, PT], F32R)
    q_hi = sb("q_hi", [P, 2, 2, NBLK, 2, QB], F32R)
    q_lo = sb("q_lo", [P, 2, 2, NBLK, 2, QB], F32R)
    kb_hi = sb("kb_hi", [P, 2, G, PT], F32R)
    kb_lo = sb("kb_lo", [P, 2, G, PT], F32R)
    vb = sb("vb", [P, 2, 4, VC], BF16)
    km = sb("km", [P, HEADS, HD])
    vm = sb("vm", [P, HEADS, HD])
    kex = flat(sq[:, :, :])[:, 0:G * P].rearrange("p (g k) -> p g k", k=P)
    mask_f = flat(km[:, 0:4, :])
    krep = km[:, 4:4 + G, :]
    vsel = sb("vsel", [P, TOK_TILES, HD])
    one = sb("one", [P, 1])
    vblk = sb("vblk", [P, 4, HD])
    top = sb("top", [P, TOK_TILES])
    mx = sb("mx", [P, 1])
    below = sb("below", [P, HEADS])
    tie = sb("tie", [P, HEADS])
    tie_mx = sb("tie_mx", [P, 1])
    ind = sb("ind", [P, HEADS])
    gexp = sb("gexp", [P, HEADS])
    gsum = sb("gsum", [P, 1])
    prob = sb("prob", [P, 2, G, P + QB])
    smax = sb("smax", [P, 2, 2, G])
    pt_hi = sb("pt_hi", [P, 4, G * P], F16)
    pt_lo = sb("pt_lo", [P, 4, G * P], F16)
    rsum = sb("rsum", [P, 2, G])
    yparts = sb("yparts", [P, 2, G, VC])

    s_ps = ps("s_ps", [P, 2, 512])
    t_ps = ps("t_ps", [P, 2, 512])
    y_ps = ps("y_ps3", [P, 512])
    fill_banks = ps("fill_ps", [P, 3, 512])
    fill = {name: fill_banks[:, bank, :] for name, bank in FILL_BANK.items()}

    c_in = sem("att_consts_in")
    prob_set = sem("prob_set")
    settled_act = sem("settled_act")
    settled_pool = sem("settled_pool")
    whi = sem("qkv_hi")
    wlo = sem("qkv_lo")
    wlo_rest = sem("qkv_lo_rest")
    ready = sem("att_consts")
    hpair_in = sem("hpair_in")
    summed = sem("att_summed")
    mean_done = sem("att_mean")
    centred = sem("att_centred")
    squared = sem("att_squared")
    sq_summed = sem("att_sq_summed")
    var_done = sem("att_var")
    std_ready = sem("att_std")
    xn_ready = sem("att_xn")
    xhi_ready = sem("att_xhi")
    norm_step = sem("att_norm_step")
    rstd_ready = sem("att_rstd")
    top_ready = sem("gate_top")
    o_step = sem("o_step")
    xlo_ready = sem("att_xlo")
    q_done = sem("q_done")
    qhi_ready = sem("qhi_ready")
    qlo_ready = sem("qlo_ready")
    kv_done = sem("kv_done")
    shift_ready = sem("gate_shift")
    gexp_ready = sem("gate_exp")
    masked = sem("kv_masked")
    sum_step = sem("pool_sum_step")
    krep_ready = sem("krep_ready")
    kt_done = sem("kt_done")
    kex_ready = sem("kex_ready")
    kbhi_ready = sem("kbhi_ready")
    kblo_ready = sem("kblo_ready")
    vsel_ready = sem("vsel_ready")
    vblk_ready = sem("vblk_ready")
    vstep = sem("v_split_step")
    vb_ready = sem("vb_ready")
    res_done = sem("res_transposed")
    res_ready = sem("res_ready")
    link_proj = sem("proj_links")
    link_att = sem("att_links")
    s_done = sem("scores_done")
    less_ready = sem("less_ready")
    p_ready = sem("p_ready")
    t_done = sem("t_done")
    pthi_ready = sem("pthi_ready")
    ptlo_ready = sem("ptlo_ready")
    y_done = sem("y3_done")
    y_read = sem("y_read")
    rsum_ready = sem("rsum_ready")
    o_ready = sem("o_ready")
    out_done = [sem("out_done0"), sem("out_done1")]

    def pieces():
        for a in range(NF):
            at = NF * LEN + a * KVG
            yield qkv_in[a], spare[:, at:at + KVG], wkv_hi[:, a, :], wkv_lo[:, a, :]
        for a in range(0, NF, 2):
            yield qkv_in[NF], spare[:, a * LEN:(a + 2) * LEN], flat(wq_hi[:, a:a + 2, :]), flat(wq_lo[:, a:a + 2, :])

    def pair(n):
        return tok[:, :, bass.ds(2 * n, 2), :].rearrange("p a c s -> p a (c s)")

    def blocks(ap):
        return ap.rearrange("p (k q) -> p k q", q=QB)

    def tile(i):
        return i // (2 * NQ), i // NQ % 2, i % NQ

    def settle(eng):
        eng.sem_inc(settled_act if eng is nc.scalar else settled_pool, 1)

    SCALE = float(HD) ** -0.5
    OUT_CREDIT = 2 * TILES

    block = t.enter_context(nc.Block())

    @block.sync
    def _(sp):
        sp.dma_start(ident[:, :], ident_d).then_inc(c_in, 16)
        sp.dma_start(mask_f, mask_d).then_inc(c_in, 16)
        sp.dma_start(diag[:, :], diag_d).then_inc(c_in, 16)
        sp.dma_start(rev[:, :], rev_d.rearrange("(o h) -> o h", o=1).broadcast_to([P, HEADS])).then_inc(c_in, 16)
        def load_pair(n):
            for g in range(NF):
                sp.dma_start(hpair[:, g // 2, :, g % 2, :], blocks(pair(n)[:, g, :])).then_inc(hpair_in, 16)

        sp.wait_ge(res_ready, 3)
        load_pair(1)

        def pair_steps(p, b, more):
            if more:
                sp.wait_ge(res_ready, 3 * p + 6)
                load_pair(p + 2)
            for r in range(2):
                sp.wait_ge(o_ready, TILES * p + 6 * (r + 1) + OUT_CREDIT)
                for x in range(2):
                    for gh in range(2):
                        g = 2 * x + gh
                        dst = out[bass.ds(2 * p + r, 1), :, P * g:P * (g + 1)].rearrange("r (j q) f -> q (r j) f", q=QB)
                        sp.dma_start(dst, res[gh * QB:(gh + 1) * QB, b, 6 * r + NQ * x:6 * r + NQ * (x + 1), :]).then_inc(out_done[r], 16)

        with sp.Fori(0, PAIRS // 2 - 1) as i:
            pair_steps(2 * i, 0, True)
            pair_steps(2 * i + 1, 1, True)
        pair_steps(PAIRS - 2, 0, False)
        pair_steps(PAIRS - 1, 1, False)
        for r in range(2):
            sp.wait_ge(out_done[r], 64 * (PAIRS + 2))

    @block.gpsimd
    def _(pool):
        pool.sem_inc(o_ready, OUT_CREDIT)
        pool.sem_inc(out_done[0], 128)
        pool.sem_inc(out_done[1], 128)
        nc.gpsimd.memset(vblk[:, :, :], 0.0).then_inc(ready, 1)
        nc.gpsimd.memset(one[:, :], 1.0).then_inc(ready, 1)
        nc.gpsimd.memset(prob[:, :, :, QB:P], 0.0).then_inc(prob_set, 1)
        for b in range(2):
            nc.gpsimd.memset(vb[:, b, :, VC - 1:VC], 1.0).then_inc(ready, 1)
        add = ALU.add
        for i, (w_in, raw, hi, lo) in enumerate(pieces()):
            if i not in (0, 2):
                pool.wait_ge(whi, i + 1)
                nc.gpsimd.tensor_tensor(lo, raw, hi.bitcast(F32), ALU.subtract).then_inc(wlo_rest, 1)
        SUM_STEPS = 2 * TOK_TILES * 3
        NORM_STEPS = 4
        norm_link = [None]

        def halve(x, step):
            for half in (8, 4, 2):
                step(nc.gpsimd.tensor_tensor(x[:, 0:half, :], x[:, 0:half, :], x[:, half:2 * half, :], add))

        def sum_chunks(x, step, done):
            step(nc.gpsimd.tensor_tensor(hsum, x[:, 0, :], x[:, 1, :], add))
            settle(nc.gpsimd)
            step(nc.gpsimd.tensor_tensor(hsum, hsum, x[:, 2, :], add))
            settle(nc.gpsimd)
            nc.gpsimd.tensor_tensor(hsum, hsum, x[:, 3, :], add).then_inc(done, 1)

        def norm(n, m):
            if m == AT_SUM:
                norm_link[0] = Links(pool, norm_step, NORM_STEPS, n - 1)
                pool.wait_ge(xn_ready, n)
                settle(nc.gpsimd)
                sum_chunks(pair(n), norm_link[0], summed)
            if m == AT_SQ_SUM:
                pool.wait_ge(squared, n + 1)
                sum_chunks(sq, norm_link[0], sq_summed)

        def values(n, b, r):
            pool.wait_ge(vblk_ready, 2 * n + r + 1)
            step = Links(pool, vstep, 8, n)
            step.k = 4 * r
            blks = slice(2 * r, 2 * r + 2)
            for part in range(3):
                piece = vb[:, b, blks, (2 - part) * HD:(3 - part) * HD]
                ins = nc.gpsimd.tensor_tensor(piece, vblk[:, blks, :], one[:, :].unsqueeze(2).to_broadcast([P, 2, HD]), ALU.mult)
                if part == 2:
                    ins.then_inc(vb_ready, 1)
                else:
                    step(ins)
                    step(nc.gpsimd.tensor_tensor(vblk[:, blks, :], vblk[:, blks, :], piece, ALU.subtract))

        def beside(p, b, m, some):
            for name, n in fills_at(m, p, some):
                nb = b if name in OWN else 1 - b
                tt = int(name[1]) if name[0] in "kt" else 0
                done = TOK_TILES * n + tt
                step = Links(pool, sum_step, SUM_STEPS, n)
                step.k = 6 * tt
                if name[0] == "k" and name[2] == "1":
                    pool.wait_ge(masked, 3 * done + 2)
                    halve(km, step)
                    pair_of = [km[:, h, :].unsqueeze(1).to_broadcast([P, G, HD]) for h in range(2)]
                    nc.gpsimd.tensor_tensor(krep, pair_of[0], pair_of[1], add).then_inc(krep_ready, 1)
                if name[0] == "k" and name[2] == "2":
                    step.k += 3
                    pool.wait_ge(masked, 3 * done + 3)
                    halve(vm, step)
                    nc.gpsimd.tensor_tensor(vsel[:, tt, :], vm[:, 0, :], vm[:, 1, :], add).then_inc(vsel_ready, 1)
                if name[0] == "t":
                    pool.wait_ge(kbhi_ready, done + 1)
                    nc.gpsimd.tensor_tensor(kb_lo[:, nb, :, tt * P:(tt + 1) * P], kex,
                                            kb_hi[:, nb, :, tt * P:(tt + 1) * P].bitcast(F32), ALU.subtract).then_inc(kblo_ready, 1)
            if m in AT_VALUES and AT_VALUES[m][1] in some:
                r, ahead = AT_VALUES[m]
                values(p + ahead, b if ahead == 0 else 1 - b, r)
            if 2 in some:
                norm(p + 2, m)

        def finish(p, b, i):
            e = i % 2
            step = Links(pool, o_step, 3 * TILES, p)
            step.k = 3 * i
            pool.wait_ge(rsum_ready, TILES * p + i + 1)
            if i % 4 == 0:
                pool.wait_ge(res_ready, 3 * p + i // 4 + 1)
            y = yparts[:, e, :, :]
            v1 = y[:, :, 2 * HD:3 * HD]
            step(nc.gpsimd.tensor_tensor(v1, v1, y[:, :, HD:2 * HD], add))
            step(nc.gpsimd.tensor_tensor(v1, v1, y[:, :, 0:HD], add))
            step(nc.gpsimd.tensor_tensor(v1, v1, rsum[:, e, :].unsqueeze(2).to_broadcast([P, G, HD]), ALU.mult))
            o = res[:, b, i, :].rearrange("p (g d) -> p g d", d=HD)
            nc.gpsimd.tensor_tensor(o, v1, o, add).then_inc(o_ready, 1)

        def pair_steps(p, b, some):
            for i in range(TILES):
                beside(p, b, 2 * i, some)
                beside(p, b, 2 * i + 1, some)
                if i > 0:
                    finish(p, b, i - 1)
            finish(p, b, TILES - 1)

        pool.wait_ge(ready, 8)
        for m in range(PLACES):
            beside(-1, 1, m, (1, 2))
        with pool.Fori(0, PAIRS // 2 - 1) as i:
            pair_steps(2 * i, 0, (0, 1, 2))
            pair_steps(2 * i + 1, 1, (0, 1, 2))
        pair_steps(PAIRS - 2, 0, (0, 1))
        pair_steps(PAIRS - 1, 1, (0,))

    @block.scalar
    def _(act):
        def split_weights(pieces_of):
            for w_in, raw, hi, lo in pieces_of:
                act.wait_ge(w_in, 16)
                nc.scalar.activation(hi, raw, ACT.Copy).then_inc(whi, 1)

        split_weights(list(pieces())[:NF])
        act.wait_ge(c_in, 64)
        nc.scalar.activation(mask[:, :, :], mask_f.rearrange("p (g q) -> p g q", g=2), ACT.Copy).then_inc(ready, 1)
        nc.scalar.activation(ident_b[:, :], ident[:, 0:QB], ACT.Copy).then_inc(ready, 1)
        act.wait_ge(wlo, 2)
        act.wait_ge(wlo_rest, 1)
        for g in range(NF):
            nc.scalar.activation(hpair[:, g // 2, :, g % 2, :], blocks(pair(0)[:, g, :]), ACT.Copy).then_inc(hpair_in, 16)
        split_weights(list(pieces())[NF:])
        act.wait_ge(wlo_rest, 2)

        def norm(n, m):
            if m == AT_SQUARE:
                act.wait_ge(centred, n + 1)
                if not isinstance(n, int) or n > 1:
                    act.wait_ge(kblo_ready, TOK_TILES * (n - 1))
                settle(nc.scalar)
                nc.scalar.activation(sq[:, :, :], pair(n), ACT.Square).then_inc(squared, 1)
            if m == AT_STD:
                act.wait_ge(var_done, n + 1)
                nc.scalar.activation(rstd, fill["var"][:, 0:PT], ACT.Sqrt, bias=eps[:, :]).then_inc(std_ready, 1)

        def split(n):
            act.wait_ge(xn_ready, n + 1)
            if not (isinstance(n, int) and n == 0):
                act.wait_ge(kv_done, 3 * TOK_TILES * n)
            settle(nc.scalar)
            for a in range(NF):
                nc.scalar.activation(xn_hi[:, a, :], pair(n)[:, a, :], ACT.Copy).then_inc(xhi_ready, 1)

        def beside(p, b, m, some):
            for name, n in fills_at(m, p, some):
                nb = b if name in OWN else 1 - b
                src = fill[name]
                if name[0] == "r":
                    f = int(name[1])
                    act.wait_ge(res_done, 3 * n + f + 1)
                    for r in sorted({4 * f // 6, (4 * f + 3) // 6}):
                        act.wait_ge(out_done[r], 64 * (n + 1))
                    nc.scalar.activation(res[:, nb, 4 * f:4 * f + 4, :], src.rearrange("p (i f) -> p i f", i=4), ACT.Copy)\
                        .then_inc(res_ready, 1)
                if name[0] == "q":
                    g = int(name[1])
                    act.wait_ge(q_done, NF * n + g + 1)
                    nc.scalar.activation(q_hi[:, nb, g // 2, :, g % 2, :], blocks(src[:, 0:PT]), ACT.Copy).then_inc(qhi_ready, 1)
                if name[0] == "k" and name[2] == "0":
                    act.wait_ge(shift_ready, TOK_TILES * n + int(name[1]) + 1)
                    nc.scalar.activation(gexp[:, :], below[:, :], ACT.Exp, accum_out=gsum[:, :]).then_inc(gexp_ready, 1)
                if name[0] == "t":
                    tt = int(name[1])
                    act.wait_ge(kex_ready, TOK_TILES * n + tt + 1)
                    nc.scalar.activation(kb_hi[:, nb, :, tt * P:(tt + 1) * P], kex, ACT.Copy).then_inc(kbhi_ready, 1)
            if m == AT_SPLIT and 1 in some:
                split(p + 1)
            if 2 in some:
                norm(p + 2, m)

        def exps(p, i):
            segs = segments(i % NQ)
            act.wait_ge(less_ready, SEGS * p + 4 * (i // NQ) + segs[-1][2] + 3)
            keys = slice(0, segs[-1][0] + segs[-1][1])
            nc.scalar.activation(prob[:, i % 2, :, keys], prob[:, i % 2, :, keys], ACT.Exp, scale=SCALE).then_inc(p_ready, 1)

        def high(p, i):
            for k0, keys, s in segments(i % NQ):
                s += 4 * (i // NQ)
                act.wait_ge(t_done, SEGS * p + s + 1)
                nc.scalar.activation(pt_hi[0:keys, s % 4, :], t_ps[0:keys, s % 2, :], ACT.Copy).then_inc(pthi_ready, 1)

        def keep_output(p, i):
            act.wait_ge(y_done, TILES * p + i + 1)
            act.wait_ge(o_ready, TILES * p + i - 1 + OUT_CREDIT)
            nc.scalar.activation(flat(yparts[:, i % 2, :, :]), y_ps[:, 0:G * VC], ACT.Copy).then_inc(y_read, 1)

        def pair_steps(p, b, some):
            for i in range(TILES):
                beside(p, b, 2 * i, some)
                high(p, i)
                if i + 1 < TILES:
                    exps(p, i + 1)
                elif 1 in some:
                    exps(p + 1, 0)
                if i:
                    keep_output(p, i - 1)
                beside(p, b, 2 * i + 1, some)
            keep_output(p, TILES - 1)

        act.sem_inc(y_read, 1)
        act.wait_ge(prob_set, 1)
        act.wait_ge(ready, 8)
        for m in range(PLACES):
            norm(0, m)
        for m in range(PLACES):
            beside(-1, 1, m, (1, 2))
        exps(0, 0)
        with act.Fori(0, PAIRS // 2 - 1) as i:
            pair_steps(2 * i, 0, (0, 1, 2))
            pair_steps(2 * i + 1, 1, (0, 1, 2))
        pair_steps(PAIRS - 2, 0, (0, 1))
        pair_steps(PAIRS - 1, 1, (0,))

    @block.vector
    def _(dve):
        nc.vector.memset(mean_w, 1.0 / LEN).then_inc(ready, 1)
        nc.vector.memset(eps[:, :], EPS).then_inc(ready, 1)
        dve.sem_inc(ptlo_ready, 2)

        for i, (w_in, raw, hi, lo) in enumerate(pieces()):
            if i in (0, 2):
                dve.wait_ge(whi, i + 1)
                nc.vector.tensor_tensor(lo, raw, hi.bitcast(F32), ALU.subtract).then_inc(wlo, 1)
        nc.vector.tensor_reduce(hsum, pair(0).rearrange("p a s -> p s a"), AX, ALU.add).then_inc(summed, 1)
        dve.sem_inc(less_ready, 2)
        PROJ_LINKS = 4 * TOK_TILES + 2 * 2

        def over_heads(x, heads):
            return x[:, heads].unsqueeze(2).to_broadcast([P, heads.stop - heads.start, HD])

        def by_head(x):
            return x.rearrange("p (h d) -> p h d", d=HD)

        def norm(n, m):
            if m == AT_CENTRE:
                dve.wait_ge(mean_done, n + 1)
                dve.wait_ge(hpair_in, 64 * (n + 1))
                nc.vector.tensor_tensor(pair(n), pair(n), fill["mean"][:, 0:PT].unsqueeze(1).to_broadcast([P, NF, PT]),
                                        ALU.subtract).then_inc(centred, 1)
            if m == AT_RSTD:
                dve.wait_ge(std_ready, n + 1)
                nc.vector.reciprocal(rstd, rstd).then_inc(rstd_ready, 1)
            if m == AT_NORM:
                dve.wait_ge(rstd_ready, n + 1)
                nc.vector.tensor_tensor(pair(n), pair(n), rstd.unsqueeze(1).to_broadcast([P, NF, PT]), ALU.mult)\
                    .then_inc(xn_ready, 1)

        def beside(p, b, m, some):
            for name, n in fills_at(m, p, some):
                nb = b if name in OWN else 1 - b
                if name[0] == "q":
                    g = int(name[1])
                    dve.wait_ge(qhi_ready, NF * n + g + 1)
                    nc.vector.tensor_tensor(q_lo[:, nb, g // 2, :, g % 2, :], blocks(fill[name][:, 0:PT]),
                                            q_hi[:, nb, g // 2, :, g % 2, :].bitcast(F32), ALU.subtract).then_inc(qlo_ready, 1)
                if name[0] == "k":
                    select(n, int(name[1]), int(name[2]), fill[name])
                if name[0] == "t":
                    tt = int(name[1])
                    dve.wait_ge(kt_done, TOK_TILES * n + tt + 1)
                    if tt:
                        dve.wait_ge(kblo_ready, TOK_TILES * n + tt)
                    squares = p + 2 if name in OWN or 2 not in some else p + 3
                    dve.wait_ge(sq_summed, min(squares, PAIRS) if isinstance(p, int) else squares)
                    nc.vector.tensor_tensor(kex, fill[name][:, 0:P].unsqueeze(1).to_broadcast([P, G, P]),
                                            diag[:, :].unsqueeze(2).to_broadcast([P, G, P]), ALU.mult).then_inc(kex_ready, 1)
            if m == AT_SPLIT and 1 in some:
                for a in range(NF):
                    dve.wait_ge(xhi_ready, NF * (p + 1) + a + 1)
                    nc.vector.tensor_tensor(xn_lo[:, a, :], pair(p + 1)[:, a, :], xn_hi[:, a, :].bitcast(F32), ALU.subtract)\
                        .then_inc(xlo_ready, 1)
            if m in AT_VALUES and AT_VALUES[m][1] in some:
                r, ahead = AT_VALUES[m]
                shift_values(p + ahead, r)
            if 2 in some:
                norm(p + 2, m)

        def select(n, tt, part, src):
            link = Links(dve, link_proj, PROJ_LINKS, n)
            link.k = 4 * tt + (2 if tt == TOK_TILES - 1 else 0)
            done = TOK_TILES * n + tt
            dve.wait_ge(kv_done, 3 * done + part + 1)
            if part == 0:
                logits = src[:, 0:HEADS]
                link(nc.vector.tensor_reduce(mx[:, :], logits, AX, ALU.max))
                nc.vector.tensor_scalar(below[:, :], logits, mx[:, :], None, ALU.subtract).then_inc(shift_ready, 1)
                dve.wait_ge(shift_ready, done + 1)
                link(nc.vector.scalar_tensor_tensor(tie[:, :], below[:, :], 0.0, rev[:, :], ALU.is_equal, ALU.mult))
                link(nc.vector.tensor_reduce(tie_mx[:, :], tie[:, :], AX, ALU.max))
                link(nc.vector.tensor_scalar(ind[:, :], tie[:, :], tie_mx[:, :], None, ALU.is_equal))
                if tt:
                    dve.wait_ge(kt_done, done)
                nc.vector.tensor_tensor(km[:, 0:10, :], by_head(src[:, 16:336]), over_heads(ind, slice(0, 10)), ALU.mult)\
                    .then_inc(masked, 1)
            if part == 1:
                nc.vector.tensor_tensor(km[:, 10:16, :], by_head(src[:, 0:192]), over_heads(ind, slice(10, 16)), ALU.mult)
                if tt:
                    dve.wait_ge(vsel_ready, done)
                nc.vector.tensor_tensor(vm[:, 0:5, :], by_head(src[:, 192:352]), over_heads(ind, slice(0, 5)), ALU.mult)\
                    .then_inc(masked, 1)
            if part == 2:
                nc.vector.tensor_tensor(vm[:, 5:16, :], by_head(src[:, 0:352]), over_heads(ind, slice(5, 16)), ALU.mult)\
                    .then_inc(masked, 1)
                dve.wait_ge(gexp_ready, done + 1)
                nc.vector.reciprocal(top[:, tt:tt + 1], gsum[:, :]).then_inc(top_ready, 1)

        def shift_values(n, r):
            link = Links(dve, link_proj, PROJ_LINKS, n)
            link.k = (4 * (TOK_TILES - 1), 4 * TOK_TILES + 2)[r]
            dve.wait_ge(vsel_ready, TOK_TILES * n + r + 2)
            dve.wait_ge(top_ready, TOK_TILES * n + r + 2)
            new = (slice(0, 2), slice(2, 3))[r]
            link(nc.vector.tensor_tensor(vsel[:, new, :], vsel[:, new, :],
                                         top[:, new].unsqueeze(2).to_broadcast([P, new.stop - new.start, HD]), ALU.mult))
            if r == 0:
                nc.vector.tensor_copy(vblk[:, 0, :], vsel[:, 0, :])
                link(nc.vector.tensor_copy(vblk[0:QB, 1, :], vsel[0:QB, 1, :]))
            else:
                nc.vector.tensor_copy(vblk[0:QB, 2, :], vsel[QB:P, 1, :])
                nc.vector.tensor_copy(vblk[QB:P, 2, :], vsel[0:QB, 2, :])
                link(nc.vector.tensor_copy(vblk[0:QB, 3, :], vsel[QB:P, 2, :]))
            dve.sem_inc(vblk_ready, 1)

        def softmax(p, i):
            e = i % 2
            segs = segments(i % NQ)
            dve.wait_ge(s_done, TILES * p + i + 1)
            for k0, keys, s in segs:
                nc.vector.tensor_reduce(smax[:, e, int(k0 > 0), :], s_ps[:, s % 2, 0:G * keys].rearrange("p (g k) -> p g k", k=keys),
                                        AX, ALU.max).then_inc(link_att, 1)
            done = 5 * (i // NQ) + (1, 2, 4)[i % NQ]
            dve.wait_ge(link_att, 20 * p + done)
            if len(segs) == 2:
                nc.vector.tensor_tensor(smax[:, e, 0, :], smax[:, e, 0, :], smax[:, e, 1, :], ALU.max).then_inc(link_att, 1)
                dve.wait_ge(link_att, 20 * p + done + 1)
            for k0, keys, s in segs:
                cols = slice(k0, k0 + keys)
                nc.vector.tensor_tensor(prob[:, e, :, cols], s_ps[:, s % 2, 0:G * keys].rearrange("p (g k) -> p g k", k=keys),
                                        smax[:, e, 0, :].unsqueeze(2).to_broadcast([P, G, keys]), ALU.subtract)\
                    .then_inc(less_ready, 1)

        def low(p, i):
            for k0, keys, s in segments(i % NQ):
                s += 4 * (i // NQ)
                dve.wait_ge(pthi_ready, SEGS * p + s + 1)
                nc.vector.tensor_tensor(pt_lo[0:keys, s % 4, :], t_ps[0:keys, s % 2, :], pt_hi[0:keys, s % 4, :], ALU.subtract)\
                    .then_inc(ptlo_ready, 1)

        def invert_sum(p, i):
            dve.wait_ge(y_read, TILES * p + i + 2)
            nc.vector.reciprocal(rsum[:, i % 2, :], yparts[:, i % 2, :, VC - 1]).then_inc(rsum_ready, 1)

        def pair_steps(p, b, some):
            for i in range(TILES):
                if i + 1 < TILES:
                    softmax(p, i + 1)
                elif 1 in some:
                    softmax(p + 1, 0)
                beside(p, b, 2 * i, some)
                low(p, i)
                beside(p, b, 2 * i + 1, some)
                if i:
                    invert_sum(p, i - 1)
            invert_sum(p, TILES - 1)

        dve.wait_ge(ready, 8)
        norm(0, AT_CENTRE)
        dve.wait_ge(squared, 1)
        nc.vector.tensor_reduce(hsum, sq.rearrange("p a s -> p s a"), AX, ALU.add).then_inc(sq_summed, 1)
        norm(0, AT_RSTD)
        dve.wait_ge(rstd_ready, 1)
        nc.vector.tensor_tensor(pair(0), pair(0), rstd.unsqueeze(1).to_broadcast([P, NF, PT]), ALU.mult).then_inc(xn_ready, 1)
        for m in range(PLACES):
            beside(-1, 1, m, (1, 2))
        softmax(0, 0)
        with dve.Fori(0, PAIRS // 2 - 1) as i:
            pair_steps(2 * i, 0, (0, 1, 2))
            pair_steps(2 * i + 1, 1, (0, 1, 2))
        pair_steps(PAIRS - 2, 0, (0, 1))
        pair_steps(PAIRS - 1, 1, (0,))

    @block.tensor
    def _(pe):
        def three(acc, lh, ll, rh, rl, first, last):
            nc.tensor.matmul(acc, lh, rh, start=first, stop=False)
            nc.tensor.matmul(acc, lh, rl, start=False, stop=False)
            return nc.tensor.matmul(acc, ll, rh, start=False, stop=last)

        def norm_fill(n, name):
            acc = fill[name][:, 0:PT]
            if name == "mean":
                pe.wait_ge(summed, n + 1)
                nc.tensor.matmul(acc, mean_w, hsum, start=True, stop=True).then_inc(mean_done, 1)
            else:
                pe.wait_ge(sq_summed, n + 1)
                nc.tensor.matmul(acc, mean_w, hsum, start=True, stop=True).then_inc(var_done, 1)

        def bank_free(p, k, some):
            while True:
                k -= 3
                name, _, ahead = FILLS[k]
                if k < 0:
                    if isinstance(p, int) and p < 0:
                        return
                    ahead -= 1
                elif ahead not in some:
                    continue
                break
            kind, n = name[0], p + ahead
            if kind == "r":
                pe.wait_ge(res_ready, 3 * n + int(name[1]) + 1)
            elif kind == "q":
                pe.wait_ge(qlo_ready, NF * n + int(name[1]) + 1)
            elif kind == "k":
                pe.wait_ge(masked, 3 * (TOK_TILES * n + int(name[1])) + int(name[2]) + 1)
            elif kind == "t":
                pe.wait_ge(kex_ready, TOK_TILES * n + int(name[1]) + 1)
            elif name == "mean":
                pe.wait_ge(centred, n + 1)
            elif name == "var":
                pe.wait_ge(std_ready, n + 1)

        def beside(p, b, m, some):
            for k, (name, place, ahead) in enumerate(FILLS):
                if place != m or ahead not in some:
                    continue
                bank_free(p, k, some)
                n = p + ahead
                src = fill[name]
                if name in ("mean", "var"):
                    norm_fill(n, name)
                if name[0] == "r":
                    f = int(name[1])
                    pe.wait_ge(hpair_in, 64 * n + 64)
                    for x in range(4):
                        r, gp, j = tile(4 * f + x)
                        ins = nc.tensor.transpose(src[:, x * P:(x + 1) * P], hpair[:, gp, NQ * r + j, :, :].rearrange("p g q -> p (g q)"),
                                                  ident[:, :])
                    ins.then_inc(res_done, 1)
                if name[0] == "q":
                    g = int(name[1])
                    cols = slice(g * P, (g + 1) * P)
                    for a in range(NF):
                        if g == 0:
                            pe.wait_ge(xlo_ready, NF * n + a + 1)
                        ins = three(src[:, 0:PT], wq_hi[:, a, cols], wq_lo[:, a, cols], xn_hi[:, a, :], xn_lo[:, a, :], a == 0, a == NF - 1)
                    ins.then_inc(q_done, 1)
                if name[0] == "k":
                    tt, part = int(name[1]), int(name[2])
                    c0 = sum(KV_BANK[:part])
                    cols = slice(c0, c0 + KV_BANK[part])
                    toks = slice(tt * P, (tt + 1) * P)
                    for a in range(NF):
                        ins = three(src[:, 0:KV_BANK[part]], xn_hi[:, a, toks], xn_lo[:, a, toks],
                                    wkv_hi[:, a, cols], wkv_lo[:, a, cols], a == 0, a == NF - 1)
                    ins.then_inc(kv_done, 1)
                if name[0] == "t":
                    pe.wait_ge(krep_ready, TOK_TILES * n + int(name[1]) + 1)
                    nc.tensor.transpose(src[:, 0:P], flat(krep), ident[:, :]).then_inc(kt_done, 1)

        def scores(p, b, i):
            r, gp, j = tile(i)
            if i in (0, TILES // 2):
                pe.wait_ge(kblo_ready, TOK_TILES * p + r + 2)
            if i in (0, NQ):
                pe.wait_ge(qlo_ready, NF * p + 2 * gp + 2)
            qh, ql = (q[:, b, gp, NQ * r + j, :, :].rearrange("p g q -> p (g q)") for q in (q_hi, q_lo))
            for k0, keys, s in segments(j):
                ks = slice(STEPS * r + k0, STEPS * r + k0 + keys)
                acc = s_ps[:, s % 2, 0:G * keys].rearrange("p (g k) -> p g k", k=keys)
                pe.wait_ge(less_ready, SEGS * p + 4 * (i // NQ) + s + 1)
                masked_here = (keys + k0) == QB * (j + 1)
                ins = three(acc, qh, ql, kb_hi[:, b, :, ks], kb_lo[:, b, :, ks], True, not masked_here)
                if masked_here:
                    ins = nc.tensor.matmul(acc[:, :, keys - QB:keys], flat(mask[:, :, :]), ident_b[:, :].unsqueeze(1).to_broadcast([P, G, QB]),
                                           start=False, stop=True)
            ins.then_inc(s_done, 1)

        def transposes_free(p, i):
            pe.wait_ge(p_ready, TILES * p + i + 1)
            pe.wait_ge(ptlo_ready, SEGS * p + 4 * (i // NQ) + segments(i % NQ)[-1][2] + 1)

        def transposes(p, i):
            for k0, keys, s in segments(i % NQ):
                s += 4 * (i // NQ)
                cols = slice(0, P) if k0 == 0 else slice(k0, k0 + keys)
                for g in range(G):
                    ins = nc.tensor.transpose(t_ps[0:cols.stop - cols.start, s % 2, g * P:(g + 1) * P], prob[:, i % 2, g, cols], ident[:, :])
                ins.then_inc(t_done, 1)

        def values(p, b, i):
            r, gp, j = tile(i)
            segs = segments(j)
            if i in (0, TILES // 2):
                pe.wait_ge(vb_ready, 2 * p + r + 1)
            pe.wait_ge(y_read, TILES * p + i + 1)
            last_seg = SEGS * p + 4 * (i // NQ) + segs[-1][2] + 1
            pe.wait_ge(ptlo_ready, last_seg + 2)
            for g in range(G):
                acc = y_ps[:, g * VC:(g + 1) * VC]
                for x, (k0, keys, s) in enumerate(segs):
                    rows = slice(0, keys)
                    v = vb[rows, b, 2 * r + (k0 > 0), :]
                    nc.tensor.matmul(acc, pt_hi[rows, s, g * P:(g + 1) * P], v, start=(x == 0), stop=False)
                    ins = nc.tensor.matmul(acc[:, HD:VC], pt_lo[rows, s, g * P:(g + 1) * P], v[:, HD:VC], start=False,
                                           stop=(x == len(segs) - 1))
            ins.then_inc(y_done, 1)

        def pair_steps(p, b, some):
            for i in range(TILES):
                if i + 1 < TILES:
                    scores(p, b, i + 1)
                elif 1 in some:
                    scores(p + 1, 1 - b, 0)
                beside(p, b, 2 * i, some)
                transposes_free(p, i)
                transposes(p, i)
                if i:
                    values(p, b, i - 1)
                beside(p, b, 2 * i + 1, some)
            values(p, b, TILES - 1)

        pe.wait_ge(ready, 8)
        norm_fill(0, "mean")
        norm_fill(0, "var")
        pe.wait_ge(wlo, 2)
        pe.wait_ge(wlo_rest, 4)
        pe.wait_ge(std_ready, 1)
        for m in range(PLACES):
            beside(-1, 1, m, (1, 2))
        scores(0, 0, 0)
        with pe.Fori(0, PAIRS // 2 - 1) as i:
            pair_steps(2 * i, 0, (0, 1, 2))
            pair_steps(2 * i + 1, 1, (0, 1, 2))
        pair_steps(PAIRS - 2, 0, (0, 1))
        pair_steps(PAIRS - 1, 1, (0,))


def layout(inputs):
    import numpy as _np
    c = _np.ascontiguousarray
    w_in = _np.asarray(inputs["L0_attn_W_in"])
    qkv = _np.asarray(inputs["L0_ffn_W_qkv"])
    width = LEN

    def chunks(w):
        return c(w.reshape(-1, P, w.shape[1]).transpose(1, 0, 2))

    wq, wk, wv = qkv[:width].T, qkv[width:2 * width].T, qkv[2 * width:].T
    kvg = _np.concatenate([_np.asarray(inputs["L0_ffn_W_gate"]).T, wk, wv], axis=1)
    q, k = _np.arange(QB), _np.arange(QB)
    mask_t = _np.zeros((P, 2, QB), _np.float32)
    mask_t[:QB] = _np.where(k[:, None, None] > q[None, None, :], _np.float32(-1e30), _np.float32(0))
    diag = (_np.arange(P)[:, None] // HD == _np.arange(P // HD)[None, :]).astype(_np.float32)
    return {
        "log_dt": c(inputs["L0_tok_log_dt"]),
        "a_imag": c(_np.asarray(inputs["L0_tok_A_imag"]).T),
        "inv_a_real": c(_np.asarray(inputs["L0_tok_inv_A_real"]).T),
        "b_ri": c(_np.asarray(inputs["L0_tok_B_ri"]).transpose(2, 1, 0)),
        "x_ri": c(_np.asarray(inputs["x"]).transpose(3, 2, 1, 0)),
        "w_x": c(w_in[:INTER]),
        "conv_t": c(_np.asarray(inputs["L0_attn_conv_w"]).T),
        "w_z": chunks(w_in[INTER:].T),
        "w_out": chunks(_np.asarray(inputs["L0_attn_W_out"]).T),
        "skip_d": c(_np.asarray(inputs["L0_attn_D"]).reshape(NI, P).T),
        "w_q": chunks(wq),
        "w_kvg": chunks(kvg),
        "mults": steps_tables(),
        "ident": _np.eye(P, dtype=_np.float32),
        "mask_t": c(mask_t.reshape(P, P)),
        "diag": diag,
        "rev": _np.arange(HEADS, 0, -1).astype(_np.float32),
    }


def kernel(**inputs):
    import concourse.bacc as _bacc
    from concourse import mybir as _mybir
    from concourse.bass_utils import run_bass_kernel_spmd as _run

    nc = _bacc.Bacc("TRN2", target_bir_lowering=False, num_devices=1)
    arrays = {f"in_{k}": a for k, a in layout(inputs).items()}
    args = [nc.dram_tensor(k, a.shape, _mybir.dt.from_np(a.dtype), kind="ExternalInput").ap() for k, a in arrays.items()]
    out = nc.dram_tensor("out_0", (ROWS, STEPS, LEN), F32, kind="ExternalOutput").ap()
    build(nc, *args, out)
    r = _run(nc, [arrays], core_ids=[0])
    return r.results[0]["out_0"]
```
